# Optimizing a Trainium2 kernel written in Bass

```python
import numpy as np
import jax
import jax.numpy as jnp

def _softmax(x, axis=-1):
    return jax.nn.softmax(x, axis=axis)

def _gelu(x):
    return jax.nn.gelu(x, approximate=True)

def _silu(x):
    return jax.nn.silu(x)

def _sigmoid(x):
    return jax.nn.sigmoid(x)

def _layernorm(x, axis=-1, eps=1e-05):
    m = jnp.mean(x, axis=axis, keepdims=True)
    v = jnp.var(x, axis=axis, keepdims=True)
    return (x - m) / jnp.sqrt(v + eps)

def _scatter_add(tgt, idx, src, axis=0):
    return tgt.at[idx].add(src)

def _segment_sum(src, seg, n):
    return jax.ops.segment_sum(src, seg, n)
kernel_name = 'mk_cond_resid_d4_seqx_r4_2d7332'

def setup_inputs(seed: int=0):
    np.random.seed(seed)
    _w = jnp.asarray

    def _rec_inputs():
        import jax
        import jax.numpy as jnp
        _rk = jax.random.key(seed)
        x = 7.22e-05 + 1 * jax.random.normal(jax.random.fold_in(_rk, 1), (64, 64, 256), jnp.float32)
        _lenS = 64 - jax.random.randint(jax.random.fold_in(_rk, 7), (64,), 0, max(1, 64 // 4) + 1, jnp.int32)
        _lenS2 = 64 - jax.random.randint(jax.random.fold_in(_rk, 8), (64,), 0, max(1, 64 // 4) + 1, jnp.int32)
        cond_2048 = 0.997298 + 0.498944 * jax.random.normal(jax.random.fold_in(_rk, 11), (64, 512), jnp.float32)
        return (x, cond_2048)
    x, cond_2048 = _rec_inputs()

    def _L0_cond_setup():
        import jax, jax.numpy as jnp
        import numpy as np
        EPS_IN = 1e-05
        EPS_DM = 1e-08

        def _dcoef(weight, style):
            return jax.lax.rsqrt(jnp.einsum('oi,bi->bo', jnp.square(weight), jnp.square(style)) + EPS_DM)
        key = jax.random.key(seed)
        ks = jax.random.split(key, 7)
        B, S, H = (8, 256, 256)
        lim = 1.0 / np.sqrt(H)
        u = lambda k, shp: jax.random.uniform(k, shp, jnp.float32, -lim, lim)
        return {'x': jax.random.normal(ks[0], (B, S, H), jnp.float32), 'q_weight': u(ks[1], (H, H)), 'k_weight': u(ks[2], (H, H)), 'v_weight': u(ks[3], (H, H)), 'w_weight': u(ks[4], (H, H)), 'u_weight': u(ks[5], (H, H)), 'styles': jax.random.normal(ks[6], (B, 2 * H), jnp.float32) * 0.5 + 1.0, 'num_heads': 16}
    _L0_cond_all = _L0_cond_setup()
    _L0_cond_in = {k: v for k, v in _L0_cond_all.items() if k in ('q_weight', 'k_weight', 'v_weight', 'w_weight', 'u_weight')}
    del _L0_cond_all

    def _L1_cond_setup():
        import jax, jax.numpy as jnp
        import numpy as np
        EPS_IN = 1e-05
        EPS_DM = 1e-08

        def _dcoef(weight, style):
            return jax.lax.rsqrt(jnp.einsum('oi,bi->bo', jnp.square(weight), jnp.square(style)) + EPS_DM)
        key = jax.random.key(seed)
        ks = jax.random.split(key, 7)
        B, S, H = (8, 256, 256)
        lim = 1.0 / np.sqrt(H)
        u = lambda k, shp: jax.random.uniform(k, shp, jnp.float32, -lim, lim)
        return {'x': jax.random.normal(ks[0], (B, S, H), jnp.float32), 'q_weight': u(ks[1], (H, H)), 'k_weight': u(ks[2], (H, H)), 'v_weight': u(ks[3], (H, H)), 'w_weight': u(ks[4], (H, H)), 'u_weight': u(ks[5], (H, H)), 'styles': jax.random.normal(ks[6], (B, 2 * H), jnp.float32) * 0.5 + 1.0, 'num_heads': 16}
    _L1_cond_all = _L1_cond_setup()
    _L1_cond_in = {k: v for k, v in _L1_cond_all.items() if k in ('q_weight', 'k_weight', 'v_weight', 'w_weight', 'u_weight')}
    del _L1_cond_all

    def _L2_cond_setup():
        import jax, jax.numpy as jnp
        import numpy as np
        B, S, D_MODEL, D_INNER, D_STATE = (4, 1024, 256, 512, 16)
        key = jax.random.key(seed)
        ks = jax.random.split(key, 12)
        inp = {'x': jax.random.normal(ks[0], (B, S, D_MODEL), jnp.float32), 't_emb': jax.random.normal(ks[1], (B, D_INNER), jnp.float32), 'W_in': jax.random.normal(ks[2], (2 * D_INNER, D_MODEL), jnp.float32) * 0.02, 'W_conv': jax.random.normal(ks[3], (D_INNER, 1, 4), jnp.float32) * 0.1, 'b_conv': jnp.zeros((D_INNER,), jnp.float32), 'ln_g': jnp.ones((D_INNER,), jnp.float32), 'ln_b': jnp.zeros((D_INNER,), jnp.float32), 'W_xproj': jax.random.normal(ks[4], (3 * D_STATE, D_INNER), jnp.float32) * 0.02, 'W_dt': jax.random.normal(ks[5], (D_STATE, D_STATE), jnp.float32) * 0.01, 'b_dt': jax.random.uniform(ks[6], (D_STATE,), jnp.float32) * 0.1, 'A_log': jax.random.normal(ks[7], (D_STATE,), jnp.float32) * 0.1, 'D': jnp.ones((D_INNER,), jnp.float32) * 0.1, 'W_out': jax.random.normal(ks[8], (D_MODEL, D_INNER), jnp.float32) * 0.02}
        return inp
    _L2_cond_all = _L2_cond_setup()
    _L2_cond_in = {k: v for k, v in _L2_cond_all.items() if k in ('W_in', 'W_conv', 'b_conv', 'ln_g', 'ln_b', 'W_xproj', 'W_dt', 'b_dt', 'A_log', 'D', 'W_out')}
    del _L2_cond_all

    def _L3_cond_setup():
        import jax, jax.numpy as jnp
        import numpy as np
        B, S, D_MODEL, D_INNER, D_STATE = (4, 1024, 256, 512, 16)
        key = jax.random.key(seed)
        ks = jax.random.split(key, 12)
        inp = {'x': jax.random.normal(ks[0], (B, S, D_MODEL), jnp.float32), 't_emb': jax.random.normal(ks[1], (B, D_INNER), jnp.float32), 'W_in': jax.random.normal(ks[2], (2 * D_INNER, D_MODEL), jnp.float32) * 0.02, 'W_conv': jax.random.normal(ks[3], (D_INNER, 1, 4), jnp.float32) * 0.1, 'b_conv': jnp.zeros((D_INNER,), jnp.float32), 'ln_g': jnp.ones((D_INNER,), jnp.float32), 'ln_b': jnp.zeros((D_INNER,), jnp.float32), 'W_xproj': jax.random.normal(ks[4], (3 * D_STATE, D_INNER), jnp.float32) * 0.02, 'W_dt': jax.random.normal(ks[5], (D_STATE, D_STATE), jnp.float32) * 0.01, 'b_dt': jax.random.uniform(ks[6], (D_STATE,), jnp.float32) * 0.1, 'A_log': jax.random.normal(ks[7], (D_STATE,), jnp.float32) * 0.1, 'D': jnp.ones((D_INNER,), jnp.float32) * 0.1, 'W_out': jax.random.normal(ks[8], (D_MODEL, D_INNER), jnp.float32) * 0.02}
        return inp
    _L3_cond_all = _L3_cond_setup()
    _L3_cond_in = {k: v for k, v in _L3_cond_all.items() if k in ('W_in', 'W_conv', 'b_conv', 'ln_g', 'ln_b', 'W_xproj', 'W_dt', 'b_dt', 'A_log', 'D', 'W_out')}
    del _L3_cond_all
    return {'x': x, 'cond_2048': cond_2048, 'L0_cond_q_weight': _L0_cond_in['q_weight'], 'L0_cond_k_weight': _L0_cond_in['k_weight'], 'L0_cond_v_weight': _L0_cond_in['v_weight'], 'L0_cond_w_weight': _L0_cond_in['w_weight'], 'L0_cond_u_weight': _L0_cond_in['u_weight'], 'L1_cond_q_weight': _L1_cond_in['q_weight'], 'L1_cond_k_weight': _L1_cond_in['k_weight'], 'L1_cond_v_weight': _L1_cond_in['v_weight'], 'L1_cond_w_weight': _L1_cond_in['w_weight'], 'L1_cond_u_weight': _L1_cond_in['u_weight'], 'L2_cond_W_in': _L2_cond_in['W_in'], 'L2_cond_W_conv': _L2_cond_in['W_conv'], 'L2_cond_b_conv': _L2_cond_in['b_conv'], 'L2_cond_ln_g': _L2_cond_in['ln_g'], 'L2_cond_ln_b': _L2_cond_in['ln_b'], 'L2_cond_W_xproj': _L2_cond_in['W_xproj'], 'L2_cond_W_dt': _L2_cond_in['W_dt'], 'L2_cond_b_dt': _L2_cond_in['b_dt'], 'L2_cond_A_log': _L2_cond_in['A_log'], 'L2_cond_D': _L2_cond_in['D'], 'L2_cond_W_out': _L2_cond_in['W_out'], 'L3_cond_W_in': _L3_cond_in['W_in'], 'L3_cond_W_conv': _L3_cond_in['W_conv'], 'L3_cond_b_conv': _L3_cond_in['b_conv'], 'L3_cond_ln_g': _L3_cond_in['ln_g'], 'L3_cond_ln_b': _L3_cond_in['ln_b'], 'L3_cond_W_xproj': _L3_cond_in['W_xproj'], 'L3_cond_W_dt': _L3_cond_in['W_dt'], 'L3_cond_b_dt': _L3_cond_in['b_dt'], 'L3_cond_A_log': _L3_cond_in['A_log'], 'L3_cond_D': _L3_cond_in['D'], 'L3_cond_W_out': _L3_cond_in['W_out']}

def reference(x, cond_2048, L0_cond_q_weight, L0_cond_k_weight, L0_cond_v_weight, L0_cond_w_weight, L0_cond_u_weight, L1_cond_q_weight, L1_cond_k_weight, L1_cond_v_weight, L1_cond_w_weight, L1_cond_u_weight, L2_cond_W_in, L2_cond_W_conv, L2_cond_b_conv, L2_cond_ln_g, L2_cond_ln_b, L2_cond_W_xproj, L2_cond_W_dt, L2_cond_b_dt, L2_cond_A_log, L2_cond_D, L2_cond_W_out, L3_cond_W_in, L3_cond_W_conv, L3_cond_b_conv, L3_cond_ln_g, L3_cond_ln_b, L3_cond_W_xproj, L3_cond_W_dt, L3_cond_b_dt, L3_cond_A_log, L3_cond_D, L3_cond_W_out):
    import jax
    import jax.numpy as jnp

    def _L0_cond_ref(x, q_weight, k_weight, v_weight, w_weight, u_weight, styles, num_heads):
        import jax, jax.numpy as jnp
        import numpy as np
        EPS_IN = 1e-05
        EPS_DM = 1e-08

        def _dcoef(weight, style):
            return jax.lax.rsqrt(jnp.einsum('oi,bi->bo', jnp.square(weight), jnp.square(style)) + EPS_DM)
        B, S, H = x.shape
        nh = num_heads
        d = H // nh
        scale = jnp.asarray(d, x.dtype) ** (-0.5)
        s1 = styles[:, :H]
        s2 = styles[:, H:]
        x = x * s1[:, None, :]
        mu = jnp.mean(x, axis=-1, keepdims=True)
        var = jnp.mean(jnp.square(x - mu), axis=-1, keepdims=True)
        x = (x - mu) * jax.lax.rsqrt(var + EPS_IN)
        q_dc = _dcoef(q_weight, s1)
        k_dc = _dcoef(k_weight, s1)
        v_dc = _dcoef(v_weight, s1)
        w_dc = _dcoef(w_weight, s2)
        u_dc = _dcoef(u_weight, s2)

        def heads(t):
            return t.reshape(B, S, nh, d).transpose(0, 2, 1, 3)
        q = heads(jnp.einsum('bsh,oh->bso', x, q_weight) * q_dc[:, None, :])
        k = heads(jnp.einsum('bsh,oh->bso', x, k_weight) * k_dc[:, None, :])
        v_flat = jnp.einsum('bsh,oh->bso', x, v_weight) * v_dc[:, None, :] * s2[:, None, :]
        skip = v_flat
        v = heads(v_flat)
        attn = jnp.einsum('bhqd,bhkd->bhqk', q, k) * scale
        attn = jax.nn.softmax(attn, axis=-1)
        out = jnp.einsum('bhqk,bhkd->bhqd', attn, v).transpose(0, 2, 1, 3).reshape(B, S, H)
        out = jnp.einsum('bsh,oh->bso', out, w_weight) * w_dc[:, None, :]
        skip = jnp.einsum('bsh,oh->bso', skip, u_weight) * u_dc[:, None, :]
        return out + skip

    def _L1_cond_ref(x, q_weight, k_weight, v_weight, w_weight, u_weight, styles, num_heads):
        import jax, jax.numpy as jnp
        import numpy as np
        EPS_IN = 1e-05
        EPS_DM = 1e-08

        def _dcoef(weight, style):
            return jax.lax.rsqrt(jnp.einsum('oi,bi->bo', jnp.square(weight), jnp.square(style)) + EPS_DM)
        B, S, H = x.shape
        nh = num_heads
        d = H // nh
        scale = jnp.asarray(d, x.dtype) ** (-0.5)
        s1 = styles[:, :H]
        s2 = styles[:, H:]
        x = x * s1[:, None, :]
        mu = jnp.mean(x, axis=-1, keepdims=True)
        var = jnp.mean(jnp.square(x - mu), axis=-1, keepdims=True)
        x = (x - mu) * jax.lax.rsqrt(var + EPS_IN)
        q_dc = _dcoef(q_weight, s1)
        k_dc = _dcoef(k_weight, s1)
        v_dc = _dcoef(v_weight, s1)
        w_dc = _dcoef(w_weight, s2)
        u_dc = _dcoef(u_weight, s2)

        def heads(t):
            return t.reshape(B, S, nh, d).transpose(0, 2, 1, 3)
        q = heads(jnp.einsum('bsh,oh->bso', x, q_weight) * q_dc[:, None, :])
        k = heads(jnp.einsum('bsh,oh->bso', x, k_weight) * k_dc[:, None, :])
        v_flat = jnp.einsum('bsh,oh->bso', x, v_weight) * v_dc[:, None, :] * s2[:, None, :]
        skip = v_flat
        v = heads(v_flat)
        attn = jnp.einsum('bhqd,bhkd->bhqk', q, k) * scale
        attn = jax.nn.softmax(attn, axis=-1)
        out = jnp.einsum('bhqk,bhkd->bhqd', attn, v).transpose(0, 2, 1, 3).reshape(B, S, H)
        out = jnp.einsum('bsh,oh->bso', out, w_weight) * w_dc[:, None, :]
        skip = jnp.einsum('bsh,oh->bso', skip, u_weight) * u_dc[:, None, :]
        return out + skip

    def _L2_cond_ref(x, t_emb, W_in, W_conv, b_conv, ln_g, ln_b, W_xproj, W_dt, b_dt, A_log, D, W_out):
        import jax, jax.numpy as jnp
        import numpy as np
        B, S, D_MODEL, D_INNER, D_STATE = (4, 1024, 256, 512, 16)
        d_inner = W_conv.shape[0]
        d_state = A_log.shape[0]
        xr, gate = jnp.split(x @ W_in.T, 2, axis=-1)
        xr = xr + t_emb[:, None, :]
        xc = jax.lax.conv_general_dilated(xr.transpose(0, 2, 1), W_conv, (1,), [(3, 0)], feature_group_count=d_inner, dimension_numbers=('NCH', 'OIH', 'NCH')) + b_conv[None, :, None]
        xc = jax.nn.silu(xc).transpose(0, 2, 1)
        mu = xc.mean(-1, keepdims=True)
        var = xc.var(-1, keepdims=True)
        xn = (xc - mu) / jnp.sqrt(var + 1e-05) * ln_g + ln_b
        Bm, Cm, dt = jnp.split(xn @ W_xproj.T, 3, axis=-1)
        dt = jnp.tanh(dt @ W_dt.T + b_dt) * 0.01
        A = -jnp.tanh(A_log)
        Ad = 1.0 + dt * A
        Bd = Bm * jnp.minimum(jnp.linalg.norm(xn, axis=-1, keepdims=True), 1.0)
        h0 = jnp.zeros((xn.shape[0], d_state, d_inner), xn.dtype)

        def step(h, inputs):
            ad, bd, xt, ct = inputs
            h = jnp.clip(h * ad[:, :, None] + bd[:, :, None] * xt[:, None, :], -10.0, 10.0)
            yt = jnp.einsum('bd,bdh->bh', ct, h)
            return (h, yt)
        _, ys = jax.lax.scan(step, h0, (Ad.transpose(1, 0, 2), Bd.transpose(1, 0, 2), xn.transpose(1, 0, 2), Cm.transpose(1, 0, 2)))
        y = ys.transpose(1, 0, 2) + D * xn
        return y * jax.nn.silu(gate) @ W_out.T

    def _L3_cond_ref(x, t_emb, W_in, W_conv, b_conv, ln_g, ln_b, W_xproj, W_dt, b_dt, A_log, D, W_out):
        import jax, jax.numpy as jnp
        import numpy as np
        B, S, D_MODEL, D_INNER, D_STATE = (4, 1024, 256, 512, 16)
        d_inner = W_conv.shape[0]
        d_state = A_log.shape[0]
        xr, gate = jnp.split(x @ W_in.T, 2, axis=-1)
        xr = xr + t_emb[:, None, :]
        xc = jax.lax.conv_general_dilated(xr.transpose(0, 2, 1), W_conv, (1,), [(3, 0)], feature_group_count=d_inner, dimension_numbers=('NCH', 'OIH', 'NCH')) + b_conv[None, :, None]
        xc = jax.nn.silu(xc).transpose(0, 2, 1)
        mu = xc.mean(-1, keepdims=True)
        var = xc.var(-1, keepdims=True)
        xn = (xc - mu) / jnp.sqrt(var + 1e-05) * ln_g + ln_b
        Bm, Cm, dt = jnp.split(xn @ W_xproj.T, 3, axis=-1)
        dt = jnp.tanh(dt @ W_dt.T + b_dt) * 0.01
        A = -jnp.tanh(A_log)
        Ad = 1.0 + dt * A
        Bd = Bm * jnp.minimum(jnp.linalg.norm(xn, axis=-1, keepdims=True), 1.0)
        h0 = jnp.zeros((xn.shape[0], d_state, d_inner), xn.dtype)

        def step(h, inputs):
            ad, bd, xt, ct = inputs
            h = jnp.clip(h * ad[:, :, None] + bd[:, :, None] * xt[:, None, :], -10.0, 10.0)
            yt = jnp.einsum('bd,bdh->bh', ct, h)
            return (h, yt)
        _, ys = jax.lax.scan(step, h0, (Ad.transpose(1, 0, 2), Bd.transpose(1, 0, 2), xn.transpose(1, 0, 2), Cm.transpose(1, 0, 2)))
        y = ys.transpose(1, 0, 2) + D * xn
        return y * jax.nn.silu(gate) @ W_out.T
    x = x + _L0_cond_ref(x, L0_cond_q_weight, L0_cond_k_weight, L0_cond_v_weight, L0_cond_w_weight, L0_cond_u_weight, cond_2048, 16)
    x = x + _L1_cond_ref(x, L1_cond_q_weight, L1_cond_k_weight, L1_cond_v_weight, L1_cond_w_weight, L1_cond_u_weight, cond_2048, 16)
    x = x + _L2_cond_ref(x, cond_2048, L2_cond_W_in, L2_cond_W_conv, L2_cond_b_conv, L2_cond_ln_g, L2_cond_ln_b, L2_cond_W_xproj, L2_cond_W_dt, L2_cond_b_dt, L2_cond_A_log, L2_cond_D, L2_cond_W_out)
    x = x + _L3_cond_ref(x, cond_2048, L3_cond_W_in, L3_cond_W_conv, L3_cond_b_conv, L3_cond_ln_g, L3_cond_ln_b, L3_cond_W_xproj, L3_cond_W_dt, L3_cond_b_dt, L3_cond_A_log, L3_cond_D, L3_cond_W_out)
    return x

_drawn_inputs = setup_inputs


def setup_inputs(seed=0):
    import zlib

    import numpy as np

    out = dict(_drawn_inputs(seed))
    spreads = {'L2_cond_b_conv': (0.0, 0.1),
     'L2_cond_ln_g': (1.0, 0.2),
     'L2_cond_ln_b': (0.0, 0.1),
     'L2_cond_D': (0.10000000149011612, 0.6),
     'L3_cond_b_conv': (0.0, 0.1),
     'L3_cond_ln_g': (1.0, 0.2),
     'L3_cond_ln_b': (0.0, 0.1),
     'L3_cond_D': (0.10000000149011612, 0.6)}
    factors = {'L2_cond_W_dt': 64.0,
     'L2_cond_b_dt': 64.0,
     'L2_cond_A_log': 34.325,
     'L3_cond_W_dt': 64.0,
     'L3_cond_b_dt': 61.369,
     'L3_cond_A_log': 28.627}
    for name, (base, spread) in spreads.items():
        noise = np.random.default_rng([zlib.crc32(name.encode()), seed]).standard_normal(out[name].shape)
        drawn = base * np.exp(spread * noise) if base else spread * noise
        out[name] = jnp.asarray(drawn.astype(out[name].dtype))
    for name, factor in factors.items():
        out[name] = (out[name] * factor).astype(out[name].dtype)
    return out
```

```python
import numpy as np
import concourse.bass as bass
from concourse import mybir
from contextlib import ExitStack

B, S, H, DI, N = 64, 64, 256, 512, 16
HEADS = 16
HD = H // HEADS
P = 128
GB = P // N
G = B // GB
TOK = GB * S
HC, DC = H // P, DI // P
TT = TOK // P
LAYERS = 2
QW = 4
PASSES = G // QW
CH = 4
CHUNKS = S // CH
PARTS = 3
XROWS = PARTS * PARTS * GB
CROW = 96
KROWS = CROW + PARTS
CLIP = 10.0
EPS_IN, EPS_DM = 1e-5, 1e-8
LEAST = 1e-18


def cond_resid_kernel(nc, xT, condT, attw, win, wconv, chan, wxp, wdt, dtv, wout,
                      ident_d, sel_d, masks_d, rowmask_d, out):
    f32, bf16 = mybir.dt.float32, mybir.dt.bfloat16
    ALU, ACT, AX = mybir.AluOpType, mybir.ActivationFunctionType, mybir.AxisListType
    ds = bass.ds

    def scratch(name, shape, dt):
        return nc.dram_tensor(name, shape, dt, kind="Internal").ap()

    xn_d = scratch("xn_d", (G, P, DC, TOK), f32)
    sg_d = scratch("sg_d", (G, P, DC, TOK), f32)
    xpart_d = scratch("xpart_d", (PARTS, G, GB, S * DI), bf16)
    bpart_d = scratch("bpart_d", (PARTS, G, GB, S * N), bf16)
    kpart_d = scratch("kpart_d", (PARTS, G, S, GB, N), bf16)
    beta_d = scratch("beta_d", (PARTS, B * S + S), bf16)
    kap_d = scratch("kap_d", (B * S + S,), f32)
    cc_d = scratch("cc_d", (G, P, S + 1), f32)
    a_d = scratch("a_d", (G, P, S), f32)
    y_d = scratch("y_d", (G, GB, S + 1, DI), f32)

    es = ExitStack()
    with es:
        es.enter_context(nc.allow_non_contiguous_dma(reason="a few short columns for each group"))

        def sem(name):
            return es.enter_context(nc.semaphore(name))

        def sb(name, shape, dt=f32, where=None):
            return (where or es).enter_context(nc.sbuf_tensor(name, shape, dt))

        PS = es.enter_context(nc.psum_tensor("PS", [P, 8, 512], f32))

        X = sb("X", [P, G, HC, TOK])
        cond = sb("cond", [P, DC, B])
        condsq = sb("condsq", [P, DC, B])
        ident = sb("ident", [P, P])
        sel = sb("sel", [N, P])
        masks = sb("masks", [P, 12])
        rowmask = sb("rowmask", [P, GB], bf16)
        ones_h = sb("ones_h", [P, P])
        ones_d = sb("ones_d", [P, P])
        ones_n = sb("ones_n", [P, N])
        zero_f = sb("zero_f", [P, 1])
        zero_b = sb("zero_b", [P, 1], bf16)
        eps = sb("eps", [P, 3])
        nmask = sb("nmask", [P, GB])
        par = [masks[:, 0:1], masks[:, 1:2]]
        half = masks[:, 2:4]
        bmask = masks[:, 4:12]

        att = ExitStack()
        W = sb("W", [P, 5, HC, H], where=att)
        Wsq = sb("Wsq", [P, 5, HC, H], where=att)
        dco = sb("dco", [P, 5, HC, B], where=att)
        qk_t = sb("qk_t", [P, HC, B], where=att)
        vs_t = sb("vs_t", [P, HC, B], where=att)
        xs = sb("xs", [P, HC, TOK], where=att)
        xm = sb("xm", [P, HC, TOK], where=att)
        sq = sb("sq", [P, HC, TOK], where=att)
        dsq = sb("dsq", [P, 5 * HC * B], where=att)
        dlg = sb("dlg", [P, 5 * HC * B], where=att)
        dt1 = sb("dt1", [P, 5 * HC * B], where=att)
        vare = sb("vare", [P, TOK], where=att)
        lg = sb("lg", [P, TOK], where=att)
        rstd = sb("rstd", [P, TOK], where=att)
        xn = sb("xn", [P, HC, TOK], where=att)
        qs = sb("qs", [P, HC, TOK], where=att)
        kz = sb("kz", [P, HC, 2, TOK], where=att)
        vTd = sb("vTd", [P, HC, GB, 2, S], where=att)
        vsc = sb("vsc", [P, HC, TOK], where=att)
        vbd = sb("vbd", [P, GB, H // 32, 2, HD], where=att)
        mx = sb("mx", [P, 2, 32], where=att)
        sm = sb("sm", [P, 2, 32], where=att)
        rs = sb("rs", [P, 2, 32], where=att)
        ex = sb("ex", [P, 2, 4, 512], where=att)
        pn = sb("pn", [P, 2, 4, 512], where=att)
        pT = sb("pT", [P, 2, 8, P], where=att)
        av = sb("av", [P, HC, TOK], where=att)
        t1 = sb("t1", [P, HC, TOK], where=att)
        t2 = sb("t2", [P, HC, TOK], where=att)
        t3 = sb("t3", [P, HC, TOK], where=att)
        att.close()

        ssm = ExitStack()
        Win = sb("Win", [P, HC, 2 * DI], where=ssm)
        Wc = sb("Wc", [P, DC, 4], where=ssm)
        Ch = sb("Ch", [P, DC, 4], where=ssm)
        Wx = sb("Wx", [P, DC, 3 * N], where=ssm)
        Wdt = sb("Wdt", [N, N], where=ssm)
        dtp = sb("dtp", [N, 2], where=ssm)
        tA = sb("tA", [N, 1], where=ssm)
        A01 = sb("A01", [N, 1], where=ssm)
        Wo = sb("Wo", [P, DC, H], where=ssm)
        front = ExitStack()
        xp = sb("xp", [P, DC, GB, S + 3], where=front)
        sgt = sb("sgt", [P, DC, TOK], where=front)
        sg = sb("sg", [P, DC, TOK], where=front)
        acc = sb("acc", [P, DC, TOK], where=front)
        th = sb("th", [P, DC, TOK], where=front)
        z = sb("z", [P, DC, TOK], where=front)
        zq = sb("zq", [P, DC, TOK], where=front)
        zve = sb("zve", [P, TOK], where=front)
        zlg = sb("zlg", [P, TOK], where=front)
        zr = sb("zr", [P, TOK], where=front)
        xnb = sb("xnb", [P, DC, TOK], where=front)
        xh = sb("xh", [P, TT, DI], bf16, where=front)
        xr1 = sb("xr1", [P, TT, DI], where=front)
        xmi = sb("xmi", [P, TT, DI], bf16, where=front)
        xlo = sb("xlo", [P, TT, DI], bf16, where=front)
        n2 = sb("n2", [N, TOK], where=front)
        n3 = sb("n3", [N, TOK], where=front)
        n4 = sb("n4", [N, TOK], where=front)
        mn = sb("mn", [N, TOK], where=front)
        dts = sb("dts", [N, TOK], where=front)
        dtt = sb("dtt", [N, TOK], where=front)
        am = sb("am", [N, TOK], where=front)
        rA = sb("rA", [N, TOK], where=front)
        Bd = sb("Bd", [N, TOK], where=front)
        Cn = sb("Cn", [N, TOK], where=front)
        stk = sb("stk", [112, TOK], where=front)
        pick = sb("pick", [P, 2, GB, S], where=front)
        ccs = sb("ccs", [P, S + 1], where=front)
        acs = sb("acs", [P, S], where=front)
        tv = sb("tv", [P, TT, 33], where=front)
        tvr = sb("tvr", [P, TT, 33], where=front)
        tvp = sb("tvp", [P, PARTS, TT, 33], bf16, where=front)
        kp = sb("kp", [P, TT], where=front)
        bsum = sb("bsum", [P, TT], where=front)
        front.close()
        post = ExitStack()
        yt = sb("yt", [P, TT, DI], where=post)
        xnp = sb("xnp", [P, DC, TOK], where=post)
        sgp = sb("sgp", [P, DC, TOK], where=post)
        yf = sb("yf", [P, DC, TOK], where=post)
        yg = sb("yg", [P, DC, TOK], where=post)
        post.close()
        scan = ExitStack()
        xq = sb("xq", [P, 2, QW, CH, DI], bf16, where=scan)
        Uw = sb("Uw", [P, 2, QW, CH, GB, N], bf16, where=scan)
        Ub = sb("Ub", [P, QW, S, N], bf16, where=scan)
        bet = sb("bet", [P, QW, S], bf16, where=scan)
        By = sb("By", [P, 2, QW, CH * CH * GB], bf16, where=scan)
        Cc = sb("Cc", [P, QW, S + 1], where=scan)
        Wy = sb("Wy", [P, 2, QW, CH * CH * GB], where=scan)
        W64 = sb("W64", [P, QW, GB], where=scan)
        At = sb("At", [P, QW, S], where=scan)
        Ast = sb("Ast", [P, 2, QW, CH], where=scan)
        kap = sb("kap", [P, CHUNKS + 1], where=scan)
        kst = sb("kst", [P, 2, 1], where=scan)
        q = sb("q", [P, 2, QW, DI], where=scan)
        R = sb("R", [P, QW, DI], where=scan)
        ys = sb("ys", [P, 2, DI], where=scan)
        ye = sb("ye", [P, DI], where=scan)
        scan.close()
        ssm.close()

        (ld, cst, csq_r) = [sem(n) for n in ("loaded", "constants", "condsq_ready")]
        (w_in, wsq_r, dco_mm, dco_e, dco_r, tab_r) = [sem(n) for n in
            ("att_weights", "att_wsq", "dcoef_mm", "dcoef_squares", "dcoef_ready", "tables_ready")]
        (xs_r, mean_r, xm_r, sq_r, var_r, rstd_r, xn_r) = [sem(n) for n in
            ("xs_ready", "mean_ready", "xm_ready", "sq_ready", "var_ready", "rstd_ready", "xn_ready")]
        (q_mm, k_mm, v_mm, q_r, k_r, v_r, vs_r) = [sem(n) for n in
            ("q_mm", "k_mm", "v_mm", "q_ready", "k_ready", "v_ready", "vscaled_ready")]
        (vt_mm, vbd_r, sc_mm, max_r, sub_r, exp_r, sum_r, rcp_r, pn_r) = [sem(n) for n in
            ("vturn_mm", "vbd_ready", "scores_mm", "max_ready", "sub_ready", "exp_ready", "sum_ready",
             "recip_ready", "probs_ready")]
        (pt_mm, pt_r, av_mm, av_r, w_mm, u_mm, t1_r, t2_r, t3_r, x_done) = [sem(n) for n in
            ("pturn_mm", "pturn_ready", "av_mm", "av_ready", "w_mm", "u_mm", "t1_ready", "t2_ready",
             "t3_ready", "att_done")]
        (sw_in, tA_r, A_r, xr_mm, g_mm, xp_r, sgt_r, sg_r, sg_st, acc_r, cv_r, th_r, z_r) = [sem(n) for n in
            ("ssm_weights", "tanhA", "A_ready", "xr_mm", "gate_mm", "xp_ready", "gate_tanh", "gate_ready",
             "gate_stored", "acc_ready", "conv_ready", "tanh_ready", "z_ready")]
        (zm_mm, zc_r, zq_r, zv_mm, zr_r, xg_r, xf_r, xf_st, x2_r, nrm_mm, bc_mm, dt_mm) = [sem(n) for n in
            ("zmean_mm", "zc_ready", "zsq_ready", "zvar_mm", "zrstd_ready", "xgain_ready", "xnorm_ready",
             "xnorm_stored", "xnsq_ready", "norm_mm", "bc_mm", "dt_mm")]
        (mn_r, dts_r, dt2_mm, dtt_r, pr_s, C_r, stk_r, pk_mm, pk_r, pick_s, pick_st) = [sem(n) for n in
            ("minnorm", "dt_copied", "dt2_mm", "dt_tanh", "proj_step", "C_ready", "stack_ready", "pick_mm",
             "pick_masked", "pick_step", "pick_stored")]
        (tok_mm, tv_s, tv_st, xt_mm, xh_r, xr1_r, xmi_r, xlo_r, xq_st, f_it) = [sem(n) for n in
            ("tok_mm", "tok_step", "tok_stored", "xturn_mm", "xhi_ready", "xrest_ready", "xmid_ready",
             "xlo_ready", "xparts_stored", "front_done")]
        dlg_r, dco_g, rg_r, zg_r, ng_r, mm_r = [sem(n) for n in
            ("dcoef_log", "dcoef_guess", "rstd_guess", "zrstd_guess", "norm_guess", "minnorm_ready")]
        zero_st = sem("zero_stored")
        passed = sem("wait_passed")
        set_r = sem("scan_set")
        tab_in = sem("scan_tables")
        xq_in = [sem("xq_in0"), sem("xq_in1")]
        pl_st, pe_w, dv_q, ac_r, pe_yq, dv_y = [sem(n) for n in
            ("staged", "w_ready", "q_ready2", "R_ready", "q_used", "y_ready")]
        y_out = [sem("y_out0"), sem("y_out1")]
        ep_w, ep_q, ep_y, ep_r, ep_out, r_init = [sem(n) for n in
            ("end_staged", "end_q", "end_y_mm", "end_y", "end_out", "R_start")]
        po_in, po_mm, yf_r, yg_r, o_mm, po_done = [sem(n) for n in
            ("post_in", "yturn_mm", "y_sum", "y_gated", "out_mm", "post_done")]
        fin = sem("final")

        XQ = 9 + 1

        block = es.enter_context(nc.Block())

        def alone(eng):
            eng.sem_inc(passed, 1)

        def diag_of(m, h, rows):
            v = m[0:rows, h, :, :]
            v = v.rearrange("p g (u r) -> p g u r", r=GB)
            return v[:, :, 0:CH * CH:CH + 1, :]

        @block.sync
        def _(sp):
            sp.dma_start(X[:, :, :, :], xT).then_inc(ld, 16)
            sp.dma_start(cond[:, :, :], condT).then_inc(ld, 16)
            sp.dma_start(ident[:, :], ident_d).then_inc(ld, 16)
            sp.dma_start(sel[:, :], sel_d).then_inc(ld, 16)
            sp.dma_start(masks[:, :], masks_d).then_inc(ld, 16)
            sp.dma_start(rowmask[:, :], rowmask_d).then_inc(ld, 16)
            sp.wait_ge(x_done, 1)
            with sp.Fori(0, LAYERS) as l:
                sp.wait_ge(x_done, l * G + 1)
                sp.dma_start(W[:, :, :, :], attw[ds(l, 1)].rearrange("a p w c o -> p (a w) c o")).then_inc(w_in, 16)

            sp.wait_ge(x_done, LAYERS * G + 1)
            sp.sem_inc(f_it, 1)
            sp.wait_ge(cst, 9)
            for i in range(PARTS):
                sp.dma_start(beta_d[i, 0:1].rearrange("(a o) -> a o", o=1), zero_b[0:1, :]).then_inc(zero_st, 16)
            sp.dma_start(kap_d[0:1].rearrange("(a o) -> a o", o=1), zero_f[0:1, :]).then_inc(zero_st, 16)
            with sp.Fori(0, LAYERS) as l:
                sp.wait_ge(po_done, l * G + 1)
                for dst, src in ((Win, win), (Wc, wconv), (Ch, chan), (Wx, wxp), (Wo, wout)):
                    sp.dma_start(dst[:, :, :], src[ds(l, 1)].rearrange("a p c o -> p (a c) o")).then_inc(sw_in, 16)
                for dst, src in ((Wdt, wdt), (dtp, dtv)):
                    sp.dma_start(dst[:, :], src[ds(l, 1)].rearrange("a p o -> (a p) o")).then_inc(sw_in, 16)
                with sp.Fori(0, G) as g:
                    it = l * G + g
                    sp.wait_ge(sg_r, it * DC + DC)
                    sp.dma_start(sg_d[ds(g, 1)].rearrange("a p c t -> p (a c) t"), sg[:, :, :]).then_inc(sg_st, 16)
                    sp.wait_ge(xf_r, it * DC + DC)
                    sp.dma_start(xn_d[ds(g, 1)].rearrange("a p c t -> p (a c) t"), z[:, :, :]).then_inc(xf_st, 16)
                    sp.wait_ge(pick_s, it * 2 + 2)
                    sp.dma_start(cc_d[ds(g, 1)].rearrange("a p s -> (a p) s"), ccs[:, :]).then_inc(pick_st, 16)
                    sp.dma_start(a_d[ds(g, 1)].rearrange("a p s -> (a p) s"), acs[:, :]).then_inc(pick_st, 16)
                    sp.wait_ge(tv_s, it * 9 + 9)
                    alone(sp)
                    for i in range(PARTS):
                        sp.dma_start(bpart_d[i, ds(g, 1)].rearrange("a (k b) (t n) -> (a b t) k n", k=TT, n=N),
                                     tvp[:, i, :, 0:N]).then_inc(tv_st, 16)
                        sp.dma_start(beta_d[i, ds(g * TOK + 1, TOK)].rearrange("(k p o) -> p k o", p=P, o=1),
                                     tvp[:, i, :, 2 * N:2 * N + 1]).then_inc(tv_st, 16)
                        for b2 in range(2):
                            sp.dma_start(kpart_d[i, ds(g, 1)].rearrange("a t (k b) n -> b (a t) k n", b=2)[b2],
                                         tvp[b2 * S:(b2 + 1) * S, i, :, N:2 * N]).then_inc(tv_st, 16)
                    sp.dma_start(kap_d[ds(g * TOK + 1, TOK)].rearrange("(k p o) -> p k o", p=P, o=1),
                                 kp[:, :].rearrange("p (k o) -> p k o", o=1)).then_inc(tv_st, 16)
                    sp.wait_ge(xh_r, it * TT + TT)
                    sp.wait_ge(xmi_r, it * TT + TT)
                    sp.wait_ge(xlo_r, it * TT + TT)
                    alone(sp)
                    for j, src in enumerate((xh, xmi, xlo)):
                        sp.dma_start(xpart_d[j, ds(g, 1)].rearrange("a (k b) (t c) -> (a b t) k c", k=TT, c=DI),
                                     src[:, :, :]).then_inc(xq_st, 16)
                    sp.wait_ge(sg_st, it * 16 + 16)
                    sp.wait_ge(xf_st, it * 16 + 16)
                    sp.wait_ge(pick_st, it * 32 + 32)
                    sp.wait_ge(tv_st, it * (13 * 16) + 13 * 16)
                    sp.wait_ge(xq_st, it * 48 + 48)
                    sp.sem_inc(f_it, 1)

                sp.wait_ge(zero_st, 16 * (PARTS + 1))
                sp.wait_ge(pick_st, l * (32 * G) + 32 * G)
                sp.wait_ge(tv_st, l * (13 * 16 * G) + 13 * 16 * G)
                sp.wait_ge(xq_st, l * (48 * G) + 48 * G)
                sp.wait_ge(set_r, l * 6 + 6)
                alone(sp)
                with sp.Fori(0, PASSES) as ps:
                    pi = l * PASSES + ps
                    sp.wait_ge(pl_st, pi * (CHUNKS * 8) + 1)
                    alone(sp)
                    sp.wait_ge(ep_w, pi + 1)
                    sp.wait_ge(ep_r, pi * QW + 1)
                    alone(sp)
                    for i in range(PARTS):
                        for j in range(PARTS):
                            r0 = (i * PARTS + j) * GB
                            sp.dma_start(Ub[r0:r0 + GB, :, :, :],
                                         bpart_d[i, ds(ps * QW, QW)].rearrange("g b (t n) -> b g t n", n=N)).then_inc(tab_in, 16)
                            sp.dma_start(bet[r0:r0 + GB, :, :],
                                         beta_d[i, ds(ps * (QW * TOK), QW * TOK)].rearrange("(g b t) -> b g t", g=QW, t=S)).then_inc(tab_in, 16)
                    sp.dma_start(Cc[:, :, :], cc_d[ds(ps * QW, QW)].rearrange("g p s -> p g s")).then_inc(tab_in, 16)
                    sp.dma_start(At[:, :, :], a_d[ds(ps * QW, QW)].rearrange("g p s -> p g s")).then_inc(tab_in, 16)
                    for w in range(QW):
                        for t in range(CH):
                            sp.dma_start(kap[32 * w + t * GB:32 * w + (t + 1) * GB, 0:CHUNKS],
                                         kap_d[ds((ps * QW + w) * TOK, TOK)].rearrange("(b c t) -> t b c", b=GB, t=CH)[t]).then_inc(tab_in, 16)
                        sp.dma_start(kap[32 * w:32 * w + GB, CHUNKS:CHUNKS + 1],
                                     kap_d[ds((ps * QW + w) * TOK + S, TOK)].rearrange("(b t) -> b t", t=S)[:, 0:1]).then_inc(tab_in, 16)

                    def load(h, cn, ck_of):
                        for i in range(PARTS):
                            for j in range(PARTS):
                                r0 = (i * PARTS + j) * GB
                                sp.dma_start(xq[r0:r0 + GB, h, :, :, :].rearrange("p g t c -> p g (t c)"),
                                             xpart_d[j, ds(ps * QW, QW), :, ds(ck_of * (CH * DI), CH * DI)].rearrange("g b f -> b g f")).then_inc(xq_in[h], 16)
                        sp.dma_start(Uw[CROW:CROW + PARTS, h, :, :, :, :].rearrange("p g t b n -> p g (t b n)"),
                                     kpart_d[:, ds(ps * QW, QW), ds(ck_of * CH, CH)].rearrange("i g t b n -> i g (t b n)")).then_inc(xq_in[h], 16)

                    def store(h, cn, ck_of):
                        sp.wait_ge(dv_y, cn + 3)
                        for w in range(QW):
                            sp.dma_start(y_d[ds(ps * QW + w, 1), :, ds(ck_of * CH, CH), :].rearrange("a b t c -> (a t) b c"),
                                         ys[32 * w:32 * w + 32, h, :]).then_inc(y_out[h], 16)

                    sp.wait_ge(pe_yq, pi * (CHUNKS * 2 * CH) + 16)
                    load(0, pi * CHUNKS, 0)
                    load(1, pi * CHUNKS + 1, 1)
                    with sp.Fori(0, CHUNKS // 2 - 1) as c2:
                        for h in range(2):
                            cn = pi * CHUNKS + c2 * 2 + h
                            store(h, cn, c2 * 2 + h)
                            sp.wait_ge(pe_yq, cn * (2 * CH) + 2 * CH + 16)
                            load(h, cn + 2, c2 * 2 + h + 2)
                    for h in range(2):
                        store(h, pi * CHUNKS + CHUNKS - 2 + h, CHUNKS - 2 + h)
                    sp.wait_ge(ep_r, pi * QW + QW + 1)
                    alone(sp)
                    for w in range(QW):
                        sp.dma_start(y_d[ds(ps * QW + w, 1), :, S, :].rearrange("a b c -> (a b) c"),
                                     ye[32 * w:32 * w + GB, :]).then_inc(ep_out, 16)

                sp.wait_ge(y_out[0], l * (PASSES * CHUNKS // 2 * QW * 16) + (PASSES * CHUNKS // 2 * QW * 16) + 64)
                sp.wait_ge(y_out[1], l * (PASSES * CHUNKS // 2 * QW * 16) + (PASSES * CHUNKS // 2 * QW * 16) + 64)
                sp.wait_ge(ep_out, l * (PASSES * QW * 16) + PASSES * QW * 16 + 16)
                alone(sp)
                sp.wait_ge(sg_st, l * (16 * G) + 16 * G)
                sp.wait_ge(xf_st, l * (16 * G) + 16 * G)
                alone(sp)
                with sp.Fori(0, G) as g:
                    it = l * G + g
                    sp.wait_ge(po_done, it + 1)
                    for b2 in range(2):
                        sp.dma_start(yt[b2 * S:(b2 + 1) * S, :, :],
                                     y_d[ds(g, 1), :, 1:S + 1, :].rearrange("a (k b) t c -> b (a t) k c", b=2)[b2]).then_inc(po_in, 16)
                    sp.dma_start(xnp[:, :, :], xn_d[ds(g, 1)].rearrange("a p c t -> p (a c) t")).then_inc(po_in, 16)
                    sp.dma_start(sgp[:, :, :], sg_d[ds(g, 1)].rearrange("a p c t -> p (a c) t")).then_inc(po_in, 16)
            sp.wait_ge(po_done, LAYERS * G + 1)
            sp.dma_start(out, X[:, :, :, :]).then_inc(fin, 16)
            sp.wait_ge(fin, 16)

        @block.gpsimd
        def _(pl):
            pl.memset(ones_h[:, :], 1.0 / H).then_inc(cst, 1)
            pl.memset(ones_d[:, :], 1.0 / DI).then_inc(cst, 1)
            pl.memset(ones_n[:, :], 1.0).then_inc(cst, 1)
            for n, value in enumerate((EPS_IN, 4 * EPS_IN, EPS_DM)):
                pl.memset(eps[:, n:n + 1], value).then_inc(cst, 1)
            pl.memset(zero_f[:, :], 0.0).then_inc(cst, 1)
            pl.memset(zero_b[:, :], 0.0).then_inc(cst, 1)
            pl.sem_inc(pl_st, 1)
            pl.sem_inc(ep_w, 1)
            pl.wait_ge(cst, 9)
            with pl.Fori(0, LAYERS) as l:
                with pl.Fori(0, G) as g:
                    it = l * G + g
                    pl.wait_ge(v_r, it * 2 + 2)
                    pl.wait_ge(tab_r, l * 2 + 2)
                    pl.tensor_tensor(vsc[:, :, :].rearrange("p c (b t) -> p c b t", t=S), vTd[:, :, :, 0, :],
                                     vs_t[:, :, ds(g * GB, GB)].unsqueeze(3).broadcast_to([P, HC, GB, S]),
                                     ALU.mult).then_inc(vs_r, 1)
                    for r in range(2):
                        pl.wait_ge(rcp_r, it * 2 + r + 1)
                        pl.tensor_tensor(pn[:, r, :, :].rearrange("p j (e k) -> p (j e) k", k=S),
                                         ex[:, r, :, :].rearrange("p j (e k) -> p (j e) k", k=S),
                                         rs[:, r, :].unsqueeze(2).broadcast_to([P, 32, S]),
                                         ALU.mult).then_inc(pn_r, 1)
                    pl.wait_ge(t1_r, it * 2 + 2)
                    pl.wait_ge(t2_r, it * 2 + 2)
                    pl.tensor_tensor(t3[:, :, :], t1[:, :, :], t2[:, :, :], ALU.add).then_inc(t3_r, 1)

            pl.wait_ge(x_done, LAYERS * G + 1)
            with pl.Fori(0, LAYERS) as l:
                pl.wait_ge(po_done, l * G + 1)
                alone(pl)
                with pl.Fori(0, G) as g:
                    it = l * G + g
                    pl.wait_ge(f_it, it + 1)
                    for k in range(TT):
                        pl.wait_ge(xmi_r, it * TT + k + 1)
                        pl.tensor_tensor(xlo[:, k, :], xr1[:, k, :], xmi[:, k, :], ALU.subtract).then_inc(xlo_r, 1)

                pl.wait_ge(f_it, l * G + G + 1)
                pl.wait_ge(pick_st, l * (32 * G) + 32 * G)
                pl.wait_ge(tv_st, l * (13 * 16 * G) + 13 * 16 * G)
                pl.wait_ge(xq_st, l * (48 * G) + 48 * G)
                pl.wait_ge(sg_st, l * (16 * G) + 16 * G)
                pl.wait_ge(xf_st, l * (16 * G) + 16 * G)
                alone(pl)
                for n, (buf, value) in enumerate(((xq[64:96, :, :, :, :], 0.0), (xq[96:128, :, :, :, :], 1.0),
                                                  (Uw[:, :, :, :, :, :], 0.0), (By[:, :, :, :], 0.0),
                                                  (Wy[:, :, :, :], 0.0), (kap[:, :], 0.0))):
                    pl.memset(buf, value).then_inc(set_r, 1)
                    pl.wait_ge(set_r, l * 6 + n + 1)
                    alone(pl)
                with pl.Fori(0, PASSES) as ps:
                    pi = l * PASSES + ps
                    pl.wait_ge(tab_in, pi * (16 * (9 + 9 + 2 + QW * (CH + 1))) + 16 * (9 + 9 + 2 + QW * (CH + 1)))
                    pl.wait_ge(set_r, l * 6 + 6)
                    alone(pl)
                    with pl.Fori(0, CHUNKS // 2) as c2:
                        for h in range(2):
                            cn = pi * CHUNKS + c2 * 2 + h
                            s0 = c2 * (2 * CH) + h * CH
                            pl.wait_ge(pe_yq, cn * (2 * CH) + 2 * CH)
                            pl.wait_ge(dv_y, cn + 1)
                            pl.wait_ge(ac_r, cn * (4 * CH) + 4)
                            for w in range(QW):
                                pl.tensor_tensor(Uw[0:XROWS, h, w, :, :, :],
                                                 Ub[0:XROWS, w, ds(s0, CH), :].unsqueeze(2).broadcast_to([XROWS, CH, GB, N]),
                                                 rowmask[0:XROWS, :].unsqueeze(1).unsqueeze(3).broadcast_to([XROWS, CH, GB, N]),
                                                 ALU.mult).then_inc(pl_st, 1)
                            pl.tensor_tensor(diag_of(By, h, XROWS), bet[0:XROWS, :, ds(s0, CH)].unsqueeze(3).broadcast_to([XROWS, QW, CH, GB]),
                                             rowmask[0:XROWS, :].unsqueeze(1).unsqueeze(1).broadcast_to([XROWS, QW, CH, GB]),
                                             ALU.mult).then_inc(pl_st, 1)
                            pl.tensor_tensor(diag_of(Wy, h, P), Cc[:, :, ds(s0, CH)].unsqueeze(3).broadcast_to([P, QW, CH, GB]),
                                             bmask.unsqueeze(1).unsqueeze(1).broadcast_to([P, QW, CH, GB]),
                                             ALU.mult).then_inc(pl_st, 1)
                            pl.tensor_copy(Ast[:, h, :, :], At[:, :, ds(s0, CH)]).then_inc(pl_st, 1)
                            pl.tensor_copy(kst[:, h, :], kap[:, ds(c2 * 2 + h, 1)]).then_inc(pl_st, 1)
                    pl.wait_ge(ep_y, pi + 1)
                    pl.tensor_tensor(W64[:, :, :], Cc[:, :, S:S + 1].broadcast_to([P, QW, GB]),
                                     bmask.unsqueeze(1).broadcast_to([P, QW, GB]), ALU.mult).then_inc(ep_w, 1)

        @block.scalar
        def _(act):
            act.wait_ge(ld, 16 * 6)
            act.wait_ge(cst, 9)
            act.activation(condsq[:, :, :], cond[:, :, :], ACT.Square).then_inc(csq_r, 1)
            with act.Fori(0, LAYERS) as l:
                act.wait_ge(w_in, l * 16 + 16)
                act.wait_ge(x_done, l * G + 1)
                act.activation(Wsq[:, :, :, :], W[:, :, :, :], ACT.Square).then_inc(wsq_r, 1)
                act.wait_ge(dco_e, l * 2 + 2)
                act.activation(dlg[:, :], dsq[:, :], ACT.Ln, bias=eps[:, 2:3]).then_inc(dlg_r, 1)
                act.wait_ge(dlg_r, l + 1)
                act.activation(dco[:, :, :, :].rearrange("p w c b -> p (w c b)"), dlg[:, :], ACT.Exp, scale=-0.5).then_inc(dco_g, 1)
                with act.Fori(0, G) as g:
                    it = l * G + g
                    act.wait_ge(x_done, it + 1)
                    act.wait_ge(xm_r, it + 1)
                    act.activation(sq[:, :, :], xm[:, :, :], ACT.Square).then_inc(sq_r, 1)
                    act.wait_ge(var_r, it + 1)
                    act.activation(lg[:, :], PS[:, 7, :], ACT.Ln, bias=eps[:, 0:1]).then_inc(rg_r, 1)
                    act.wait_ge(rg_r, it * 2 + 1)
                    act.activation(rstd[:, :], lg[:, :], ACT.Exp, scale=-0.5).then_inc(rg_r, 1)
                    for c in range(HC):
                        act.wait_ge(k_mm, it * 2 + c + 1)
                        for e in range(2):
                            act.activation(kz[:, c, e, :], PS[:, 4 + c, :], ACT.Copy, scale=par[e]).then_inc(k_r, 1)
                    for c in range(HC):
                        act.wait_ge(v_mm, it * 2 + c + 1)
                        act.activation(vTd[:, c, :, :, :],
                                       PS[:, c, :].rearrange("p (b t) -> p b t", t=S).unsqueeze(2).broadcast_to([P, GB, 2, S]),
                                       ACT.Copy).then_inc(v_r, 1)
                    for r in range(2):
                        act.wait_ge(sub_r, it * 2 + r + 1)
                        act.activation(ex[:, r, :, :], ex[:, r, :, :], ACT.Exp).then_inc(exp_r, 1)
                        for bp in range(2):
                            act.wait_ge(pt_mm, it * 4 + 2 * r + bp + 1)
                            if r:
                                act.wait_ge(av_mm, it * 2 + 1)
                            act.activation(pT[:, bp, :, :], PS[:, 4:6, :].rearrange("p a (e k) -> p (a e) k", k=P), ACT.Copy).then_inc(pt_r, 1)

            act.wait_ge(x_done, LAYERS * G + 1)
            act.sem_inc(y_out[0], 64)
            act.sem_inc(y_out[1], 64)
            act.sem_inc(ep_out, 16)
            with act.Fori(0, LAYERS) as l:
                act.wait_ge(sw_in, l * 112 + 112)
                act.wait_ge(po_done, l * G + 1)
                alone(act)
                act.activation(tA[:, :], dtp[:, 1:2], ACT.Tanh).then_inc(tA_r, 1)
                with act.Fori(0, G) as g:
                    it = l * G + g
                    act.wait_ge(f_it, it + 1)
                    for m in range(DC):
                        act.wait_ge(g_mm, it * DC + m + 1)
                        act.activation(sgt[:, m, :], PS[:, 4 + m, :], ACT.Tanh, scale=0.5).then_inc(sgt_r, 1)
                    for m in range(DC):
                        act.wait_ge(xp_r, it * DC + m + 1)
                        act.activation(acc[:, m, :].rearrange("p (b t) -> p b t", t=S), xp[:, m, :, 3:3 + S], ACT.Identity,
                                       scale=Wc[:, m, 3:4], bias=Ch[:, m, 0:1]).then_inc(acc_r, 1)
                    for m in range(DC):
                        act.wait_ge(cv_r, it * 12 + 2 * DC + m + 1)
                        act.activation(th[:, m, :], acc[:, m, :], ACT.Tanh, scale=0.5).then_inc(th_r, 1)
                    for m in range(DC):
                        act.wait_ge(zc_r, it * DC + m + 1)
                        act.activation(zq[:, m, :], z[:, m, :], ACT.Square).then_inc(zq_r, 1)
                    act.wait_ge(zv_mm, it + 1)
                    act.activation(zlg[:, :], PS[:, 1, :], ACT.Ln, bias=eps[:, 1:2]).then_inc(zg_r, 1)
                    act.wait_ge(zg_r, it * 2 + 1)
                    act.activation(zr[:, :], zlg[:, :], ACT.Exp, scale=-0.5).then_inc(zg_r, 1)
                    for m in range(DC):
                        act.wait_ge(xg_r, it * DC + m + 1)
                        act.activation(z[:, m, :], xnb[:, m, :], ACT.Identity, bias=Ch[:, m, 2:3]).then_inc(xf_r, 1)
                    for m in range(DC):
                        act.wait_ge(xf_r, it * DC + m + 1)
                        if m == 0:
                            act.wait_ge(zv_mm, it + 1)
                        act.activation(zq[:, m, :], z[:, m, :], ACT.Square).then_inc(x2_r, 1)
                    act.wait_ge(pr_s, it * 4 + 1)
                    act.activation(n4[:, :], n2[:, :], ACT.Ln).then_inc(ng_r, 1)
                    act.wait_ge(ng_r, it * 2 + 1)
                    act.activation(mn[:, :], n4[:, :], ACT.Exp, scale=-0.5).then_inc(ng_r, 1)
                    act.wait_ge(dt_mm, it + 1)
                    act.activation(dts[:, :], PS[0:N, 5, :], ACT.Copy).then_inc(dts_r, 1)
                    act.wait_ge(bc_mm, it * 2 + 2)
                    act.activation(Cn[:, :], PS[0:N, 4, :], ACT.Copy).then_inc(C_r, 1)
                    act.wait_ge(dt2_mm, it + 1)
                    act.activation(dtt[:, :], PS[0:N, 6, :], ACT.Tanh, bias=dtp[:, 0:1]).then_inc(dtt_r, 1)
                    for k in range(TT):
                        act.wait_ge(xt_mm, it * TT + k + 1)
                        act.activation(xh[:, k, :], PS[:, k, :], ACT.Copy).then_inc(xh_r, 1)
                        act.wait_ge(xr1_r, it * TT + k + 1)
                        act.activation(xmi[:, k, :], xr1[:, k, :], ACT.Copy).then_inc(xmi_r, 1)

                with act.Fori(0, PASSES) as ps:
                    pi = l * PASSES + ps
                    with act.Fori(0, CHUNKS // 2) as c2:
                        for h in range(2):
                            cn = pi * CHUNKS + c2 * 2 + h
                            act.wait_ge(pl_st, cn * 8 + 8 + 1)
                            for t in range(CH):
                                for w in range(QW):
                                    if w % 2 == 0:
                                        act.wait_ge(dv_q, cn * (2 * CH) + 2 * t + w // 2 + 1 + 2)
                                    act.activation(R[:, w, :], q[:, t % 2, w, :], ACT.Relu,
                                                   scale=Ast[:, h, w, t:t + 1]).then_inc(ac_r, 1)

        @block.tensor
        def _(pe):
            def project(bank, w, rhs, done, chunks=HC):
                for m in range(HC):
                    for c in range(HC):
                        mm = pe.matmul(PS[:, bank + m, :], W[:, w, c, m * P:(m + 1) * P], rhs[:, c, :],
                                       start=(c == 0), stop=(c == HC - 1))
                    mm.then_inc(done, 1)

            pe.wait_ge(cst, 9)
            pe.wait_ge(ld, 16 * 6)
            pe.wait_ge(csq_r, 1)
            with pe.Fori(0, LAYERS) as l:
                pe.wait_ge(wsq_r, l + 1)
                pe.wait_ge(x_done, l * G + 1)
                for w in range(5):
                    st = 0 if w < 3 else HC
                    for m in range(HC):
                        for c in range(HC):
                            mm = pe.matmul(PS[:, w // 4, (w % 4) * P + m * B:(w % 4) * P + (m + 1) * B],
                                           Wsq[:, w, c, m * P:(m + 1) * P], condsq[:, st + c, :],
                                           start=(c == 0), stop=(c == HC - 1))
                mm.then_inc(dco_mm, 1)
                pe.wait_ge(dco_e, l * 2 + 2)
                alone(pe)
                with pe.Fori(0, G) as g:
                    it = l * G + g
                    pe.wait_ge(x_done, it + 1)
                    pe.wait_ge(xs_r, it + 1)
                    for c in range(HC):
                        mm = pe.matmul(PS[:, 6, :], ones_h[:, :], xs[:, c, :], start=(c == 0), stop=(c == HC - 1))
                    mm.then_inc(mean_r, 1)
                    pe.wait_ge(sq_r, it + 1)
                    for c in range(HC):
                        mm = pe.matmul(PS[:, 7, :], ones_h[:, :], sq[:, c, :], start=(c == 0), stop=(c == HC - 1))
                    mm.then_inc(var_r, 1)
                    pe.wait_ge(xn_r, it + 1)
                    project(4, 1, xn, k_mm)
                    project(6, 0, xn, q_mm)
                    project(0, 2, xn, v_mm)

                    pe.wait_ge(q_r, it * 2 + 2)
                    pe.wait_ge(k_r, it * 4 + 4)
                    pe.wait_ge(v_r, it * 2 + 2)
                    for r in range(2):
                        if r:
                            pe.wait_ge(sub_r, it * 2 + 1)
                        for j in range(4):
                            for b in range(4):
                                for c in range(HC):
                                    bb = 4 * r + b
                                    col = ((b // 2) * HC + c) * P
                                    mm = pe.matmul(PS[(b % 2) * S:(b % 2 + 1) * S, j, col:col + P],
                                                   qs[32 * j:32 * j + 32, c, bb * S:(bb + 1) * S],
                                                   kz[32 * j:32 * j + 32, c, :, bb * S:(bb + 1) * S],
                                                   start=True, stop=True)
                        mm.then_inc(sc_mm, 1)
                        if r == 0:
                            for b2 in range(GB // 2):
                                bank = 6 + b2 % 2
                                if b2 >= 2:
                                    pe.wait_ge(vbd_r, it * 4 + b2 - 1)
                                for bb in (2 * b2, 2 * b2 + 1):
                                    for c in range(HC):
                                        col = (bb % 2) * H + c * P
                                        mm = pe.transpose(PS[:, bank, col:col + P],
                                                          vTd[:, c, bb, :, :].rearrange("p a t -> p (a t)"), ident[:, :])
                                mm.then_inc(vt_mm, 1)
                            pe.wait_ge(vbd_r, it * 4 + 4)
                        for bp in range(2):
                            pe.wait_ge(pn_r, it * 2 + r + 1)
                            if (r, bp) != (0, 0):
                                pe.wait_ge(pt_r, it * 4 + 2 * r + bp)
                            for c in range(HC):
                                for j in range(4):
                                    col = (bp * HC + c) * P
                                    mm = pe.transpose(PS[:, 4 + c, j * P:(j + 1) * P], pn[:, r, j, col:col + P], ident[:, :])
                            mm.then_inc(pt_mm, 1)
                        for bp in range(2):
                            pe.wait_ge(pt_r, it * 4 + 2 * r + bp + 1)
                            for b in range(2):
                                bb = 4 * r + 2 * bp + b
                                for c in range(HC):
                                    for j in range(4):
                                        col = c * (4 * S) + (2 * bp + b) * S
                                        mm = pe.matmul(PS[32 * j:32 * j + 32, 6 + r, col:col + S],
                                                       vbd[:, bb, c * 4 + j, :, :].rearrange("p a d -> p (a d)"),
                                                       pT[:, bp, c * 4 + j, b * S:(b + 1) * S], start=True, stop=True)
                        mm.then_inc(av_mm, 1)
                    pe.wait_ge(sub_r, it * 2 + 2)
                    pe.wait_ge(vs_r, it + 1)
                    project(2, 4, vsc, u_mm)
                    pe.wait_ge(av_r, it * 2 + 2)
                    project(0, 3, av, w_mm)

            pe.wait_ge(x_done, LAYERS * G + 1)
            pe.sem_inc(pe_yq, 16)
            pe.sem_inc(ep_y, 1)
            with pe.Fori(0, LAYERS) as l:
                pe.wait_ge(sw_in, l * 112 + 112)
                pe.wait_ge(po_done, l * G + 1)
                alone(pe)
                with pe.Fori(0, G) as g:
                    it = l * G + g
                    pe.wait_ge(f_it, it + 1)
                    for m in range(2 * DC):
                        for c in range(HC):
                            mm = pe.matmul(PS[:, m, :], Win[:, c, m * P:(m + 1) * P],
                                           X[:, ds(g, 1), c, :].rearrange("p a t -> p (a t)"), start=(c == 0), stop=(c == HC - 1))
                        mm.then_inc(xr_mm if m < DC else g_mm, 1)
                    pe.wait_ge(z_r, it * DC + DC)
                    for m in range(DC):
                        mm = pe.matmul(PS[:, 0, :], ones_d[:, :], z[:, m, :], start=(m == 0), stop=(m == DC - 1))
                    mm.then_inc(zm_mm, 1)
                    for m in range(DC):
                        pe.wait_ge(zq_r, it * DC + m + 1)
                        mm = pe.matmul(PS[:, 1, :], ones_d[:, :], zq[:, m, :], start=(m == 0), stop=(m == DC - 1))
                    mm.then_inc(zv_mm, 1)
                    pe.wait_ge(xf_r, it * DC + DC)
                    pe.wait_ge(sg_r, it * DC + DC)
                    for k, bank, done in ((2, 5, dt_mm), (0, 3, bc_mm), (1, 4, bc_mm)):
                        for m in range(DC):
                            mm = pe.matmul(PS[0:N, bank, :], Wx[:, m, k * N:(k + 1) * N], z[:, m, :],
                                           start=(m == 0), stop=(m == DC - 1))
                        mm.then_inc(done, 1)
                    for m in range(DC):
                        pe.wait_ge(x2_r, it * DC + m + 1)
                        mm = pe.matmul(PS[0:N, 2, :], ones_n[:, :], zq[:, m, :], start=(m == 0), stop=(m == DC - 1))
                    mm.then_inc(nrm_mm, 1)
                    pe.wait_ge(dts_r, it + 1)
                    alone(pe)
                    pe.matmul(PS[0:N, 6, :], Wdt[:, :], dts[:, :], start=True, stop=True).then_inc(dt2_mm, 1)
                    pe.wait_ge(C_r, it + 1)
                    pe.matmul(PS[:, 7, :], sel[:, :], Cn[:, :], start=True, stop=True).then_inc(pk_mm, 1)
                    pe.wait_ge(pr_s, it * 4 + 3)
                    pe.matmul(PS[:, 5, :], sel[:, :], am[:, :], start=True, stop=True).then_inc(pk_mm, 1)
                    pe.wait_ge(stk_r, it * 5 + 5)
                    pe.wait_ge(dtt_r, it + 1)
                    for k in range(TT):
                        mm = pe.transpose(PS[:, 6, k * 112:(k + 1) * 112], stk[:, k * P:(k + 1) * P], ident[0:112, 0:112])
                    mm.then_inc(tok_mm, 1)
                    pe.wait_ge(pr_s, it * 4 + 4)
                    for k in range(TT):
                        for m in range(DC):
                            mm = pe.transpose(PS[:, k, m * P:(m + 1) * P], z[:, m, k * P:(k + 1) * P], ident[:, :])
                        mm.then_inc(xt_mm, 1)

                pe.wait_ge(f_it, l * G + G + 1)
                alone(pe)
                with pe.Fori(0, PASSES) as ps:
                    pi = l * PASSES + ps
                    pe.wait_ge(set_r, l * 6 + 6)
                    alone(pe)
                    with pe.Fori(0, CHUNKS // 2) as c2:
                        for h in range(2):
                            cn = pi * CHUNKS + c2 * 2 + h
                            sn = cn * (2 * CH)
                            pe.wait_ge(xq_in[h], (pi * (CHUNKS // 2) + c2) * (XQ * 16) + XQ * 16)
                            pe.wait_ge(pl_st, cn * 8 + 8 + 1)
                            pe.wait_ge(dv_y, cn + 1)

                            def y_of(t, p):
                                pe.wait_ge(dv_q, sn + 2 * t + p + 1 + 2)
                                for w in (2 * p, 2 * p + 1):
                                    pe.matmul(PS[32 * w:32 * w + 32, 4 + h, :], Wy[:, h, w, t * 32:(t + 1) * 32],
                                              q[:, t % 2, w, :], start=(t == 0), stop=False, skip_group_check=True)
                                for w in (2 * p, 2 * p + 1):
                                    mm = pe.matmul(PS[32 * w:32 * w + 32, 4 + h, :], By[0:XROWS, h, w, t * 32:(t + 1) * 32],
                                                   xq[0:XROWS, h, w, t, :], start=False, stop=(t == CH - 1), skip_group_check=True)
                                mm.then_inc(pe_yq, 1)
                                return mm

                            for t in range(CH):
                                for p in range(2):
                                    pe.wait_ge(dv_q, sn + 2 * t + p + 1)
                                    for w in (2 * p, 2 * p + 1):
                                        mm = pe.matmul(PS[:, w, :], Uw[0:KROWS, h, w, t, :, :].rearrange("p b n -> p (b n)"),
                                                       xq[0:KROWS, h, w, t, :], start=True, stop=True)
                                    mm.then_inc(pe_w, 1)
                                if t:
                                    y_of(t - 1, 0)
                                    y_of(t - 1, 1)
                            y_of(CH - 1, 0)
                            y_of(CH - 1, 1)
                    pe.wait_ge(ep_q, pi + 1)
                    pe.wait_ge(ep_w, pi + 2)
                    for w in range(QW):
                        mm = pe.matmul(PS[32 * w:32 * w + GB, 6, :], W64[:, w, :], q[:, 0, w, :], start=True, stop=True)
                    mm.then_inc(ep_y, 1)

                with pe.Fori(0, G) as g:
                    it = l * G + g
                    pe.wait_ge(ep_r, l * (PASSES * QW) + PASSES * QW + 1)
                    pe.wait_ge(dv_y, l * (PASSES * CHUNKS) + PASSES * CHUNKS + 2)
                    pe.wait_ge(po_in, it * 64 + 64)
                    pe.wait_ge(po_done, it + 1)
                    for m in range(DC):
                        for k in range(TT):
                            mm = pe.transpose(PS[:, m, k * P:(k + 1) * P], yt[:, k, m * P:(m + 1) * P], ident[:, :])
                        mm.then_inc(po_mm, 1)
                    for m in range(HC):
                        for c in range(DC):
                            if m == 0:
                                pe.wait_ge(yg_r, it * DC + c + 1)
                            mm = pe.matmul(PS[:, 4 + m, :], Wo[:, c, m * P:(m + 1) * P], yg[:, c, :],
                                           start=(c == 0), stop=(c == DC - 1))
                        mm.then_inc(o_mm, 1)

        @block.vector
        def _(v):
            def tiled(ap):
                return ap.rearrange("p (b t) -> p b t", t=S)

            def by_batch(tab, c, g):
                return tab[:, c, ds(g * GB, GB)].unsqueeze(2).broadcast_to([P, GB, S])

            def root(y, x, e, y0, tmp, done, n):
                v.scalar_tensor_tensor(out=tmp, in0=x, scalar=e, in1=y0, op0=ALU.add, op1=ALU.mult).then_inc(done, 1)
                v.wait_ge(done, n + 1)
                v.scalar_tensor_tensor(out=tmp, in0=tmp, scalar=-0.5, in1=y0, op0=ALU.mult, op1=ALU.mult).then_inc(done, 1)
                v.wait_ge(done, n + 2)
                v.scalar_tensor_tensor(out=y, in0=tmp, scalar=1.5, in1=y0, op0=ALU.add, op1=ALU.mult).then_inc(done, 1)
                v.wait_ge(done, n + 3)

            v.wait_ge(ld, 16 * 6)
            v.tensor_scalar(nmask[:, :], bmask, -1.0, None, ALU.mult).then_inc(cst, 1)
            v.sem_inc(x_done, 1)
            with v.Fori(0, LAYERS) as l:
                v.wait_ge(dco_mm, l + 1)
                dcv = dco[:, :, :, :].rearrange("p w c b -> p (w c b)")
                v.tensor_copy(dsq[:, 0:512], PS[:, 0, :]).then_inc(dco_e, 1)
                v.tensor_copy(dsq[:, 512:5 * P], PS[:, 1, 0:P]).then_inc(dco_e, 1)
                v.wait_ge(dco_e, l * 2 + 2)
                v.wait_ge(dco_g, l + 1)
                root(dcv, dsq[:, :], EPS_DM, dcv, dt1[:, :], dco_r, l * 3)
                v.scalar_tensor_tensor(out=qk_t[:, :, :], in0=dco[:, 0, :, :], scalar=float(HD) ** -0.5,
                                       in1=dco[:, 1, :, :], op0=ALU.mult, op1=ALU.mult).then_inc(tab_r, 1)
                v.tensor_tensor(vs_t[:, :, :], dco[:, 2, :, :], cond[:, HC:2 * HC, :], ALU.mult).then_inc(tab_r, 1)
                v.wait_ge(tab_r, l * 2 + 2)
                alone(v)
                with v.Fori(0, G) as g:
                    it = l * G + g
                    v.wait_ge(x_done, it + 1)
                    v.tensor_tensor(xs[:, :, :].rearrange("p c (b t) -> p c b t", t=S),
                                    X[:, ds(g, 1), :, :].rearrange("p a c (b t) -> p (a c) b t", t=S),
                                    cond[:, 0:HC, ds(g * GB, GB)].unsqueeze(3).broadcast_to([P, HC, GB, S]),
                                    ALU.mult).then_inc(xs_r, 1)
                    v.wait_ge(mean_r, it + 1)
                    v.tensor_tensor(xm[:, :, :], xs[:, :, :], PS[:, 6:7, :].broadcast_to([P, HC, TOK]),
                                    ALU.subtract).then_inc(xm_r, 1)
                    v.wait_ge(var_r, it + 1)
                    v.wait_ge(rg_r, it * 2 + 2)
                    root(rstd[:, :], PS[:, 7, :], EPS_IN, rstd[:, :], vare[:, :], rstd_r, it * 3)
                    v.tensor_tensor(xn[:, :, :], xm[:, :, :], rstd[:, :].unsqueeze(1).broadcast_to([P, HC, TOK]),
                                    ALU.mult).then_inc(xn_r, 1)
                    for c in range(HC):
                        v.wait_ge(q_mm, it * 2 + c + 1)
                        v.tensor_tensor(tiled(qs[:, c, :]), tiled(PS[:, 6 + c, :]), by_batch(qk_t, c, g),
                                        ALU.mult).then_inc(q_r, 1)

                    def scores(r):
                        sc = PS[:, 0:4, :].rearrange("p j (e k) -> p (j e) k", k=S)
                        v.wait_ge(sc_mm, it * 2 + r + 1)
                        v.tensor_reduce(mx[:, r, :], sc, AX.X, ALU.max).then_inc(max_r, 1)
                        v.wait_ge(max_r, it * 2 + r + 1)
                        v.tensor_tensor(ex[:, r, :, :].rearrange("p j (e k) -> p (j e) k", k=S), sc,
                                        mx[:, r, :].unsqueeze(2).broadcast_to([P, 32, S]), ALU.subtract).then_inc(sub_r, 1)

                    def sums(r):
                        v.wait_ge(exp_r, it * 2 + r + 1)
                        v.tensor_reduce(sm[:, r, :], ex[:, r, :, :].rearrange("p j (e k) -> p (j e) k", k=S),
                                        AX.X, ALU.add).then_inc(sum_r, 1)
                        v.wait_ge(sum_r, it * 2 + r + 1)
                        v.reciprocal(rs[:, r, :], sm[:, r, :]).then_inc(rcp_r, 1)

                    def out_of(r):
                        v.wait_ge(av_mm, it * 2 + r + 1)
                        v.tensor_tensor(av[:, :, r * 4 * S:(r + 1) * 4 * S].rearrange("p c (b t) -> p c b t", t=S),
                                        PS[:, 6 + r, :].rearrange("p (c b t) -> p c b t", c=HC, t=S),
                                        vs_t[:, :, ds(g * GB + 4 * r, 4)].unsqueeze(3).broadcast_to([P, HC, 4, S]),
                                        ALU.mult).then_inc(av_r, 1)

                    scores(0)
                    for b2 in range(GB // 2):
                        v.wait_ge(vt_mm, it * 4 + b2 + 1)
                        v.tensor_tensor(vbd[:, 2 * b2:2 * b2 + 2, :, :, :].rearrange("p b h e d -> p (b h) e d"),
                                        PS[:, 6 + b2 % 2, :].rearrange("p (m e d) -> p m e d", e=2, d=HD),
                                        half.unsqueeze(1).unsqueeze(3).broadcast_to([P, 2 * (H // 32), 2, HD]),
                                        ALU.mult).then_inc(vbd_r, 1)
                    sums(0)
                    scores(1)
                    sums(1)
                    out_of(0)
                    out_of(1)
                    for c in range(HC):
                        v.wait_ge(u_mm, it * 2 + c + 1)
                        v.tensor_tensor(tiled(t2[:, c, :]), tiled(PS[:, 2 + c, :]), by_batch(dco[:, 4, :, :], c, g),
                                        ALU.mult).then_inc(t2_r, 1)
                    for c in range(HC):
                        v.wait_ge(w_mm, it * 2 + c + 1)
                        v.tensor_tensor(tiled(t1[:, c, :]), tiled(PS[:, c, :]), by_batch(dco[:, 3, :, :], c, g),
                                        ALU.mult).then_inc(t1_r, 1)
                    v.wait_ge(t3_r, it + 1)
                    xg = X[:, ds(g, 1), :, :].rearrange("p a c t -> p (a c t)")
                    v.tensor_tensor(xg, xg, t3[:, :, :].rearrange("p c t -> p (c t)"), ALU.add).then_inc(x_done, 1)

            v.wait_ge(x_done, LAYERS * G + 1)
            v.sem_inc(po_done, 1)
            v.sem_inc(dv_q, 2)
            v.sem_inc(ac_r, 20)
            v.sem_inc(dv_y, 2)
            v.sem_inc(ep_r, 1)
            with v.Fori(0, LAYERS) as l:
                v.wait_ge(po_done, l * G + 1)
                v.wait_ge(tA_r, l + 1)
                v.tensor_scalar(A01[:, :], tA[:, :], -0.01, None, ALU.mult).then_inc(A_r, 1)
                v.memset(xp[:, :, :, 0:3], 0.0).then_inc(A_r, 1)
                v.memset(stk[:, :], 0.0).then_inc(A_r, 1)
                v.memset(ccs[:, 0:1], 0.0).then_inc(A_r, 1)
                v.wait_ge(A_r, l * 4 + 4)
                alone(v)
                with v.Fori(0, G) as g:
                    it = l * G + g
                    v.wait_ge(f_it, it + 1)
                    for m in range(DC):
                        v.wait_ge(xr_mm, it * DC + m + 1)
                        v.tensor_tensor(xp[:, m, :, 3:3 + S], tiled(PS[:, m, :]), by_batch(cond, m, g), ALU.add).then_inc(xp_r, 1)
                    for m in range(DC):
                        v.wait_ge(sgt_r, it * DC + m + 1)
                        v.scalar_tensor_tensor(out=sg[:, m, :], in0=sgt[:, m, :], scalar=1.0, in1=PS[:, 4 + m, :],
                                               op0=ALU.add, op1=ALU.mult).then_inc(sg_r, 1)
                    for j in range(3):
                        for m in range(DC):
                            if j == 0:
                                v.wait_ge(acc_r, it * DC + m + 1)
                            else:
                                v.wait_ge(cv_r, it * 12 + (j - 1) * DC + m + 1)
                            v.scalar_tensor_tensor(out=tiled(acc[:, m, :]), in0=xp[:, m, :, j:j + S], scalar=Wc[:, m, j:j + 1],
                                                   in1=tiled(acc[:, m, :]), op0=ALU.mult, op1=ALU.add).then_inc(cv_r, 1)
                    for m in range(DC):
                        v.wait_ge(th_r, it * DC + m + 1)
                        v.scalar_tensor_tensor(out=z[:, m, :], in0=th[:, m, :], scalar=1.0, in1=acc[:, m, :],
                                               op0=ALU.add, op1=ALU.mult).then_inc(z_r, 1)
                    v.wait_ge(zm_mm, it + 1)
                    for m in range(DC):
                        v.tensor_tensor(z[:, m, :], z[:, m, :], PS[:, 0, :], ALU.subtract).then_inc(zc_r, 1)
                    v.wait_ge(zv_mm, it + 1)
                    v.wait_ge(zg_r, it * 2 + 2)
                    root(zr[:, :], PS[:, 1, :], 4 * EPS_IN, zr[:, :], zve[:, :], zr_r, it * 3)
                    for m in range(DC):
                        v.scalar_tensor_tensor(out=xnb[:, m, :], in0=z[:, m, :], scalar=Ch[:, m, 1:2], in1=zr[:, :],
                                               op0=ALU.mult, op1=ALU.mult).then_inc(xg_r, 1)
                    v.wait_ge(nrm_mm, it + 1)
                    v.tensor_scalar(n2[:, :], PS[0:N, 2, :], 1.0, LEAST, ALU.min, ALU.max).then_inc(pr_s, 1)
                    v.wait_ge(pr_s, it * 4 + 1)
                    v.wait_ge(ng_r, it * 2 + 2)
                    root(mn[:, :], n2[:, :], 0.0, mn[:, :], n3[:, :], mn_r, it * 3)
                    v.wait_ge(bc_mm, it * 2 + 1)
                    v.tensor_tensor(mn[:, :], mn[:, :], n2[:, :], ALU.mult).then_inc(mm_r, 1)
                    v.wait_ge(mm_r, it + 1)
                    v.tensor_tensor(Bd[:, :], PS[0:N, 3, :], mn[:, :], ALU.mult).then_inc(pr_s, 1)
                    v.wait_ge(dtt_r, it + 1)
                    v.tensor_scalar(am[:, :], dtt[:, :], A01[:, 0:1], 1.0, ALU.mult, ALU.add).then_inc(pr_s, 1)
                    v.wait_ge(pr_s, it * 4 + 3)
                    v.reciprocal(rA[:, :], am[:, :]).then_inc(pr_s, 1)
                    v.wait_ge(pr_s, it * 4 + 4)
                    v.wait_ge(C_r, it + 1)
                    v.tensor_tensor(stk[0:N, :], Bd[:, :], rA[:, :], ALU.mult).then_inc(stk_r, 1)
                    v.tensor_scalar(stk[32:32 + N, :], rA[:, :], -CLIP, CLIP, ALU.mult, ALU.add).then_inc(stk_r, 1)
                    v.scalar_tensor_tensor(out=tiled(stk[96:96 + N, :])[:, :, 0:S - 1], in0=tiled(rA[:, :])[:, :, 1:S], scalar=CLIP,
                                           in1=tiled(Cn[:, :])[:, :, 0:S - 1], op0=ALU.mult, op1=ALU.mult).then_inc(stk_r, 1)
                    v.tensor_scalar(tiled(stk[96:96 + N, :])[:, :, S - 1:S], tiled(Cn[:, :])[:, :, S - 1:S], CLIP, None,
                                    ALU.mult).then_inc(stk_r, 1)
                    v.wait_ge(stk_r, it * 5 + 1)
                    v.tensor_tensor(tiled(stk[64:64 + N, :])[:, :, 0:S - 1], tiled(Cn[:, :])[:, :, 0:S - 1],
                                    tiled(stk[0:N, :])[:, :, 1:S], ALU.mult).then_inc(stk_r, 1)
                    for n, (bank, mask, dst) in enumerate(((7, nmask[:, :], ccs[:, 1:S + 1]), (5, bmask, acs[:, :]))):
                        v.wait_ge(pk_mm, it * 2 + n + 1)
                        v.tensor_tensor(pick[:, n, :, :], tiled(PS[:, bank, :]), mask.unsqueeze(2).broadcast_to([P, GB, S]),
                                        ALU.mult).then_inc(pk_r, 1)
                        v.wait_ge(pk_r, it * 2 + n + 1)
                        v.tensor_reduce(dst, pick[:, n, :, :].rearrange("p b t -> p t b"), AX.X, ALU.add).then_inc(pick_s, 1)
                    v.wait_ge(tok_mm, it + 1)
                    rows = PS[:, 6, 0:TT * 112].rearrange("p (k r) -> p k r", r=112)
                    v.tensor_copy(tv[:, :, 0:N], rows[:, :, 0:N]).then_inc(tv_s, 1)
                    v.tensor_copy(tv[:, :, N:2 * N], rows[:, :, 32:32 + N]).then_inc(tv_s, 1)
                    v.tensor_reduce(bsum[:, :], rows[:, :, 64:64 + N], AX.X, ALU.add).then_inc(tv_s, 1)
                    v.tensor_reduce(kp[:, :], rows[:, :, 96:96 + N], AX.X, ALU.add).then_inc(tv_s, 1)
                    v.wait_ge(tv_s, it * 9 + 3)
                    v.tensor_scalar(tv[:, :, 2 * N:2 * N + 1], bsum[:, :].unsqueeze(2), -1.0, None, ALU.mult).then_inc(tv_s, 1)
                    v.wait_ge(tv_s, it * 9 + 5)
                    v.tensor_copy(tvp[:, 0, :, :], tv[:, :, :]).then_inc(tv_s, 1)
                    v.wait_ge(tv_s, it * 9 + 6)
                    v.tensor_tensor(tvr[:, :, :], tv[:, :, :], tvp[:, 0, :, :], ALU.subtract).then_inc(tv_s, 1)
                    v.wait_ge(tv_s, it * 9 + 7)
                    v.tensor_copy(tvp[:, 1, :, :], tvr[:, :, :]).then_inc(tv_s, 1)
                    v.wait_ge(tv_s, it * 9 + 8)
                    v.tensor_tensor(tvp[:, 2, :, :], tvr[:, :, :], tvp[:, 1, :, :], ALU.subtract).then_inc(tv_s, 1)
                    for k in range(TT):
                        v.wait_ge(xh_r, it * TT + k + 1)
                        v.tensor_tensor(xr1[:, k, :], PS[:, k, :], xh[:, k, :], ALU.subtract).then_inc(xr1_r, 1)

                v.wait_ge(set_r, l * 6 + 6)
                alone(v)
                with v.Fori(0, PASSES) as ps:
                    pi = l * PASSES + ps
                    v.wait_ge(ep_y, pi + 1)
                    v.memset(R[:, :, :], CLIP).then_inc(r_init, 1)
                    v.wait_ge(r_init, pi + 1)
                    alone(v)
                    with v.Fori(0, CHUNKS // 2) as c2:
                        for h in range(2):
                            cn = pi * CHUNKS + c2 * 2 + h
                            for t in range(CH):
                                for p in range(2):
                                    n = 2 * t + p
                                    v.wait_ge(pe_w, cn * (2 * CH) + n + 1)
                                    v.wait_ge(ac_r, cn * (4 * CH) + 4 * t + 2 * p + 18)
                                    v.wait_ge(pe_yq, cn * (2 * CH) + n + 13)
                                    v.scalar_tensor_tensor(out=q[:, t % 2, 2 * p:2 * p + 2, :].rearrange("p w c -> p (w c)"),
                                                           in0=R[:, 2 * p:2 * p + 2, :].rearrange("p w c -> p (w c)"), scalar=2 * CLIP,
                                                           in1=PS[:, 2 * p:2 * p + 2, :].rearrange("p w c -> p (w c)"),
                                                           op0=ALU.min, op1=ALU.subtract).then_inc(dv_q, 1)
                            v.wait_ge(pe_yq, cn * (2 * CH) + 2 * CH + 16)
                            v.wait_ge(pl_st, cn * 8 + 9)
                            v.wait_ge(y_out[h], (pi * (CHUNKS // 2) + c2) * 64 + 64)
                            v.tensor_scalar(ys[:, h, :], PS[:, 4 + h, :], kst[:, h, :], None, ALU.add).then_inc(dv_y, 1)
                    v.wait_ge(ac_r, pi * (4 * S) + 4 * S + 20)
                    v.tensor_scalar(q[:, 0, :, :], R[:, :, :], 2 * CLIP, None, ALU.min).then_inc(ep_q, 1)
                    v.wait_ge(ep_y, pi + 2)
                    v.wait_ge(ep_out, pi * 64 + 16)
                    for w in range(QW):
                        v.tensor_scalar(ye[32 * w:32 * w + GB, :], PS[32 * w:32 * w + GB, 6, :],
                                        kap[32 * w:32 * w + GB, CHUNKS:CHUNKS + 1], None, ALU.add).then_inc(ep_r, 1)

                with v.Fori(0, G) as g:
                    it = l * G + g
                    v.wait_ge(po_in, it * 64 + 64)
                    for m in range(DC):
                        v.wait_ge(po_mm, it * DC + m + 1)
                        v.scalar_tensor_tensor(out=yf[:, m, :], in0=xnp[:, m, :], scalar=Ch[:, m, 3:4], in1=PS[:, m, :],
                                               op0=ALU.mult, op1=ALU.add).then_inc(yf_r, 1)
                        v.wait_ge(yf_r, it * DC + m + 1)
                        v.tensor_tensor(yg[:, m, :], yf[:, m, :], sgp[:, m, :], ALU.mult).then_inc(yg_r, 1)
                    v.wait_ge(o_mm, it * HC + HC)
                    xg = X[:, ds(g, 1), :, :].rearrange("p a c t -> p (a c t)")
                    v.scalar_tensor_tensor(out=xg, in0=PS[:, 4:6, :].rearrange("p c t -> p (c t)"), scalar=0.5,
                                           in1=xg, op0=ALU.mult, op1=ALU.add).then_inc(po_done, 1)


def kernel(**inputs):
    import concourse.bacc as bacc
    from concourse.bass_utils import run_bass_kernel_spmd

    a = {k: np.asarray(v) for k, v in inputs.items()}

    def cols(w):
        return w.T.reshape(-1, P, w.shape[0]).transpose(1, 0, 2)

    def chan(v):
        return v.reshape(-1, P, v.shape[-1]).transpose(1, 0, 2)

    def two(name, fn):
        return np.stack([fn(a[f"L{n}_cond_{name}"]) for n in (2, 3)])

    arrays = {
        "xT": a["x"].reshape(G, TOK, HC, P).transpose(3, 0, 2, 1),
        "condT": a["cond_2048"].reshape(B, DC, P).transpose(2, 1, 0),
        "attw": np.stack([np.stack([cols(a[f"L{n}_cond_{w}_weight"]) for w in "qkvwu"], axis=1) for n in (0, 1)]),
        "win": two("W_in", cols),
        "wconv": two("W_conv", lambda w: chan(w[:, 0, :])),
        "chan": np.stack([chan(np.stack([a[f"L{n}_cond_{v}"] for v in ("b_conv", "ln_g", "ln_b", "D")], axis=1)) for n in (2, 3)]),
        "wxp": two("W_xproj", cols),
        "wdt": two("W_dt", lambda w: w.T),
        "dtv": np.stack([np.stack([a[f"L{n}_cond_{v}"] for v in ("b_dt", "A_log")], axis=1) for n in (2, 3)]),
        "wout": two("W_out", cols),
    }
    p = np.arange(P)
    arrays["ident"] = np.eye(P, dtype=np.float32)
    arrays["sel"] = (p[None, :] % N == np.arange(N)[:, None]).astype(np.float32)
    arrays["masks"] = np.concatenate([(p[:, None] // HD % 2 == np.arange(2)), (p[:, None] // S == np.arange(2)),
                                      (p[:, None] // N == np.arange(GB))], axis=1).astype(np.float32)
    rowmask = ((p[:, None] % GB == np.arange(GB)) & (p[:, None] < XROWS)).astype(np.float32)

    nc = bacc.Bacc("TRN2", target_bir_lowering=False, num_devices=1)
    bf = mybir.dt.np(mybir.dt.bfloat16)
    arrays["rowmask"] = rowmask.astype(bf)
    feed, args = {}, []
    for name in ("xT", "condT", "attw", "win", "wconv", "chan", "wxp", "wdt", "dtv", "wout", "ident", "sel", "masks", "rowmask"):
        arr = np.ascontiguousarray(arrays[name])
        feed[f"in_{name}"] = arr
        args.append(nc.dram_tensor(f"in_{name}", arr.shape, mybir.dt.from_np(arr.dtype), kind="ExternalInput").ap())
    args.append(nc.dram_tensor("out_x", (P, G, HC, TOK), mybir.dt.float32, kind="ExternalOutput").ap())
    cond_resid_kernel(nc, *args)
    r = run_bass_kernel_spmd(nc, [feed], core_ids=[0])
    return np.ascontiguousarray(r.results[0]["out_x"].transpose(1, 3, 2, 0).reshape(B, S, H))
```

```python
import numpy as np
import concourse.bass as bass
from concourse import mybir
from contextlib import ExitStack

B, S, H, DI, N = 64, 64, 256, 512, 16
HEADS = 16
HD = H // HEADS
P = 128
GB = P // N
G = B // GB
TOK = GB * S
HC, DC = H // P, DI // P
TT = TOK // P
LAYERS = 2
QW = 4
PASSES = G // QW
CH = 4
CHUNKS = S // CH
PARTS = 3
XROWS = PARTS * PARTS * GB
CROW = XROWS
KROWS = CROW + PARTS
CLIP = 10.0
EPS_IN, EPS_DM = 1e-5, 1e-8
TABLES = 2 * PARTS * PARTS + 2 + QW * (CH + 1)
SSM_LOADS = 9
LEAST = 1e-18


def cond_resid_kernel(nc, xT, condT, attw, win, wconv, chan, wxp, wdt, dtv, wout,
                      ident_d, sel_d, masks_d, rowmask_d, out):
    f32, bf16 = mybir.dt.float32, mybir.dt.bfloat16
    ALU, ACT, AX = mybir.AluOpType, mybir.ActivationFunctionType, mybir.AxisListType
    ds = bass.ds

    def scratch(name, shape, dt):
        return nc.dram_tensor(name, shape, dt, kind="Internal").ap()

    xn_d = scratch("xn_d", (G, P, DC, TOK), f32)
    sg_d = scratch("sg_d", (G, P, DC, TOK), f32)
    xpart_d = scratch("xpart_d", (G, PARTS, GB, S * DI), bf16)
    bpart_d = scratch("bpart_d", (PARTS, G, GB, S * N), bf16)
    kpart_d = scratch("kpart_d", (PARTS, G, S, GB, N), bf16)
    beta_d = scratch("beta_d", (PARTS, B * S + S), bf16)
    kap_d = scratch("kap_d", (B * S + S,), f32)
    cc_d = scratch("cc_d", (G, P, S + 1), f32)
    a_d = scratch("a_d", (G, P, S), f32)
    y_d = scratch("y_d", (G, GB, S + 1, DI), f32)

    es = ExitStack()
    with es:
        es.enter_context(nc.allow_non_contiguous_dma(reason="a few short columns for each group"))

        def sem(name):
            return es.enter_context(nc.semaphore(name))

        def sb(name, shape, dt=f32, where=None):
            return (where or es).enter_context(nc.sbuf_tensor(name, shape, dt))

        PS = es.enter_context(nc.psum_tensor("PS", [P, 8, 512], f32))

        X = sb("X", [P, G, HC, TOK])
        cond = sb("cond", [P, DC, B])
        condsq = sb("condsq", [P, DC, B])
        ident = sb("ident", [P, P])
        sel = sb("sel", [N, GB, P])
        masks = sb("masks", [P, 12])
        rowmask = sb("rowmask", [P, GB], bf16)
        ones_h = sb("ones_h", [P, P])
        ones_d = sb("ones_d", [P, P])
        ones_n = sb("ones_n", [P, N])
        zero_f = sb("zero_f", [P, 1])
        zero_b = sb("zero_b", [P, 1], bf16)
        eps = sb("eps", [P, 3])
        par = [masks[:, 0:1], masks[:, 1:2]]
        half = masks[:, 2:4]
        bmask = masks[:, 4:12]

        att = ExitStack()
        W = sb("W", [P, 5, HC, H], where=att)
        Wl = sb("Wl", [P, LAYERS * 5, HC, H], where=att)
        dco = sb("dco", [P, LAYERS * 5, HC, B], where=att)
        qk_t = sb("qk_t", [P, LAYERS * HC, B], where=att)
        vs_t = sb("vs_t", [P, LAYERS * HC, B], where=att)
        setup = ExitStack()
        Wsq = sb("Wsq", [P, LAYERS * 5, HC, H], where=setup)
        dsq = sb("dsq", [P, LAYERS, 5 * HC * B], where=setup)
        dlg = sb("dlg", [P, LAYERS, 5 * HC * B], where=setup)
        dt1 = sb("dt1", [P, LAYERS, 5 * HC * B], where=setup)
        setup.close()
        xs = sb("xs", [P, HC, TOK], where=att)
        xm = sb("xm", [P, HC, TOK], where=att)
        sq = sb("sq", [P, HC, TOK], where=att)
        vare = sb("vare", [P, TOK], where=att)
        lg = sb("lg", [P, TOK], where=att)
        rstd = sb("rstd", [P, TOK], where=att)
        xn = sb("xn", [P, HC, TOK], where=att)
        qs = sb("qs", [P, HC, TOK], where=att)
        kz = sb("kz", [P, HC, 2, TOK], where=att)
        vTd = sb("vTd", [P, HC, GB, 2, S], where=att)
        vsc = sb("vsc", [P, HC, TOK], where=att)
        vbd = sb("vbd", [P, GB, H // 32, 2, HD], where=att)
        mx = sb("mx", [P, 2, 32], where=att)
        sm = sb("sm", [P, 2, 32], where=att)
        rs = sb("rs", [P, 2, 32], where=att)
        ex = sb("ex", [P, 2, 4, 512], where=att)
        pn = sb("pn", [P, 2, 4, 512], where=att)
        pT = sb("pT", [P, 4, 4, P], where=att)
        av = sb("av", [P, HC, TOK], where=att)
        t1 = sb("t1", [P, HC, TOK], where=att)
        t2 = sb("t2", [P, HC, TOK], where=att)
        t3 = sb("t3", [P, HC, TOK], where=att)
        att.close()

        ssm = ExitStack()
        Win = sb("Win", [P, HC, 2 * DI], where=ssm)
        Wc = sb("Wc", [P, DC, 4], where=ssm)
        Ch = sb("Ch", [P, DC, 4], where=ssm)
        Wx = sb("Wx", [P, DC, 96], where=ssm)
        Wdt = sb("Wdt", [N, N], where=ssm)
        dtp = sb("dtp", [N, 2], where=ssm)
        tA = sb("tA", [N, 1], where=ssm)
        A01 = sb("A01", [N, 1], where=ssm)
        Wo = sb("Wo", [P, DC, H], where=ssm)
        Uw = sb("Uw", [P, 2, QW, CH, GB, N], bf16, where=ssm)
        By = sb("By", [P, 2, QW, CH * CH * GB], bf16, where=ssm)
        Wy = sb("Wy", [P, 2, QW, CH * CH * GB], where=ssm)
        W64 = sb("W64", [P, QW, GB], where=ssm)
        Ast = sb("Ast", [P, 2, QW, CH], where=ssm)
        kst = sb("kst", [P, 2, 1], where=ssm)
        k64 = sb("k64", [P, 1], where=ssm)
        kap = sb("kap", [P, PASSES, CHUNKS + 1], where=ssm)

        def tables(n, where):
            return (sb(f"Ub{n}", [P, QW, S, N], bf16, where=where), sb(f"bet{n}", [P, QW, S], bf16, where=where),
                    sb(f"Cc{n}", [P, QW, S + 1], where=where), sb(f"At{n}", [P, QW, S], where=where))

        pass_tables = [tables(0, ssm)]
        front = ExitStack()
        xp = sb("xp", [P, DC, GB, S + 3], where=front)
        acc = sb("acc", [P, DC, TOK], where=front)
        th = sb("th", [P, DC, TOK], where=front)
        zs = sb("zs", [P, DC, TOK], where=front)
        sg = sb("sg", [P, DC, TOK], where=front)
        z = sb("z", [P, DC, TOK], where=front)
        zq = sb("zq", [P, DC, TOK], where=front)
        zve = sb("zve", [P, TOK], where=front)
        zlg = sb("zlg", [P, TOK], where=front)
        zr = sb("zr", [P, TOK], where=front)
        xh = sb("xh", [P, TT, DI], bf16, where=front)
        xr1 = sb("xr1", [P, TT, DI], where=front)
        xmi = sb("xmi", [P, TT, DI], bf16, where=front)
        xlo = sb("xlo", [P, TT, DI], bf16, where=front)
        n2 = sb("n2", [N, TOK], where=front)
        n3 = sb("n3", [N, TOK], where=front)
        n4 = sb("n4", [N, TOK], where=front)
        mn = sb("mn", [N, TOK], where=front)
        dts = sb("dts", [N, TOK], where=front)
        dtt = sb("dtt", [N, TOK], where=front)
        am = sb("am", [N, TOK], where=front)
        am1 = sb("am1", [N, TOK], where=front)
        Bd = sb("Bd", [N, TOK + 1], where=front)
        Cn = sb("Cn", [N, TOK], where=front)
        ccs = sb("ccs", [P, S + 1], where=front)
        acs = sb("acs", [P, S], where=front)
        rT = sb("rT", [P, 2, TT, N], where=front)
        tb = sb("tb", [P, TT, N], where=front)
        tb2 = sb("tb2", [P, TT, N], where=front)
        tc = sb("tc", [P, TT, N], where=front)
        tv = sb("tv", [P, TT, 33], where=front)
        tvr = sb("tvr", [P, TT, 33], where=front)
        tvp = sb("tvp", [P, PARTS, TT, 33], bf16, where=front)
        kp = sb("kp", [P, TT], where=front)
        front.close()
        scan = ExitStack()
        xq = sb("xq", [P, 2, QW, CH, DI], bf16, where=scan)
        pass_tables.append(tables(1, scan))
        q = sb("q", [P, 2, QW, DI], where=scan)
        R = sb("R", [P, QW, DI], where=scan)
        ys = sb("ys", [P, 2, DI], where=scan)
        ye = sb("ye", [P, DI], where=scan)
        scan.close()
        post = ExitStack()
        yt = sb("yt", [P, 2, TT, DI], where=post)
        xnp = sb("xnp", [P, 2, DC, TOK], where=post)
        sgp = sb("sgp", [P, 2, DC, TOK], where=post)
        yf = sb("yf", [P, DC, TOK], where=post)
        yg = sb("yg", [P, DC, TOK], where=post)
        post.close()
        ssm.close()

        (ld, cst, csq_r) = [sem(n) for n in ("loaded", "constants", "condsq_ready")]
        (wsq_r, dco_mm, dco_e, dco_r, tab_r) = [sem(n) for n in
            ("att_wsq", "dcoef_mm", "dcoef_squares", "dcoef_ready", "tables_ready")]
        (xs_r, mean_r, xm_r, sq_r, var_r, rstd_r, xn_r) = [sem(n) for n in
            ("xs_ready", "mean_ready", "xm_ready", "sq_ready", "var_ready", "rstd_ready", "xn_ready")]
        (q_mm, k_mm, v_mm, q_r, k_r, v_r, vs_r) = [sem(n) for n in
            ("q_mm", "k_mm", "v_mm", "q_ready", "k_ready", "v_ready", "vscaled_ready")]
        (vt_mm, vbd_r, sc_mm, max_r, sub_r, exp_r, sum_r, rcp_r, pn_r, pe_r) = [sem(n) for n in
            ("vturn_mm", "vbd_ready", "scores_mm", "max_ready", "sub_ready", "exp_ready", "sum_ready",
             "recip_ready", "probs_late", "probs_early")]
        (pt_mm, pt_r, av_mm, av_r, w_mm, u_mm, t1_r, t2_r, t3_r, x_done) = [sem(n) for n in
            ("pturn_mm", "pturn_ready", "av_mm", "av_ready", "w_mm", "u_mm", "t1_ready", "t2_ready",
             "t3_ready", "att_done")]
        (sw_in, tA_r, A_r, xr_mm, g_mm, xp_r, sgt_r, sg_r, sg_st, acc_r, cv_r, th_r, z_r) = [sem(n) for n in
            ("ssm_weights", "tanhA", "A_ready", "xr_mm", "gate_mm", "xp_ready", "gate_tanh", "gate_ready",
             "gate_stored", "acc_ready", "conv_ready", "tanh_ready", "z_ready")]
        (zm_mm, zc_r, zq_r, zv_mm, zr_r, xg_r, xf_r, xf_st, x2_r, nrm_mm, xw_mm, rt_r) = [sem(n) for n in
            ("zmean_mm", "zc_ready", "zsq_ready", "zvar_mm", "zrstd_ready", "xgain_ready", "xnorm_ready",
             "xnorm_stored", "xnsq_ready", "norm_mm", "xproj_mm", "tok_recip")]
        (mn_r, dts_r, dt2_mm, dtt_r, am_r, C_r, Bd_r, pk_mm, n2_r, pick_s, pick_st) = [sem(n) for n in
            ("minnorm", "dt_copied", "dt2_mm", "dt_tanh", "decay_ready", "C_ready", "Bd_ready", "pick_mm",
             "n2_ready", "pick_ready", "pick_stored")]
        (tok_mm, tv_s, tv_st, xt_mm, xh_r, xr1_r, xmi_r, xlo_r, xq_st) = [sem(n) for n in
            ("tok_mm", "tok_step", "tok_stored", "xturn_mm", "xhi_ready", "xrest_ready", "xmid_ready",
             "xlo_ready", "xparts_stored")]
        dlg_r, dco_g, rg_r, zg_r, ng_r, mm_r = [sem(n) for n in
            ("dcoef_log", "dcoef_guess", "rstd_guess", "zrstd_guess", "norm_guess", "minnorm_ready")]
        zero_st = sem("zero_stored")
        w_in = [sem(f"att_weights{n}") for n in range(LAYERS)]
        w_use = sem("att_weights_in_use")
        cond_in = sem("cond_loaded")
        x_in = [sem("x_first"), sem("x_rest")]
        passed = sem("wait_passed")
        set_r = sem("scan_set")
        pad_r = sem("pads_set")
        one_r = sem("ones_rows_set")
        tab_in = [sem(f"scan_tables{n}") for n in range(PASSES)]
        xq_in = [sem("xq_in0"), sem("xq_in1")]
        pl_st, pe_w, dv_q, ac_r, pe_yq, dv_y = [sem(n) for n in
            ("staged", "w_ready", "q_ready2", "R_ready", "q_used", "y_ready")]
        y_out = [sem("y_out0"), sem("y_out1")]
        ep_w, ep_q, ep_y, ep_r, ep_out, r_init = [sem(n) for n in
            ("end_staged", "end_q", "end_y_mm", "end_y", "end_out", "R_start")]
        po_in = [sem("post_in0"), sem("post_in1")]
        po_mm, yf_r, yg_r, o_mm, po_done = [sem(n) for n in
            ("yturn_mm", "y_sum", "y_gated", "out_mm", "post_done")]
        fin = sem("final")

        turn_bank = (4, 6, 4, 6, 4, 0, 4, 0)
        XQ = PARTS + 1

        block = es.enter_context(nc.Block())

        def alone(eng):
            eng.sem_inc(passed, 1)

        def early_half(m, r):
            return m[:, r, :, :].rearrange("p j (e k) -> p j e k", k=S)[:, :, 0:4, :]

        def late_half(m, r):
            return m[:, r, :, :].rearrange("p j (e k) -> p j e k", k=S)[:, :, 4:8, :]

        def diag_of(m, h, rows):
            v = m[0:rows, h, :, :]
            v = v.rearrange("p g (u r) -> p g u r", r=GB)
            return v[:, :, 0:CH * CH:CH + 1, :]

        @block.sync
        def _(sp):
            sp.dma_start(cond[:, :, :], condT).then_inc(cond_in, 16)
            sp.dma_start(Wl[:, 0:5, :, :], attw[0]).then_inc(w_in[0], 16)
            sp.dma_start(masks[:, :], masks_d).then_inc(ld, 16)
            sp.dma_start(ident[:, :], ident_d).then_inc(ld, 16)
            sp.dma_start(Wl[:, 5:10, :, :], attw[1]).then_inc(w_in[1], 16)
            sp.dma_start(X[:, 0, :, :], xT[:, 0]).then_inc(x_in[0], 16)
            sp.dma_start(X[:, 1:G, :, :], xT[:, 1:G]).then_inc(x_in[1], 16)
            sp.dma_start(sel[:, :, :], sel_d).then_inc(ld, 16)
            sp.dma_start(rowmask[:, :], rowmask_d).then_inc(ld, 16)
            sp.wait_ge(cst, 8)
            for i in range(PARTS):
                sp.dma_start(beta_d[i, 0:1].rearrange("(a o) -> a o", o=1), zero_b[0:1, :]).then_inc(zero_st, 16)
            sp.dma_start(kap_d[0:1].rearrange("(a o) -> a o", o=1), zero_f[0:1, :]).then_inc(zero_st, 16)
            sp.wait_ge(zero_st, 16 * (PARTS + 1))

            sp.wait_ge(x_done, LAYERS * G + 1)

            with sp.Fori(0, LAYERS) as l:
                sp.wait_ge(po_done, l * G + 1)
                for dst, src in ((Win, win), (Wc, wconv), (Ch, chan), (Wo, wout)):
                    sp.dma_start(dst[:, :, :], src[ds(l, 1)].rearrange("a p c o -> p (a c) o")).then_inc(sw_in, 16)
                sp.wait_ge(set_r, 4)
                for k in range(3):
                    sp.dma_start(Wx[:, :, 32 * k:32 * k + N],
                                 wxp[ds(l, 1)].rearrange("a p c o -> p (a c) o")[:, :, k * N:(k + 1) * N]).then_inc(sw_in, 16)
                for dst, src in ((Wdt, wdt), (dtp, dtv)):
                    sp.dma_start(dst[:, :], src[ds(l, 1)].rearrange("a p o -> (a p) o")).then_inc(sw_in, 16)

                def store_gate(n, g):
                    sp.wait_ge(sg_r, n * DC + DC)
                    sp.dma_start(sg_d[ds(g, 1)].rearrange("a p c t -> p (a c) t"), sg[:, :, :]).then_inc(sg_st, 16)

                def store_x(it, g):
                    sp.wait_ge(xf_r, it * DC + DC)
                    sp.dma_start(xn_d[ds(g, 1)].rearrange("a p c t -> p (a c) t"), z[:, :, :]).then_inc(xf_st, 16)

                def store_scan(it, g):
                    sp.wait_ge(pick_s, it * 2 + 2)
                    sp.dma_start(cc_d[ds(g, 1)].rearrange("a p s -> (a p) s"), ccs[:, :]).then_inc(pick_st, 16)
                    sp.dma_start(a_d[ds(g, 1)].rearrange("a p s -> (a p) s"), acs[:, :]).then_inc(pick_st, 16)
                    sp.wait_ge(tv_s, it * 11 + 11)
                    alone(sp)
                    for i in range(PARTS):
                        sp.dma_start(bpart_d[i, ds(g, 1)].rearrange("a (k b) (t n) -> (a b t) k n", k=TT, n=N),
                                     tvp[:, i, :, 0:N]).then_inc(tv_st, 16)
                        sp.dma_start(beta_d[i, ds(g * TOK + 1, TOK)].rearrange("(k p o) -> p k o", p=P, o=1),
                                     tvp[:, i, :, 2 * N:2 * N + 1]).then_inc(tv_st, 16)
                        for b2 in range(2):
                            sp.dma_start(kpart_d[i, ds(g, 1)].rearrange("a t (k b) n -> b (a t) k n", b=2)[b2],
                                         tvp[b2 * S:(b2 + 1) * S, i, :, N:2 * N]).then_inc(tv_st, 16)
                    sp.dma_start(kap_d[ds(g * TOK + 1, TOK)].rearrange("(k p o) -> p k o", p=P, o=1),
                                 kp[:, :].rearrange("p (k o) -> p k o", o=1)).then_inc(tv_st, 16)
                    sp.wait_ge(xh_r, it * TT + TT)
                    sp.wait_ge(xmi_r, it * TT + TT)
                    sp.wait_ge(xlo_r, it * TT + TT)
                    alone(sp)
                    for j, src in enumerate((xh, xmi, xlo)):
                        sp.dma_start(xpart_d[ds(g, 1), j].rearrange("a (k b) (t c) -> (a b t) k c", k=TT, c=DI),
                                     src[:, :, :]).then_inc(xq_st, 16)

                def stored(groups):
                    n = l * G + groups + 1
                    for landed, dmas in ((pick_st, 2), (tv_st, 13), (xq_st, 3)):
                        sp.wait_ge(landed, n * (16 * dmas))
                        alone(sp)

                def load_tables(ps):
                    Ub, bet, Cc, At = pass_tables[ps]
                    for i in range(PARTS):
                        for j in range(PARTS):
                            r0 = (i * PARTS + j) * GB
                            sp.dma_start(Ub[r0:r0 + GB, :, :, :],
                                         bpart_d[i, ps * QW:ps * QW + QW].rearrange("g b (t n) -> b g t n", n=N)).then_inc(tab_in[ps], 16)
                            sp.dma_start(bet[r0:r0 + GB, :, :],
                                         beta_d[i, ps * (QW * TOK):(ps + 1) * (QW * TOK)].rearrange("(g b t) -> b g t", g=QW, t=S)).then_inc(tab_in[ps], 16)
                    sp.dma_start(Cc[:, :, :], cc_d[ps * QW:ps * QW + QW].rearrange("g p s -> p g s")).then_inc(tab_in[ps], 16)
                    sp.dma_start(At[:, :, :], a_d[ps * QW:ps * QW + QW].rearrange("g p s -> p g s")).then_inc(tab_in[ps], 16)
                    for w in range(QW):
                        t0 = (ps * QW + w) * TOK
                        for t in range(CH):
                            sp.dma_start(kap[32 * w + t * GB:32 * w + (t + 1) * GB, ps, 0:CHUNKS],
                                         kap_d[t0:t0 + TOK].rearrange("(b c t) -> t b c", b=GB, t=CH)[t]).then_inc(tab_in[ps], 16)
                        sp.dma_start(kap[32 * w:32 * w + GB, ps, CHUNKS:CHUNKS + 1],
                                     kap_d[t0 + S:t0 + S + TOK].rearrange("(b t) -> b t", t=S)[:, 0:1]).then_inc(tab_in[ps], 16)

                def load(h, ps, ck_of):
                    for i in range(PARTS):
                        r0 = i * (PARTS * GB)
                        sp.dma_start(xq[r0:r0 + PARTS * GB, h, :, :, :].rearrange("p g t c -> p g (t c)"),
                                     xpart_d[ps * QW:ps * QW + QW, :, :, ds(ck_of * (CH * DI), CH * DI)]
                                     .rearrange("g j b f -> (j b) g f")).then_inc(xq_in[h], 16)
                    sp.dma_start(Uw[CROW:CROW + PARTS, h, :, :, :, :].rearrange("p g t b n -> p g (t b n)"),
                                 kpart_d[:, ps * QW:ps * QW + QW, ds(ck_of * CH, CH)].rearrange("i g t b n -> i g (t b n)")).then_inc(xq_in[h], 16)

                def store(h, ps, cn, ck_of):
                    sp.wait_ge(dv_y, cn + 3)
                    for w in range(QW):
                        sp.dma_start(y_d[ps * QW + w, :, ds(ck_of * CH, CH), :].rearrange("b t c -> t b c"),
                                     ys[32 * w:32 * w + 32, h, :]).then_inc(y_out[h], 16)

                store_gate(l * G, 0)
                with sp.Fori(0, QW) as g:
                    store_x(l * G + g, g)
                    store_gate(l * G + g + 1, g + 1)
                    store_scan(l * G + g, g)
                stored(QW)
                load_tables(0)
                with sp.Fori(QW, G - 1) as g:
                    store_x(l * G + g, g)
                    store_gate(l * G + g + 1, g + 1)
                    store_scan(l * G + g, g)
                store_x(l * G + G - 1, G - 1)
                sp.wait_ge(one_r, l + 1)
                load(0, 0, 0)
                load(1, 0, 1)
                store_scan(l * G + G - 1, G - 1)
                stored(G)
                load_tables(1)
                for ps in range(PASSES):
                    c0 = (l * PASSES + ps) * CHUNKS
                    with sp.Fori(0, CHUNKS // 2 - 1) as c2:
                        for h in range(2):
                            cn = c0 + c2 * 2 + h
                            sp.wait_ge(pe_yq, cn * (2 * CH) + 2 * CH + 16)
                            load(h, ps, c2 * 2 + h + 2)
                            store(h, ps, cn, c2 * 2 + h)
                    for h in range(2):
                        cn = c0 + CHUNKS - 2 + h
                        if ps + 1 < PASSES:
                            sp.wait_ge(pe_yq, cn * (2 * CH) + 2 * CH + 16)
                            load(h, ps + 1, h)
                        store(h, ps, cn, CHUNKS - 2 + h)
                    sp.wait_ge(ep_r, (l * PASSES + ps) * QW + QW + 1)
                    alone(sp)
                    for w in range(QW):
                        sp.dma_start(y_d[ps * QW + w, :, S, :], ye[32 * w:32 * w + GB, :]).then_inc(ep_out, 16)

                sp.wait_ge(y_out[0], l * (PASSES * CHUNKS // 2 * QW * 16) + (PASSES * CHUNKS // 2 * QW * 16) + 64)
                sp.wait_ge(y_out[1], l * (PASSES * CHUNKS // 2 * QW * 16) + (PASSES * CHUNKS // 2 * QW * 16) + 64)
                sp.wait_ge(ep_out, l * (PASSES * QW * 16) + PASSES * QW * 16 + 16)
                alone(sp)
                sp.wait_ge(sg_st, l * (16 * G) + 16 * G + 16)
                sp.wait_ge(xf_st, l * (16 * G) + 16 * G + 16)
                alone(sp)

                def load_post(g, u):
                    for b2 in range(2):
                        sp.dma_start(yt[b2 * S:(b2 + 1) * S, u, :, :],
                                     y_d[ds(g, 1), :, 1:S + 1, :].rearrange("a (k b) t c -> b (a t) k c", b=2)[b2]).then_inc(po_in[u], 16)
                    sp.dma_start(xnp[:, u, :, :], xn_d[ds(g, 1)].rearrange("a p c t -> p (a c) t")).then_inc(po_in[u], 16)
                    sp.dma_start(sgp[:, u, :, :], sg_d[ds(g, 1)].rearrange("a p c t -> p (a c) t")).then_inc(po_in[u], 16)

                for u in range(2):
                    load_post(u, u)
                with sp.Fori(0, G // 2 - 1) as g2:
                    for u in range(2):
                        sp.wait_ge(yg_r, (l * G + g2 * 2 + u) * DC + DC)
                        load_post(g2 * 2 + u + 2, u)
            sp.wait_ge(po_done, LAYERS * G + 1)
            sp.dma_start(out, X[:, :, :, :]).then_inc(fin, 16)
            sp.wait_ge(fin, 16)

        @block.gpsimd
        def _(pl):
            pl.memset(ones_h[:, :], 1.0 / H).then_inc(cst, 1)
            pl.memset(ones_d[:, :], 1.0 / DI).then_inc(cst, 1)
            pl.memset(ones_n[:, :], 1.0).then_inc(cst, 1)
            for n, value in enumerate((EPS_IN, 4 * EPS_IN, EPS_DM)):
                pl.memset(eps[:, n:n + 1], value).then_inc(cst, 1)
            pl.memset(zero_f[:, :], 0.0).then_inc(cst, 1)
            pl.memset(zero_b[:, :], 0.0).then_inc(cst, 1)
            pl.sem_inc(pl_st, 1)
            pl.sem_inc(ep_w, 1)
            pl.wait_ge(cst, 8)
            with pl.Fori(0, LAYERS) as l:
                with pl.Fori(0, G) as g:
                    it = l * G + g
                    pl.wait_ge(v_r, it * 2 + 2)
                    pl.wait_ge(tab_r, LAYERS * 2)
                    pl.tensor_tensor(vsc[:, :, :].rearrange("p c (b t) -> p c b t", t=S), vTd[:, :, :, 0, :],
                                     vs_t[:, ds(l * HC, HC), ds(g * GB, GB)].unsqueeze(3).broadcast_to([P, HC, GB, S]),
                                     ALU.mult).then_inc(vs_r, 1)
                    for r in range(2):
                        pl.wait_ge(rcp_r, it * 2 + r + 1)
                        pl.tensor_tensor(late_half(pn, r), late_half(ex, r), rs[:, r, :].rearrange("p (j e) -> p j e", j=4)[:, :, 4:8]
                                         .unsqueeze(3).broadcast_to([P, 4, 4, S]), ALU.mult).then_inc(pn_r, 1)
                    pl.wait_ge(t2_r, it * 2 + 2)
                    pl.tensor_tensor(t3[:, :, :], X[:, ds(g, 1), :, :].rearrange("p a c t -> p (a c) t"), t2[:, :, :],
                                     ALU.add).then_inc(t3_r, 1)

            pl.wait_ge(x_done, LAYERS * G + 1)
            for buf, value in ((Wx[:, :, :], 0.0), (By[:, :, :, :], 0.0), (Wy[:, :, :, :], 0.0), (kap[:, :, :], 0.0)):
                pl.memset(buf, value).then_inc(set_r, 1)
            pl.wait_ge(set_r, 4)
            alone(pl)
            with pl.Fori(0, LAYERS) as l:
                pl.wait_ge(po_done, l * G + 1)
                alone(pl)

                def last_parts(it):
                    pl.wait_ge(xq_st, it * 48 + 48)
                    for k in range(TT):
                        pl.wait_ge(xmi_r, it * TT + k + 1)
                        pl.tensor_tensor(xlo[:, k, :], xr1[:, k, :], xmi[:, k, :], ALU.subtract).then_inc(xlo_r, 1)

                with pl.Fori(0, G - 1) as g:
                    last_parts(l * G + g)
                pl.wait_ge(xlo_r, l * (G * TT) + (G - 1) * TT)
                pl.wait_ge(zc_r, l * (G * DC) + G * DC)
                alone(pl)
                pl.memset(xq[64:96, :, :, :, :], 1.0).then_inc(one_r, 1)
                pl.wait_ge(one_r, l + 1)
                last_parts(l * G + G - 1)

                for ps in range(PASSES):
                    pi = l * PASSES + ps
                    Ub, bet, Cc, At = pass_tables[ps]
                    pl.wait_ge(tab_in[ps], l * (16 * TABLES) + 16 * TABLES)
                    alone(pl)
                    with pl.Fori(0, CHUNKS // 2) as c2:
                        for h in range(2):
                            cn = pi * CHUNKS + c2 * 2 + h
                            s0 = c2 * (2 * CH) + h * CH
                            pl.wait_ge(pe_yq, cn * (2 * CH) + 2 * CH)
                            pl.wait_ge(dv_y, cn + 1)
                            pl.wait_ge(ac_r, cn * (4 * CH) + 4)
                            for w in range(QW):
                                pl.tensor_tensor(Uw[0:XROWS, h, w, :, :, :],
                                                 Ub[0:XROWS, w, ds(s0, CH), :].unsqueeze(2).broadcast_to([XROWS, CH, GB, N]),
                                                 rowmask[0:XROWS, :].unsqueeze(1).unsqueeze(3).broadcast_to([XROWS, CH, GB, N]),
                                                 ALU.mult).then_inc(pl_st, 1)
                            pl.tensor_tensor(diag_of(By, h, XROWS), bet[0:XROWS, :, ds(s0, CH)].unsqueeze(3).broadcast_to([XROWS, QW, CH, GB]),
                                             rowmask[0:XROWS, :].unsqueeze(1).unsqueeze(1).broadcast_to([XROWS, QW, CH, GB]),
                                             ALU.mult).then_inc(pl_st, 1)
                            pl.tensor_tensor(diag_of(Wy, h, P), Cc[:, :, ds(s0, CH)].unsqueeze(3).broadcast_to([P, QW, CH, GB]),
                                             bmask.unsqueeze(1).unsqueeze(1).broadcast_to([P, QW, CH, GB]),
                                             ALU.mult).then_inc(pl_st, 1)
                            pl.tensor_copy(Ast[:, h, :, :], At[:, :, ds(s0, CH)]).then_inc(pl_st, 1)
                            pl.tensor_copy(kst[:, h, :], kap[:, ps, ds(c2 * 2 + h, 1)]).then_inc(pl_st, 1)
                    pl.wait_ge(ep_y, pi + 1)
                    pl.wait_ge(ep_r, pi * QW + 1)
                    alone(pl)
                    pl.tensor_tensor(W64[:, :, :], Cc[:, :, S:S + 1].broadcast_to([P, QW, GB]),
                                     bmask.unsqueeze(1).broadcast_to([P, QW, GB]), ALU.mult).then_inc(ep_w, 1)
                    pl.tensor_copy(k64[:, :], kap[:, ps, CHUNKS:CHUNKS + 1]).then_inc(ep_w, 1)

        @block.scalar
        def _(act):
            act.wait_ge(cond_in, 16)
            act.wait_ge(cst, 8)
            act.activation(condsq[:, :, :], cond[:, :, :], ACT.Square).then_inc(csq_r, 1)
            for l in range(LAYERS):
                act.wait_ge(w_in[l], 16)
                act.activation(Wsq[:, l * 5:l * 5 + 5, :, :], Wl[:, l * 5:l * 5 + 5, :, :], ACT.Square).then_inc(wsq_r, 1)
            act.wait_ge(dco_e, LAYERS * 2)
            act.activation(dlg[:, :, :], dsq[:, :, :], ACT.Ln, bias=eps[:, 2:3]).then_inc(dlg_r, 1)
            act.wait_ge(dlg_r, 1)
            act.activation(dco[:, :, :, :].rearrange("p w c b -> p (w c b)"), dlg[:, :, :].rearrange("p l f -> p (l f)"), ACT.Exp,
                           scale=-0.5).then_inc(dco_g, 1)
            act.wait_ge(ld, 16 * 4)
            act.wait_ge(tab_r, LAYERS * 2)
            with act.Fori(0, LAYERS) as l:

                def squares(n):
                    act.wait_ge(xm_r, n + 1)
                    act.activation(sq[:, :, :], xm[:, :, :], ACT.Square).then_inc(sq_r, 1)

                def deviation(n):
                    act.wait_ge(var_r, n + 1)
                    act.activation(lg[:, :], PS[:, 7, :], ACT.Ln, bias=eps[:, 0:1]).then_inc(rg_r, 1)
                    act.wait_ge(rg_r, n * 2 + 1)
                    act.activation(rstd[:, :], lg[:, :], ACT.Exp, scale=-0.5).then_inc(rg_r, 1)

                def keys(n):
                    for c in range(HC):
                        act.wait_ge(k_mm, n * 2 + c + 1)
                        for e in range(2):
                            act.activation(kz[:, c, e, :], PS[:, 6 + c, :], ACT.Copy, scale=par[e]).then_inc(k_r, 1)

                def values(n):
                    for c in range(HC):
                        act.wait_ge(v_mm, n * 2 + c + 1)
                        act.activation(vTd[:, c, :, :, :],
                                       PS[:, 6 + c, :].rearrange("p (b t) -> p b t", t=S).unsqueeze(2).broadcast_to([P, GB, 2, S]),
                                       ACT.Copy).then_inc(v_r, 1)

                def turned(it, r):
                    for k in range(4 * r, 4 * r + 4):
                        act.wait_ge(pt_mm, it * 8 + k + 1)
                        if k >= 4:
                            act.wait_ge(av_mm, it * 8 + k - 3)
                        act.activation(pT[:, k % 4, :, :].rearrange("p j q -> p (j q)"), PS[:, turn_bank[k], :], ACT.Copy).then_inc(pt_r, 1)

                def body(it, ahead):
                    def by_parity(b2):
                        act.wait_ge(vt_mm, it * 4 + b2 + 1)
                        for e in range(2):
                            act.activation(vbd[:, 2 * b2:2 * b2 + 2, :, e, :].rearrange("p b h d -> p (b h) d"),
                                           PS[:, 4 + b2 % 2, :].rearrange("p (m e d) -> p m e d", e=2, d=HD)[:, :, e, :],
                                           ACT.Copy, scale=masks[:, 2 + e:3 + e]).then_inc(vbd_r, 1)

                    by_parity(0)
                    by_parity(1)
                    act.wait_ge(sub_r, it * 2 + 1)
                    act.activation(ex[:, 0, :, :], ex[:, 0, :, :], ACT.Exp).then_inc(exp_r, 1)
                    by_parity(2)
                    by_parity(3)
                    if ahead:
                        squares(it + 1)
                        deviation(it + 1)
                    turned(it, 0)
                    act.wait_ge(sub_r, it * 2 + 2)
                    act.activation(ex[:, 1, :, :], ex[:, 1, :, :], ACT.Exp).then_inc(exp_r, 1)
                    if ahead:
                        keys(it + 1)
                    turned(it, 1)
                    if ahead:
                        values(it + 1)

                squares(l * G)
                deviation(l * G)
                keys(l * G)
                values(l * G)
                with act.Fori(0, G - 1) as g:
                    body(l * G + g, True)
                body(l * G + G - 1, False)

            act.wait_ge(x_done, LAYERS * G + 1)
            act.sem_inc(y_out[0], 64)
            act.sem_inc(y_out[1], 64)
            act.sem_inc(ep_out, 16)
            act.sem_inc(sg_st, 16)
            act.sem_inc(xf_st, 16)
            act.sem_inc(pick_st, 32)
            act.sem_inc(tv_st, 13 * 16)
            act.sem_inc(xq_st, 48)
            with act.Fori(0, LAYERS) as l:
                act.wait_ge(sw_in, l * (16 * SSM_LOADS) + 16 * SSM_LOADS)
                act.wait_ge(po_done, l * G + 1)
                alone(act)
                act.activation(tA[:, :], dtp[:, 1:2], ACT.Tanh).then_inc(tA_r, 1)

                def tap(n):
                    for m in range(DC):
                        act.wait_ge(xp_r, n * DC + m + 1)
                        act.activation(acc[:, m, :].rearrange("p (b t) -> p b t", t=S), xp[:, m, :, 3:3 + S], ACT.Identity,
                                       scale=Wc[:, m, 3:4], bias=Ch[:, m, 0:1]).then_inc(acc_r, 1)

                def gate_tanh(n):
                    for m in range(DC):
                        act.wait_ge(g_mm, n * DC + m + 1)
                        act.wait_ge(z_r, n * DC + m + 1)
                        act.activation(th[:, m, :], PS[:, m, :], ACT.Tanh, scale=0.5).then_inc(sgt_r, 1)

                def conv_tanh(n):
                    for m in range(DC):
                        act.wait_ge(cv_r, n * (3 * DC) + 2 * DC + m + 1)
                        act.activation(th[:, m, :], acc[:, m, :], ACT.Tanh, scale=0.5).then_inc(th_r, 1)

                def squares(n):
                    for m in range(DC):
                        act.wait_ge(zc_r, n * DC + m + 1)
                        act.activation(zq[:, m, :], z[:, m, :], ACT.Square).then_inc(zq_r, 1)

                def body(it, ahead):
                    if ahead:
                        tap(it + 1)
                    act.wait_ge(zv_mm, it + 1)
                    act.activation(zlg[:, :], PS[:, 5, :], ACT.Ln, bias=eps[:, 1:2]).then_inc(zg_r, 1)
                    act.wait_ge(zg_r, it * 2 + 1)
                    act.activation(zr[:, :], zlg[:, :], ACT.Exp, scale=-0.5).then_inc(zg_r, 1)
                    for m in range(DC):
                        act.wait_ge(xg_r, it * DC + m + 1)
                        act.activation(z[:, m, :], z[:, m, :], ACT.Identity, bias=Ch[:, m, 2:3]).then_inc(xf_r, 1)
                    for m in range(DC):
                        act.wait_ge(xf_r, it * DC + m + 1)
                        act.activation(zq[:, m, :], z[:, m, :], ACT.Square).then_inc(x2_r, 1)
                    if ahead:
                        conv_tanh(it + 1)
                        gate_tanh(it + 1)
                    act.wait_ge(xw_mm, it + 1)
                    act.activation(dts[:, :], PS[64:64 + N, 6, :], ACT.Copy).then_inc(dts_r, 1)
                    act.activation(Cn[:, :], PS[32:32 + N, 6, :], ACT.Copy).then_inc(C_r, 1)
                    act.wait_ge(dt2_mm, it + 1)
                    act.activation(dtt[:, :], PS[0:N, 4, :], ACT.Tanh, bias=dtp[:, 0:1]).then_inc(dtt_r, 1)
                    act.wait_ge(n2_r, it + 1)
                    act.activation(n4[:, :], n2[:, :], ACT.Ln).then_inc(ng_r, 1)
                    act.wait_ge(ng_r, it * 2 + 1)
                    act.activation(mn[:, :], n4[:, :], ACT.Exp, scale=-0.5).then_inc(ng_r, 1)
                    act.wait_ge(pick_st, it * 32 + 32)
                    act.wait_ge(pk_mm, it * 2 + 1)
                    act.activation(ccs[:, 1:S + 1], PS[:, 5, 0:S], ACT.Copy, scale=-1.0).then_inc(pick_s, 1)
                    act.wait_ge(xq_st, it * 48 + 48)
                    for k in range(TT):
                        act.wait_ge(xt_mm, it * TT + k + 1)
                        act.activation(xh[:, k, :], PS[:, k, :], ACT.Copy).then_inc(xh_r, 1)
                    act.wait_ge(pk_mm, it * 2 + 2)
                    act.activation(acs[:, :], PS[:, 6, 0:S], ACT.Copy).then_inc(pick_s, 1)
                    for k in range(TT):
                        act.wait_ge(xr1_r, it * TT + k + 1 + TT)
                        act.activation(xmi[:, k, :], xr1[:, k, :], ACT.Copy).then_inc(xmi_r, 1)
                    if ahead:
                        squares(it + 1)

                tap(l * G)
                conv_tanh(l * G)
                gate_tanh(l * G)
                squares(l * G)
                with act.Fori(0, G - 1) as g:
                    body(l * G + g, True)
                body(l * G + G - 1, False)

                with act.Fori(0, PASSES) as ps:
                    pi = l * PASSES + ps
                    with act.Fori(0, CHUNKS // 2) as c2:
                        for h in range(2):
                            cn = pi * CHUNKS + c2 * 2 + h
                            act.wait_ge(pl_st, cn * 8 + 8 + 1)
                            for t in range(CH):
                                for w in range(QW):
                                    if w % 2 == 0:
                                        act.wait_ge(dv_q, cn * (2 * CH) + 2 * t + w // 2 + 1 + 2)
                                    act.activation(R[:, w, :], q[:, t % 2, w, :], ACT.Relu,
                                                   scale=Ast[:, h, w, t:t + 1]).then_inc(ac_r, 1)

        @block.tensor
        def _(pe):
            def project(bank, w, rhs, done, free=None):
                for m in range(HC):
                    if free:
                        free(m)
                    for c in range(HC):
                        mm = pe.matmul(PS[:, bank + m, :], W[:, w, c, m * P:(m + 1) * P], rhs[:, c, :],
                                       start=(c == 0), stop=(c == HC - 1))
                    mm.then_inc(done, 1)

            pe.wait_ge(cst, 8)
            pe.wait_ge(csq_r, 1)
            for l in range(LAYERS):
                pe.wait_ge(wsq_r, l + 1)
                for w in range(5):
                    st = 0 if w < 3 else HC
                    for m in range(HC):
                        for c in range(HC):
                            mm = pe.matmul(PS[:, 2 * l + w // 4, (w % 4) * P + m * B:(w % 4) * P + (m + 1) * B],
                                           Wsq[:, l * 5 + w, c, m * P:(m + 1) * P], condsq[:, st + c, :],
                                           start=(c == 0), stop=(c == HC - 1))
                mm.then_inc(dco_mm, 1)
            pe.wait_ge(dco_e, LAYERS * 2)
            pe.wait_ge(ld, 16 * 4)
            alone(pe)
            with pe.Fori(0, LAYERS) as l:

                def mean(n):
                    pe.wait_ge(xs_r, n + 1)
                    for c in range(HC):
                        mm = pe.matmul(PS[:, 6, :], ones_h[:, :], xs[:, c, :], start=(c == 0), stop=(c == HC - 1))
                    mm.then_inc(mean_r, 1)

                def variance(n):
                    pe.wait_ge(sq_r, n + 1)
                    for c in range(HC):
                        mm = pe.matmul(PS[:, 7, :], ones_h[:, :], sq[:, c, :], start=(c == 0), stop=(c == HC - 1))
                    mm.then_inc(var_r, 1)

                def keys_queries(n):
                    pe.wait_ge(xn_r, n + 1)
                    project(6, 1, xn, k_mm)
                    project(6, 0, xn, q_mm, lambda m: pe.wait_ge(k_r, n * 4 + 2 * m + 2))

                def values(n):
                    project(6, 2, xn, v_mm, lambda m: pe.wait_ge(q_r, n * 2 + m + 1))

                def scores(it, r):
                    for j in range(4):
                        for b in range(4):
                            for c in range(HC):
                                bb = 4 * r + b
                                col = ((b // 2) * HC + c) * P
                                mm = pe.matmul(PS[(b % 2) * S:(b % 2 + 1) * S, j, col:col + P],
                                               qs[32 * j:32 * j + 32, c, bb * S:(bb + 1) * S],
                                               kz[32 * j:32 * j + 32, c, :, bb * S:(bb + 1) * S],
                                               start=True, stop=True)
                    mm.then_inc(sc_mm, 1)

                def turn_values(it, b2s):
                    for b2 in b2s:
                        if b2 >= 2:
                            pe.wait_ge(vbd_r, it * 8 + 2 * b2 - 2)
                        for bb in (2 * b2, 2 * b2 + 1):
                            for c in range(HC):
                                col = (bb % 2) * H + c * P
                                mm = pe.transpose(PS[:, 4 + b2 % 2, col:col + P],
                                                  vTd[:, c, bb, :, :].rearrange("p a t -> p (a t)"), ident[:, :])
                        mm.then_inc(vt_mm, 1)

                def turn(it, k):
                    if k % 4 >= 2:
                        pe.wait_ge(pt_r, it * 8 + k - 1)
                    for j in range(4):
                        mm = pe.transpose(PS[:, turn_bank[k], j * P:(j + 1) * P],
                                          pn[:, k // 4, j, (k % 4) * P:(k % 4 + 1) * P], ident[:, :])
                    mm.then_inc(pt_mm, 1)

                def weigh(it, k):
                    pe.wait_ge(pt_r, it * 8 + k + 1)
                    for b in range(2):
                        for j in range(4):
                            bb, h4 = 4 * (k // 4) + 2 * (k // 2 % 2) + b, (k % 2) * 4 + j
                            col = (k % 2) * (4 * S) + (2 * (k // 2 % 2) + b) * S
                            mm = pe.matmul(PS[32 * j:32 * j + 32, 5, col:col + S],
                                           vbd[:, bb, h4, :, :].rearrange("p a d -> p (a d)"),
                                           pT[:, k % 4, j, b * S:(b + 1) * S], start=True, stop=True)
                    mm.then_inc(av_mm, 1)

                def attend(it, r):
                    pe.wait_ge(pe_r, it * 2 + r + 1)
                    if r == 0:
                        pe.wait_ge(vbd_r, it * 8 + 8)
                    else:
                        pe.wait_ge(sub_r, it * 2 + 2)
                        pe.wait_ge(av_r, it * 2 + 1)
                    k0 = 4 * r
                    turn(it, k0)
                    turn(it, k0 + 1)
                    for k in range(k0 + 2, k0 + 4):
                        weigh(it, k - 2)
                        if k == k0 + 2:
                            pe.wait_ge(pn_r, it * 2 + r + 1)
                        turn(it, k)
                    weigh(it, k0 + 2)
                    weigh(it, k0 + 3)

                def body(it, ahead):
                    pe.wait_ge(t1_r, it * 2 + 2)
                    pe.wait_ge(q_r, it * 2 + 2)
                    scores(it, 0)
                    pe.wait_ge(v_r, it * 2 + 2)
                    turn_values(it, (0, 1))
                    if ahead:
                        mean(it + 1)
                    turn_values(it, (2, 3))
                    pe.wait_ge(sub_r, it * 2 + 1)
                    scores(it, 1)
                    if ahead:
                        variance(it + 1)
                    attend(it, 0)
                    if ahead:
                        keys_queries(it + 1)
                    attend(it, 1)
                    pe.wait_ge(vs_r, it + 1)
                    project(2, 4, vsc, u_mm)
                    pe.wait_ge(av_r, it * 2 + 2)
                    project(0, 3, av, w_mm)
                    if ahead:
                        values(it + 1)

                mean(l * G)
                variance(l * G)
                pe.wait_ge(w_use, l + 1)
                keys_queries(l * G)
                values(l * G)
                with pe.Fori(0, G - 1) as g:
                    body(l * G + g, True)
                body(l * G + G - 1, False)

            pe.wait_ge(x_done, LAYERS * G + 1)
            pe.sem_inc(pe_yq, 16)
            pe.sem_inc(ep_y, 1)
            with pe.Fori(0, LAYERS) as l:
                pe.wait_ge(sw_in, l * (16 * SSM_LOADS) + 16 * SSM_LOADS)
                pe.wait_ge(po_done, l * G + 1)
                alone(pe)

                def into(n, g, m, done):
                    for c in range(HC):
                        mm = pe.matmul(PS[:, m % DC, :], Win[:, c, m * P:(m + 1) * P],
                                       X[:, ds(g, 1), c, :].rearrange("p a t -> p (a t)"), start=(c == 0), stop=(c == HC - 1))
                    mm.then_inc(done, 1)

                def gates(n, g):
                    for m in range(DC):
                        pe.wait_ge(xp_r, n * DC + m + 1)
                        into(n, g, DC + m, g_mm)

                def mean(n):
                    for m in range(DC):
                        pe.wait_ge(z_r, n * DC + m + 1)
                        mm = pe.matmul(PS[:, 4, :], ones_d[:, :], zs[:, m, :], start=(m == 0), stop=(m == DC - 1))
                    mm.then_inc(zm_mm, 1)

                def body(it, g, ahead):
                    if ahead:
                        for m in range(DC):
                            pe.wait_ge(sg_r, it * DC + m + 1)
                            pe.wait_ge(xr1_r, it * TT + m + 1)
                            into(it + 1, g + 1, m, xr_mm)
                    for m in range(DC):
                        pe.wait_ge(zq_r, it * DC + m + 1)
                        mm = pe.matmul(PS[:, 5, :], ones_d[:, :], zq[:, m, :], start=(m == 0), stop=(m == DC - 1))
                    mm.then_inc(zv_mm, 1)
                    if ahead:
                        gates(it + 1, g + 1)
                    for m in range(DC):
                        pe.wait_ge(xf_r, it * DC + m + 1)
                        mm = pe.matmul(PS[0:96, 6, :], Wx[:, m, :], z[:, m, :], start=(m == 0), stop=(m == DC - 1))
                    mm.then_inc(xw_mm, 1)
                    for m in range(DC):
                        pe.wait_ge(x2_r, it * DC + m + 1)
                        mm = pe.matmul(PS[0:N, 7, :], ones_n[:, :], zq[:, m, :], start=(m == 0), stop=(m == DC - 1))
                    mm.then_inc(nrm_mm, 1)
                    pe.wait_ge(dts_r, it + 1)
                    alone(pe)
                    pe.matmul(PS[0:N, 4, :], Wdt[:, :], dts[:, :], start=True, stop=True).then_inc(dt2_mm, 1)

                    def pick(src, bank):
                        for b in range(GB):
                            mm = pe.matmul(PS[:, bank, 0:S], sel[:, b, :], src[:, b * S:(b + 1) * S],
                                           start=(b == 0), stop=(b == GB - 1))
                        mm.then_inc(pk_mm, 1)

                    pe.wait_ge(C_r, it + 1)
                    pick(Cn, 5)
                    for k in range(TT):
                        pe.wait_ge(sg_r, (it + (1 if ahead else 0)) * DC + k + 1)
                        for m in range(DC):
                            mm = pe.transpose(PS[:, k, m * P:(m + 1) * P], z[:, m, k * P:(k + 1) * P], ident[:, :])
                        mm.then_inc(xt_mm, 1)
                    if ahead:
                        pe.wait_ge(dtt_r, it + 1)
                        mean(it + 1)
                    pe.wait_ge(Bd_r, it + 1)
                    pe.wait_ge(am_r, it * 2 + 2)
                    pick(am, 6)
                    for i, (src, off) in enumerate(((Bd, 0), (am, 0), (Bd, 1), (am1, 0), (Cn, 0))):
                        for k in range(TT):
                            c0 = (i * TT + k) * N
                            mm = pe.transpose(PS[:, 7, c0:c0 + N], src[:, k * P + off:(k + 1) * P + off], ident[0:N, 0:N])
                    mm.then_inc(tok_mm, 1)

                for m in range(DC):
                    into(l * G, 0, m, xr_mm)
                gates(l * G, 0)
                mean(l * G)
                with pe.Fori(0, G - 1) as g:
                    body(l * G + g, g, True)
                body(l * G + G - 1, G - 1, False)

                pe.wait_ge(xr1_r, l * (G * TT) + G * TT + TT)
                pe.wait_ge(pick_s, l * (2 * G) + 2 * G)
                pe.wait_ge(tv_s, l * (11 * G) + 11 * G)
                alone(pe)
                with pe.Fori(0, PASSES) as ps:
                    pi = l * PASSES + ps

                    def inputs(cn, c2, h, t):
                        if t == 0:
                            pe.wait_ge(xq_in[h], (pi * (CHUNKS // 2) + c2) * (XQ * 16) + XQ * 16)
                            pe.wait_ge(pl_st, cn * 8 + 8 + 1)
                        for p in range(2):
                            pe.wait_ge(dv_q, cn * (2 * CH) + 2 * t + p + 1)
                            for w in (2 * p, 2 * p + 1):
                                mm = pe.matmul(PS[:, w, :], Uw[0:KROWS, h, w, t, :, :].rearrange("p b n -> p (b n)"),
                                               xq[0:KROWS, h, w, t, :], start=True, stop=True)
                            mm.then_inc(pe_w, 1)

                    def y_of(cn, h, t):
                        if t == 0:
                            pe.wait_ge(dv_y, cn + 1)
                        for p in range(2):
                            pe.wait_ge(dv_q, cn * (2 * CH) + 2 * t + p + 1 + 2)
                            for w in (2 * p, 2 * p + 1):
                                pe.matmul(PS[32 * w:32 * w + 32, 4 + h, :], Wy[:, h, w, t * 32:(t + 1) * 32],
                                          q[:, t % 2, w, :], start=(t == 0), stop=False, skip_group_check=True)
                            for w in (2 * p, 2 * p + 1):
                                mm = pe.matmul(PS[32 * w:32 * w + 32, 4 + h, :], By[0:XROWS, h, w, t * 32:(t + 1) * 32],
                                               xq[0:XROWS, h, w, t, :], start=False, stop=(t == CH - 1), skip_group_check=True)
                            mm.then_inc(pe_yq, 1)

                    def chunk(c2, h, ahead):
                        cn = pi * CHUNKS + c2 * 2 + h
                        for t in range(1, CH):
                            inputs(cn, c2, h, t)
                            y_of(cn, h, t - 1)
                        if ahead:
                            inputs(cn + 1, c2 + h, 1 - h, 0)
                        y_of(cn, h, CH - 1)

                    inputs(pi * CHUNKS, 0, 0, 0)
                    with pe.Fori(0, CHUNKS // 2 - 1) as c2:
                        for h in range(2):
                            chunk(c2, h, True)
                    chunk(CHUNKS // 2 - 1, 0, True)
                    chunk(CHUNKS // 2 - 1, 1, False)
                    pe.wait_ge(ep_q, pi + 1)
                    pe.wait_ge(ep_w, pi * 2 + 3)
                    for w in range(QW):
                        mm = pe.matmul(PS[32 * w:32 * w + GB, 6, :], W64[:, w, :], q[:, 0, w, :], start=True, stop=True)
                    mm.then_inc(ep_y, 1)

                pe.wait_ge(ep_r, l * (PASSES * QW) + PASSES * QW + 1)
                pe.wait_ge(dv_y, l * (PASSES * CHUNKS) + PASSES * CHUNKS + 2)
                alone(pe)
                with pe.Fori(0, G // 2) as g2:
                    for u in range(2):
                        it = l * G + g2 * 2 + u
                        pe.wait_ge(po_in[u], (l * (G // 2) + g2) * 64 + 64)
                        pe.wait_ge(po_done, it + 1)
                        for m in range(DC):
                            for k in range(TT):
                                mm = pe.transpose(PS[:, m, k * P:(k + 1) * P], yt[:, u, k, m * P:(m + 1) * P], ident[:, :])
                            mm.then_inc(po_mm, 1)
                        for m in range(HC):
                            for c in range(DC):
                                if m == 0:
                                    pe.wait_ge(yg_r, it * DC + c + 1)
                                mm = pe.matmul(PS[:, 4 + 2 * u + m, :], Wo[:, c, m * P:(m + 1) * P], yg[:, c, :],
                                               start=(c == 0), stop=(c == DC - 1))
                            mm.then_inc(o_mm, 1)

        @block.vector
        def _(v):
            def tiled(ap):
                return ap.rearrange("p (b t) -> p b t", t=S)

            def by_batch(tab, c, g):
                return tab[:, c, ds(g * GB, GB)].unsqueeze(2).broadcast_to([P, GB, S])

            def of_layer(tab, n, g):
                return tab[:, ds(n, 1), ds(g * GB, GB)].rearrange("p a b -> p (a b)").unsqueeze(2).broadcast_to([P, GB, S])

            def root(y, x, e, y0, tmp, done, n):
                v.scalar_tensor_tensor(out=tmp, in0=x, scalar=e, in1=y0, op0=ALU.add, op1=ALU.mult).then_inc(done, 1)
                v.wait_ge(done, n + 1)
                v.scalar_tensor_tensor(out=tmp, in0=tmp, scalar=-0.5, in1=y0, op0=ALU.mult, op1=ALU.mult).then_inc(done, 1)
                v.wait_ge(done, n + 2)
                v.scalar_tensor_tensor(out=y, in0=tmp, scalar=1.5, in1=y0, op0=ALU.add, op1=ALU.mult).then_inc(done, 1)
                v.wait_ge(done, n + 3)

            v.wait_ge(cond_in, 16)
            v.sem_inc(x_done, 1)
            v.sem_inc(t1_r, 2)
            for l in range(LAYERS):
                v.wait_ge(dco_mm, l + 1)
                v.tensor_copy(dsq[:, l, 0:512], PS[:, 2 * l, :]).then_inc(dco_e, 1)
                v.tensor_copy(dsq[:, l, 512:5 * P], PS[:, 2 * l + 1, 0:P]).then_inc(dco_e, 1)
            v.wait_ge(dco_e, LAYERS * 2)
            v.wait_ge(dco_g, 1)
            dcv = dco[:, :, :, :].rearrange("p w c b -> p (w c b)")
            root(dcv, dsq[:, :, :].rearrange("p l f -> p (l f)"), EPS_DM, dcv, dt1[:, :, :].rearrange("p l f -> p (l f)"), dco_r, 0)
            for l in range(LAYERS):
                v.scalar_tensor_tensor(out=qk_t[:, l * HC:l * HC + HC, :], in0=dco[:, l * 5, :, :], scalar=float(HD) ** -0.5,
                                       in1=dco[:, l * 5 + 1, :, :], op0=ALU.mult, op1=ALU.mult).then_inc(tab_r, 1)
                v.tensor_tensor(vs_t[:, l * HC:l * HC + HC, :], dco[:, l * 5 + 2, :, :], cond[:, HC:2 * HC, :], ALU.mult).then_inc(tab_r, 1)
            v.wait_ge(tab_r, LAYERS * 2)
            for n in range(2):
                v.wait_ge(x_in[n], 16)
            v.wait_ge(ld, 16 * 4)
            alone(v)
            with v.Fori(0, LAYERS) as l:
                v.wait_ge(x_done, l * G + 1)
                alone(v)

                def styled(n, g):
                    v.tensor_tensor(xs[:, :, :].rearrange("p c (b t) -> p c b t", t=S),
                                    X[:, ds(g, 1), :, :].rearrange("p a c (b t) -> p (a c) b t", t=S),
                                    cond[:, 0:HC, ds(g * GB, GB)].unsqueeze(3).broadcast_to([P, HC, GB, S]),
                                    ALU.mult).then_inc(xs_r, 1)

                def centred(n):
                    v.wait_ge(mean_r, n + 1)
                    v.tensor_tensor(xm[:, :, :], xs[:, :, :], PS[:, 6:7, :].broadcast_to([P, HC, TOK]),
                                    ALU.subtract).then_inc(xm_r, 1)

                def normed(n):
                    v.wait_ge(var_r, n + 1)
                    v.wait_ge(rg_r, n * 2 + 2)
                    root(rstd[:, :], PS[:, 7, :], EPS_IN, rstd[:, :], vare[:, :], rstd_r, n * 3)
                    v.tensor_tensor(xn[:, :, :], xm[:, :, :], rstd[:, :].unsqueeze(1).broadcast_to([P, HC, TOK]),
                                    ALU.mult).then_inc(xn_r, 1)

                def queries(n, g):
                    for c in range(HC):
                        v.wait_ge(q_mm, n * 2 + c + 1)
                        v.tensor_tensor(tiled(qs[:, c, :]), tiled(PS[:, 6 + c, :]), of_layer(qk_t, l * HC + c, g),
                                        ALU.mult).then_inc(q_r, 1)

                def scores(it, r):
                    sc = PS[:, 0:4, :].rearrange("p j (e k) -> p (j e) k", k=S)
                    v.wait_ge(sc_mm, it * 2 + r + 1)
                    v.tensor_reduce(mx[:, r, :], sc, AX.X, ALU.max).then_inc(max_r, 1)
                    v.wait_ge(max_r, it * 2 + r + 1)
                    v.tensor_tensor(ex[:, r, :, :].rearrange("p j (e k) -> p (j e) k", k=S), sc,
                                    mx[:, r, :].unsqueeze(2).broadcast_to([P, 32, S]), ALU.subtract).then_inc(sub_r, 1)

                def sums(it, r):
                    v.wait_ge(exp_r, it * 2 + r + 1)
                    v.tensor_reduce(sm[:, r, :], ex[:, r, :, :].rearrange("p j (e k) -> p (j e) k", k=S),
                                    AX.X, ALU.add).then_inc(sum_r, 1)
                    v.wait_ge(sum_r, it * 2 + r + 1)
                    v.reciprocal(rs[:, r, :], sm[:, r, :]).then_inc(rcp_r, 1)
                    v.wait_ge(rcp_r, it * 2 + r + 1)
                    v.tensor_tensor(early_half(pn, r), early_half(ex, r), rs[:, r, :].rearrange("p (j e) -> p j e", j=4)[:, :, 0:4]
                                    .unsqueeze(3).broadcast_to([P, 4, 4, S]), ALU.mult).then_inc(pe_r, 1)

                def out_of(it, g, r):
                    v.wait_ge(av_mm, it * 8 + 4 * r + 4)
                    v.tensor_tensor(av[:, :, r * 4 * S:(r + 1) * 4 * S].rearrange("p c (b t) -> p c b t", t=S),
                                    PS[:, 5, :].rearrange("p (c b t) -> p c b t", c=HC, t=S),
                                    vs_t[:, ds(l * HC, HC), ds(g * GB + 4 * r, 4)].unsqueeze(3).broadcast_to([P, HC, 4, S]),
                                    ALU.mult).then_inc(av_r, 1)

                def body(it, g, ahead):
                    if ahead:
                        styled(it + 1, g + 1)
                    scores(it, 0)
                    if ahead:
                        centred(it + 1)
                    sums(it, 0)
                    scores(it, 1)
                    if ahead:
                        normed(it + 1)
                    sums(it, 1)
                    out_of(it, g, 0)
                    if ahead:
                        queries(it + 1, g + 1)
                    out_of(it, g, 1)
                    for c in range(HC):
                        v.wait_ge(u_mm, it * 2 + c + 1)
                        v.tensor_tensor(tiled(t2[:, c, :]), tiled(PS[:, 2 + c, :]), of_layer(dco[:, :, :, :].rearrange("p w c b -> p (w c) b"), l * (5 * HC) + 4 * HC + c, g),
                                        ALU.mult).then_inc(t2_r, 1)
                    for c in range(HC):
                        v.wait_ge(w_mm, it * 2 + c + 1)
                        v.tensor_tensor(tiled(t1[:, c, :]), tiled(PS[:, c, :]), of_layer(dco[:, :, :, :].rearrange("p w c b -> p (w c) b"), l * (5 * HC) + 3 * HC + c, g),
                                        ALU.mult).then_inc(t1_r, 1)
                    v.wait_ge(t1_r, it * 2 + 4)
                    v.wait_ge(t3_r, it + 1)
                    v.tensor_tensor(X[:, ds(g, 1), :, :].rearrange("p a c t -> p (a c t)"), t3[:, :, :].rearrange("p c t -> p (c t)"),
                                    t1[:, :, :].rearrange("p c t -> p (c t)"), ALU.add).then_inc(x_done, 1)

                styled(l * G, 0)
                v.tensor_copy(W[:, :, :, :], Wl[:, ds(l * 5, 5), :, :]).then_inc(w_use, 1)
                centred(l * G)
                normed(l * G)
                queries(l * G, 0)
                with v.Fori(0, G - 1) as g:
                    body(l * G + g, g, True)
                body(l * G + G - 1, G - 1, False)

            v.wait_ge(x_done, LAYERS * G + 1)
            v.sem_inc(po_done, 1)
            v.sem_inc(xr1_r, TT)
            v.sem_inc(dv_q, 2)
            v.sem_inc(ac_r, 20)
            v.sem_inc(dv_y, 2)
            v.sem_inc(ep_r, 1)
            with v.Fori(0, LAYERS) as l:
                v.wait_ge(po_done, l * G + 1)
                v.wait_ge(tA_r, l + 1)
                v.tensor_scalar(A01[:, :], tA[:, :], -0.01, None, ALU.mult).then_inc(A_r, 1)
                v.memset(xp[:, :, :, 0:3], 0.0).then_inc(A_r, 1)
                v.memset(ccs[:, 0:1], 0.0).then_inc(A_r, 1)
                v.memset(am1[:, :], 1.0).then_inc(A_r, 1)
                v.memset(Bd[:, TOK:TOK + 1], 0.0).then_inc(A_r, 1)
                v.wait_ge(A_r, l * 5 + 5)
                alone(v)

                def embed(n, g):
                    for m in range(DC):
                        v.wait_ge(xr_mm, n * DC + m + 1)
                        v.tensor_tensor(xp[:, m, :, 3:3 + S], tiled(PS[:, m, :]), by_batch(cond, m, g), ALU.add).then_inc(xp_r, 1)

                def conv(n, taps):
                    for j in taps:
                        for m in range(DC):
                            if j == 0:
                                v.wait_ge(acc_r, n * DC + m + 1)
                            else:
                                v.wait_ge(cv_r, n * (3 * DC) + (j - 1) * DC + m + 1)
                            v.scalar_tensor_tensor(out=tiled(acc[:, m, :]), in0=xp[:, m, :, j:j + S], scalar=Wc[:, m, j:j + 1],
                                                   in1=tiled(acc[:, m, :]), op0=ALU.mult, op1=ALU.add).then_inc(cv_r, 1)

                def silu(n):
                    for m in range(DC):
                        v.wait_ge(th_r, n * DC + m + 1)
                        v.scalar_tensor_tensor(out=zs[:, m, :], in0=th[:, m, :], scalar=1.0, in1=acc[:, m, :],
                                               op0=ALU.add, op1=ALU.mult).then_inc(z_r, 1)

                def gate(n):
                    v.wait_ge(sg_st, n * 16 + 16)
                    for m in range(DC):
                        v.wait_ge(sgt_r, n * DC + m + 1)
                        v.scalar_tensor_tensor(out=sg[:, m, :], in0=th[:, m, :], scalar=1.0, in1=PS[:, m, :],
                                               op0=ALU.add, op1=ALU.mult).then_inc(sg_r, 1)

                def centred(n):
                    v.wait_ge(xf_st, n * 16 + 16)
                    v.wait_ge(zm_mm, n + 1)
                    for m in range(DC):
                        v.tensor_tensor(z[:, m, :], zs[:, m, :], PS[:, 4, :], ALU.subtract).then_inc(zc_r, 1)

                def body(it, g, ahead):
                    if ahead:
                        embed(it + 1, g + 1)
                        conv(it + 1, (0, 1))
                    v.wait_ge(zv_mm, it + 1)
                    v.wait_ge(zg_r, it * 2 + 2)
                    root(zr[:, :], PS[:, 5, :], 4 * EPS_IN, zr[:, :], zve[:, :], zr_r, it * 3)
                    for m in range(DC):
                        v.scalar_tensor_tensor(out=z[:, m, :], in0=z[:, m, :], scalar=Ch[:, m, 1:2], in1=zr[:, :],
                                               op0=ALU.mult, op1=ALU.mult).then_inc(xg_r, 1)
                    if ahead:
                        conv(it + 1, (2,))
                        silu(it + 1)
                        gate(it + 1)
                    v.wait_ge(nrm_mm, it + 1)
                    v.tensor_scalar(n2[:, :], PS[0:N, 7, :], 1.0, LEAST, ALU.min, ALU.max).then_inc(n2_r, 1)
                    v.wait_ge(dtt_r, it + 1)
                    v.tensor_scalar(am[:, :], dtt[:, :], A01[:, 0:1], 1.0, ALU.mult, ALU.add).then_inc(am_r, 1)
                    v.tensor_scalar(tiled(am1[:, :])[:, :, 0:S - 1], tiled(dtt[:, :])[:, :, 1:S], A01[:, 0:1], 1.0,
                                    ALU.mult, ALU.add).then_inc(am_r, 1)
                    v.wait_ge(n2_r, it + 1)
                    v.wait_ge(ng_r, it * 2 + 2)
                    root(mn[:, :], n2[:, :], 0.0, mn[:, :], n3[:, :], mn_r, it * 3)
                    v.tensor_tensor(mn[:, :], mn[:, :], n2[:, :], ALU.mult).then_inc(mm_r, 1)
                    v.wait_ge(mm_r, it + 1)
                    v.tensor_tensor(Bd[:, 0:TOK], PS[0:N, 6, :], mn[:, :], ALU.mult).then_inc(Bd_r, 1)
                    for k in range(TT):
                        v.wait_ge(xh_r, it * TT + k + 1)
                        v.tensor_tensor(xr1[:, k, :], PS[:, k, :], xh[:, k, :], ALU.subtract).then_inc(xr1_r, 1)
                    if ahead:
                        centred(it + 1)
                    v.wait_ge(tv_st, it * (13 * 16) + 13 * 16)
                    v.wait_ge(tok_mm, it + 1)
                    rows = PS[:, 7, 0:5 * TT * N].rearrange("p (i k n) -> p i k n", i=5, n=N)
                    v.reciprocal(rT[:, :, :, :], rows[:, 1:4:2, :, :]).then_inc(rt_r, 1)
                    v.wait_ge(rt_r, it + 1)
                    v.tensor_tensor(tv[:, :, 0:N], rows[:, 0, :, :], rT[:, 0, :, :], ALU.mult).then_inc(tv_s, 1)
                    v.tensor_scalar(tv[:, :, N:2 * N], rT[:, 0, :, :], -CLIP, CLIP, ALU.mult, ALU.add).then_inc(tv_s, 1)
                    v.tensor_tensor(tb[:, :, :], rows[:, 2, :, :], rT[:, 1, :, :], ALU.mult).then_inc(tv_s, 1)
                    v.scalar_tensor_tensor(out=tc[:, :, :], in0=rT[:, 1, :, :], scalar=CLIP, in1=rows[:, 4, :, :],
                                           op0=ALU.mult, op1=ALU.mult).then_inc(tv_s, 1)
                    v.wait_ge(tv_s, it * 11 + 3)
                    v.scalar_tensor_tensor(out=tb2[:, :, :], in0=tb[:, :, :], scalar=-1.0, in1=rows[:, 4, :, :],
                                           op0=ALU.mult, op1=ALU.mult).then_inc(tv_s, 1)
                    v.wait_ge(tv_s, it * 11 + 4)
                    v.tensor_reduce(kp[:, :], tc[:, :, :], AX.X, ALU.add).then_inc(tv_s, 1)
                    v.wait_ge(tv_s, it * 11 + 5)
                    v.tensor_reduce(tv[:, :, 2 * N], tb2[:, :, :], AX.X, ALU.add).then_inc(tv_s, 1)
                    v.wait_ge(tv_s, it * 11 + 7)
                    v.tensor_copy(tvp[:, 0, :, :], tv[:, :, :]).then_inc(tv_s, 1)
                    v.wait_ge(tv_s, it * 11 + 8)
                    v.tensor_tensor(tvr[:, :, :], tv[:, :, :], tvp[:, 0, :, :], ALU.subtract).then_inc(tv_s, 1)
                    v.wait_ge(tv_s, it * 11 + 9)
                    v.tensor_copy(tvp[:, 1, :, :], tvr[:, :, :]).then_inc(tv_s, 1)
                    v.wait_ge(tv_s, it * 11 + 10)
                    v.tensor_tensor(tvp[:, 2, :, :], tvr[:, :, :], tvp[:, 1, :, :], ALU.subtract).then_inc(tv_s, 1)

                embed(l * G, 0)
                conv(l * G, range(3))
                silu(l * G)
                gate(l * G)
                centred(l * G)
                with v.Fori(0, G - 1) as g:
                    body(l * G + g, g, True)
                body(l * G + G - 1, G - 1, False)

                v.wait_ge(xf_st, l * (16 * G) + 16 * G + 16)
                v.wait_ge(sg_st, l * (16 * G) + 16 * G + 16)
                v.wait_ge(pick_st, l * (32 * G) + 32 * G + 32)
                v.wait_ge(tv_st, l * (13 * 16 * G) + 13 * 16 * G + 13 * 16)
                v.wait_ge(xq_st, l * (48 * G) + 48 * G + 48)
                alone(v)
                with v.Fori(0, PASSES) as ps:
                    pi = l * PASSES + ps
                    v.wait_ge(ep_y, pi + 1)
                    v.memset(R[:, :, :], CLIP).then_inc(r_init, 1)
                    v.wait_ge(r_init, pi + 1)
                    alone(v)

                    def step(cn, t):
                        for p in range(2):
                            n = 2 * t + p
                            v.wait_ge(pe_w, cn * (2 * CH) + n + 1)
                            v.wait_ge(ac_r, cn * (4 * CH) + 4 * t + 2 * p + 18)
                            v.wait_ge(pe_yq, cn * (2 * CH) + n + 13)
                            v.scalar_tensor_tensor(out=q[:, t % 2, 2 * p:2 * p + 2, :].rearrange("p w c -> p (w c)"),
                                                   in0=R[:, 2 * p:2 * p + 2, :].rearrange("p w c -> p (w c)"), scalar=2 * CLIP,
                                                   in1=PS[:, 2 * p:2 * p + 2, :].rearrange("p w c -> p (w c)"),
                                                   op0=ALU.min, op1=ALU.subtract).then_inc(dv_q, 1)

                    def chunk(c2, h, ahead):
                        cn = pi * CHUNKS + c2 * 2 + h
                        for t in range(1, CH):
                            step(cn, t)
                        if ahead:
                            step(cn + 1, 0)
                        v.wait_ge(pe_yq, cn * (2 * CH) + 2 * CH + 16)
                        v.wait_ge(pl_st, cn * 8 + 9)
                        v.wait_ge(y_out[h], (pi * (CHUNKS // 2) + c2) * 64 + 64)
                        v.tensor_scalar(ys[:, h, :], PS[:, 4 + h, :], kst[:, h, :], None, ALU.add).then_inc(dv_y, 1)

                    step(pi * CHUNKS, 0)
                    with v.Fori(0, CHUNKS // 2 - 1) as c2:
                        for h in range(2):
                            chunk(c2, h, True)
                    chunk(CHUNKS // 2 - 1, 0, True)
                    chunk(CHUNKS // 2 - 1, 1, False)
                    v.wait_ge(ac_r, pi * (4 * S) + 4 * S + 20)
                    v.tensor_scalar(q[:, 0, :, :], R[:, :, :], 2 * CLIP, None, ALU.min).then_inc(ep_q, 1)
                    v.wait_ge(ep_y, pi + 2)
                    v.wait_ge(ep_out, pi * 64 + 16)
                    v.wait_ge(ep_w, pi * 2 + 3)
                    for w in range(QW):
                        v.tensor_scalar(ye[32 * w:32 * w + GB, :], PS[32 * w:32 * w + GB, 6, :],
                                        k64[32 * w:32 * w + GB, :], None, ALU.add).then_inc(ep_r, 1)

                with v.Fori(0, G // 2) as g2:
                    for u in range(2):
                        g = g2 * 2 + u
                        it = l * G + g
                        v.wait_ge(po_in[u], (l * (G // 2) + g2) * 64 + 64)
                        for m in range(DC):
                            v.wait_ge(po_mm, it * DC + m + 1)
                            v.scalar_tensor_tensor(out=yf[:, m, :], in0=xnp[:, u, m, :], scalar=Ch[:, m, 3:4], in1=PS[:, m, :],
                                                   op0=ALU.mult, op1=ALU.add).then_inc(yf_r, 1)
                            v.wait_ge(yf_r, it * DC + m + 1)
                            v.tensor_tensor(yg[:, m, :], yf[:, m, :], sgp[:, u, m, :], ALU.mult).then_inc(yg_r, 1)
                        v.wait_ge(o_mm, it * HC + HC)
                        xg = X[:, ds(g, 1), :, :].rearrange("p a c t -> p (a c t)")
                        v.scalar_tensor_tensor(out=xg, in0=PS[:, 4 + 2 * u:6 + 2 * u, :].rearrange("p c t -> p (c t)"), scalar=0.5,
                                               in1=xg, op0=ALU.mult, op1=ALU.add).then_inc(po_done, 1)


def kernel(**inputs):
    import concourse.bacc as bacc
    from concourse.bass_utils import run_bass_kernel_spmd

    a = {k: np.asarray(v) for k, v in inputs.items()}

    def cols(w):
        return w.T.reshape(-1, P, w.shape[0]).transpose(1, 0, 2)

    def chan(v):
        return v.reshape(-1, P, v.shape[-1]).transpose(1, 0, 2)

    def two(name, fn):
        return np.stack([fn(a[f"L{n}_cond_{name}"]) for n in (2, 3)])

    arrays = {
        "xT": a["x"].reshape(G, TOK, HC, P).transpose(3, 0, 2, 1),
        "condT": a["cond_2048"].reshape(B, DC, P).transpose(2, 1, 0),
        "attw": np.stack([np.stack([cols(a[f"L{n}_cond_{w}_weight"]) for w in "qkvwu"], axis=1) for n in (0, 1)]),
        "win": two("W_in", cols),
        "wconv": two("W_conv", lambda w: chan(w[:, 0, :])),
        "chan": np.stack([chan(np.stack([a[f"L{n}_cond_{v}"] for v in ("b_conv", "ln_g", "ln_b", "D")], axis=1)) for n in (2, 3)]),
        "wxp": two("W_xproj", cols),
        "wdt": two("W_dt", lambda w: w.T),
        "dtv": np.stack([np.stack([a[f"L{n}_cond_{v}"] for v in ("b_dt", "A_log")], axis=1) for n in (2, 3)]),
        "wout": two("W_out", cols),
    }
    p = np.arange(P)
    arrays["ident"] = np.eye(P, dtype=np.float32)
    arrays["sel"] = (p == np.arange(GB)[:, None] * N + np.arange(N)[:, None, None]).astype(np.float32)
    arrays["masks"] = np.concatenate([(p[:, None] // HD % 2 == np.arange(2)), (p[:, None] // S == np.arange(2)),
                                      (p[:, None] // N == np.arange(GB))], axis=1).astype(np.float32)
    rowmask = ((p[:, None] % GB == np.arange(GB)) & (p[:, None] < XROWS)).astype(np.float32)

    nc = bacc.Bacc("TRN2", target_bir_lowering=False, num_devices=1)
    bf = mybir.dt.np(mybir.dt.bfloat16)
    arrays["rowmask"] = rowmask.astype(bf)
    feed, args = {}, []
    for name in ("xT", "condT", "attw", "win", "wconv", "chan", "wxp", "wdt", "dtv", "wout", "ident", "sel", "masks", "rowmask"):
        arr = np.ascontiguousarray(arrays[name])
        feed[f"in_{name}"] = arr
        args.append(nc.dram_tensor(f"in_{name}", arr.shape, mybir.dt.from_np(arr.dtype), kind="ExternalInput").ap())
    args.append(nc.dram_tensor("out_x", (P, G, HC, TOK), mybir.dt.float32, kind="ExternalOutput").ap())
    cond_resid_kernel(nc, *args)
    r = run_bass_kernel_spmd(nc, [feed], core_ids=[0])
    return np.ascontiguousarray(r.results[0]["out_x"].transpose(1, 3, 2, 0).reshape(B, S, H))
```

```python
import numpy as np
import concourse.bass as bass
from concourse import mybir
from contextlib import ExitStack

B, S, H, DI, N = 64, 64, 256, 512, 16
HEADS = 16
HD = H // HEADS
P = 128
GB = P // N
G = B // GB
TOK = GB * S
HC, DC = H // P, DI // P
TT = TOK // P
LAYERS = 2
QW = 4
PASSES = G // QW
CH = 4
CHUNKS = S // CH
PARTS = 3
XROWS = PARTS * PARTS * GB
CROW = XROWS
KROWS = CROW + PARTS
STRIP = (2 * CH - 1) * GB
MID = (CH - 1) * GB
NB = N + 1
CLIP = 10.0
EPS_IN, EPS_DM = 1e-5, 1e-8
TABLES = PARTS * PARTS + 3
SSM_LOADS = 6
LN_EXP_SET = 6
LEAST = 1e-18


def cond_resid_kernel(nc, xT, condT, attw, win, wconv, chan, wxp, wdt, dtv, wout, dskip,
                      ident_d, sel_d, masks_d, rowmask_d, out):
    f32, bf16 = mybir.dt.float32, mybir.dt.bfloat16
    ALU, ACT, AX = mybir.AluOpType, mybir.ActivationFunctionType, mybir.AxisListType
    ds = bass.ds

    def scratch(name, shape, dt):
        return nc.dram_tensor(name, shape, dt, kind="Internal").ap()

    xn_d = scratch("xn_d", (G, P, DC, TOK), f32)
    sg_d = scratch("sg_d", (G, P, DC, TOK), f32)
    xpart_d = scratch("xpart_d", (G, PARTS, GB, S * DI), bf16)
    bpart_d = scratch("bpart_d", (PARTS, (B * S + 1) * NB), bf16)
    kpart_d = scratch("kpart_d", (PARTS, G, S, GB, N), bf16)
    kap_d = scratch("kap_d", (PASSES, PARTS, S + 1, QW, GB), bf16)
    cc_d = scratch("cc_d", (G, P, S + 1), f32)
    a_d = scratch("a_d", (G, P, S), f32)
    y_d = scratch("y_d", (G, GB, S + 1, DI), f32)

    es = ExitStack()
    with es:
        es.enter_context(nc.allow_non_contiguous_dma(reason="a few short columns for each group"))

        def sem(name):
            return es.enter_context(nc.semaphore(name))

        def sb(name, shape, dt=f32, where=None):
            return (where or es).enter_context(nc.sbuf_tensor(name, shape, dt))

        PS = es.enter_context(nc.psum_tensor("PS", [P, 8, 512], f32))

        X = sb("X", [P, G, HC, TOK])
        cond = sb("cond", [P, DC, B])
        condsq = sb("condsq", [P, DC, B])
        ident = sb("ident", [P, P])
        sel = sb("sel", [N, GB, P])
        masks = sb("masks", [P, 12])
        rowmask = sb("rowmask", [P, GB], bf16)
        ones_h = sb("ones_h", [P, P])
        ones_d = sb("ones_d", [P, P])
        ones_n = sb("ones_n", [P, N])
        zero_b = sb("zero_b", [P, QW * GB], bf16)
        one_b = sb("one_b", [P, DI], bf16)
        eps = sb("eps", [P, 3])
        par = [masks[:, 0:1], masks[:, 1:2]]
        half = masks[:, 2:4]
        bmask = masks[:, 4:12]

        att = ExitStack()
        Wl = sb("Wl", [P, LAYERS * 5, HC, H], where=att)
        W = sb("W", [P, 5, HC, H], where=att)
        dco = sb("dco", [P, LAYERS * 5, HC, B], where=att)
        qk_t = sb("qk_t", [P, LAYERS * HC, B], where=att)
        vs_t = sb("vs_t", [P, LAYERS * HC, B], where=att)
        dsq = sb("dsq", [P, LAYERS, 5 * HC * B], where=att)
        setup = ExitStack()
        Wsq = sb("Wsq", [P, LAYERS * 5, HC, H], where=setup)
        dlg = sb("dlg", [P, LAYERS, 5 * HC * B], where=setup)
        setup.close()
        xs = sb("xs", [P, HC, TOK], where=att)
        xm = sb("xm", [P, HC, TOK], where=att)
        sq = sb("sq", [P, HC, TOK], where=att)
        vare = sb("vare", [P, TOK], where=att)
        rstd = sb("rstd", [P, TOK], where=att)
        xn = sb("xn", [P, HC, TOK], where=att)
        qs = sb("qs", [P, HC, TOK], where=att)
        kz = sb("kz", [P, HC, 2, TOK], where=att)
        vTd = sb("vTd", [P, HC, GB, 2, S], where=att)
        vsc = sb("vsc", [P, HC, TOK], where=att)
        vbd = sb("vbd", [P, GB, H // 32, 2, HD], where=att)
        mx = sb("mx", [P, 2, 32], where=att)
        sm = sb("sm", [P, 2, 32], where=att)
        rs = sb("rs", [P, 2, 32], where=att)
        ex = sb("ex", [P, 2, 4, 512], where=att)
        pn = sb("pn", [P, 2, 4, 512], where=att)
        pT = sb("pT", [P, 4, 4, P], where=att)
        av = sb("av", [P, HC, TOK], where=att)
        t1 = sb("t1", [P, HC, TOK], where=att)
        t2 = sb("t2", [P, HC, TOK], where=att)
        t3 = sb("t3", [P, HC, TOK], where=att)
        att.close()

        ssm = ExitStack()
        Win = sb("Win", [P, HC, 2 * DI], where=ssm)
        Wc = sb("Wc", [P, DC, 4], where=ssm)
        Ch = sb("Ch", [P, DC, 3], where=ssm)
        Wx = sb("Wx", [P, DC, 96], where=ssm)
        Wdt = sb("Wdt", [N, N], where=ssm)
        dtp = sb("dtp", [N, 2], where=ssm)
        tA = sb("tA", [N, 1], where=ssm)
        A01 = sb("A01", [N, 1], where=ssm)
        Wo = sb("Wo", [P, DC, H], where=ssm)
        Dsk = sb("Dsk", [P, DC, 1], where=ssm)
        Uw = sb("Uw", [P, 2, QW, CH, GB, N], bf16, where=ssm)
        By = sb("By", [P, 2, CH, QW, STRIP], bf16, where=ssm)
        Wy = sb("Wy", [P, 2, QW, CH * CH * GB], where=ssm)
        W64 = sb("W64", [P, QW, 32], where=ssm)
        Ast = sb("Ast", [P, 2, QW, CH], where=ssm)
        Bk = sb("Bk", [P, PASSES, QW, 32], bf16, where=ssm)

        def tables(n, where):
            return (sb(f"Ub{n}", [P, QW, S, NB], bf16, where=where), sb(f"Cc{n}", [P, QW, S + 1], where=where),
                    sb(f"At{n}", [P, QW, S], where=where))

        pass_tables = [tables(0, ssm)]
        front = ExitStack()
        xp = sb("xp", [P, DC, GB, S + 3], where=front)
        acc = sb("acc", [P, DC, TOK], where=front)
        th = sb("th", [P, DC, TOK], where=front)
        zs = sb("zs", [P, DC, TOK], where=front)
        sg = sb("sg", [P, DC, TOK], where=front)
        z = sb("z", [P, DC, TOK], where=front)
        zq = sb("zq", [P, DC, TOK], where=front)
        zve = sb("zve", [P, TOK], where=front)
        zlg = sb("zlg", [P, TOK], where=front)
        zr = sb("zr", [P, TOK], where=front)
        xh = sb("xh", [P, TT, DI], bf16, where=front)
        xr1 = sb("xr1", [P, TT, DI], where=front)
        xmi = sb("xmi", [P, TT, DI], bf16, where=front)
        xlo = sb("xlo", [P, TT, DI], bf16, where=front)
        n2 = sb("n2", [N, TOK], where=front)
        n3 = sb("n3", [N, TOK], where=front)
        n4 = sb("n4", [N, TOK], where=front)
        mn = sb("mn", [N, TOK], where=front)
        dts = sb("dts", [N, TOK], where=front)
        dtt = sb("dtt", [N, TOK], where=front)
        am = sb("am", [N, TOK], where=front)
        am1 = sb("am1", [N, TOK], where=front)
        Bd = sb("Bd", [N, TOK + 1], where=front)
        Cn = sb("Cn", [N, TOK], where=front)
        ccs = sb("ccs", [P, S + 1], where=front)
        acs = sb("acs", [P, S], where=front)
        rT = sb("rT", [P, 2, TT, N], where=front)
        tb = sb("tb", [P, TT, N], where=front)
        tb2 = sb("tb2", [P, TT, N], where=front)
        tc = sb("tc", [P, TT, N], where=front)
        tv = sb("tv", [P, TT, 34], where=front)
        tvr = sb("tvr", [P, TT, 34], where=front)
        tvp = sb("tvp", [P, PARTS, TT, 34], bf16, where=front)
        front.close()
        scan = ExitStack()
        xq = sb("xq", [P, 2, QW, CH, DI], bf16, where=scan)
        q = sb("q", [P, 2, QW, DI], where=scan)
        R = sb("R", [P, QW, DI], where=scan)
        ys = sb("ys", [P, 2, DI], where=scan)
        ye = sb("ye", [P, DI], where=scan)
        pass_tables.append(tables(1, scan))
        xnp = sb("xnp", [P, 2, DC, TOK], where=scan)
        sgp = sb("sgp", [P, 2, DC, TOK], where=scan)
        scan.close()
        post = ExitStack()
        yt = sb("yt", [P, 2, TT, DI], where=post)
        yf = sb("yf", [P, DC, TOK], where=post)
        yg = sb("yg", [P, 2, DC, TOK], where=post)
        post.close()
        ssm.close()

        (ld, cst, csq_r) = [sem(n) for n in ("loaded", "constants", "condsq_ready")]
        (wsq_r, dco_mm, dco_e, dco_r, tab_r) = [sem(n) for n in
            ("att_wsq", "dcoef_mm", "dcoef_squares", "dcoef_ready", "tables_ready")]
        (xs_r, mean_r, xm_r, sq_r, var_r, rstd_r, xn_r) = [sem(n) for n in
            ("xs_ready", "mean_ready", "xm_ready", "sq_ready", "var_ready", "rstd_ready", "xn_ready")]
        (q_mm, k_mm, v_mm, q_r, k_r, v_r, vs_r) = [sem(n) for n in
            ("q_mm", "k_mm", "v_mm", "q_ready", "k_ready", "v_ready", "vscaled_ready")]
        (vt_mm, vbd_r, sc_mm, max_r, sub_r, exp_r, sum_r, rcp_r, pn_r, pe_r) = [sem(n) for n in
            ("vturn_mm", "vbd_ready", "scores_mm", "max_ready", "sub_ready", "exp_ready", "sum_ready",
             "recip_ready", "probs_late", "probs_early")]
        (pt_mm, pt_r, av_mm, av_r, w_mm, u_mm, t1_r, t2_r, t3_r, x_done) = [sem(n) for n in
            ("pturn_mm", "pturn_ready", "av_mm", "av_ready", "w_mm", "u_mm", "t1_ready", "t2_ready",
             "t3_ready", "att_done")]
        (sw_in, tA_r, A_r, xr_mm, g_mm, xp_r, sgt_r, sg_r, sg_st, acc_r, cv_r, th_r, z_r) = [sem(n) for n in
            ("ssm_weights", "tanhA", "A_ready", "xr_mm", "gate_mm", "xp_ready", "gate_tanh", "gate_ready",
             "gate_stored", "acc_ready", "conv_ready", "tanh_ready", "z_ready")]
        (zm_mm, zc_r, zq_r, zv_mm, zr_r, xg_r, xf_r, xf_st, x2_r, nrm_mm, xw_mm, rt_r) = [sem(n) for n in
            ("zmean_mm", "zc_ready", "zsq_ready", "zvar_mm", "zrstd_ready", "xgain_ready", "xnorm_ready",
             "xnorm_stored", "xnsq_ready", "norm_mm", "xproj_mm", "tok_recip")]
        (mn_r, dts_r, dt2_mm, dtt_r, am_r, C_r, Bd_r, pk_mm, n2_r, pick_s, pick_st) = [sem(n) for n in
            ("minnorm", "dt_copied", "dt2_mm", "dt_tanh", "decay_ready", "C_ready", "Bd_ready", "pick_mm",
             "n2_ready", "pick_ready", "pick_stored")]
        (tok_mm, tv_s, tv_st, xt_mm, xh_r, xr1_r, xmi_r, xlo_r, xq_st) = [sem(n) for n in
            ("tok_mm", "tok_step", "tok_stored", "xturn_mm", "xhi_ready", "xrest_ready", "xmid_ready",
             "xlo_ready", "xparts_stored")]
        dlg_r, dco_g, rg_r, zg_r, ng_r, mm_r = [sem(n) for n in
            ("dcoef_log", "dcoef_guess", "rstd_guess", "zrstd_guess", "norm_guess", "minnorm_ready")]
        zero_st = sem("zero_stored")
        w_in = [sem(f"att_weights{n}") for n in range(LAYERS)]
        w_use = sem("att_weights_in_use")
        so_in = sem("ssm_out_weights")
        cond_in = sem("cond_loaded")
        x_in = [sem("x_first"), sem("x_rest")]
        passed = sem("wait_passed")
        set_r = sem("scan_set")
        one_r = sem("ones_rows_set")
        tab_in = [sem(f"scan_tables{n}") for n in range(PASSES)]
        xq_in = [sem("xq_in0"), sem("xq_in1")]
        pl_st, pe_w, dv_q, ac_r, pe_yq, dv_y = [sem(n) for n in
            ("staged", "w_ready", "q_ready2", "R_ready", "q_used", "y_ready")]
        y_out = [sem("y_out0"), sem("y_out1")]
        ep_w, ep_q, ep_y, ep_r, ep_out, r_init = [sem(n) for n in
            ("end_staged", "end_q", "end_y_mm", "end_y", "end_out", "R_start")]
        po_in = [sem("post_in0"), sem("post_in1")]
        po_mm, yf_r, yg_r, o_mm, po_done = [sem(n) for n in
            ("yturn_mm", "y_sum", "y_gated", "out_mm", "post_done")]
        fin = sem("final")

        turn_bank = (4, 6, 4, 6, 4, 0, 4, 0)
        STAGED = QW + 3
        Y_STORES = PASSES * CHUNKS // 2 * QW * 16
        TV_STORES = 6 * PARTS
        XQ = PARTS + 2

        block = es.enter_context(nc.Block())

        def alone(eng):
            eng.sem_inc(passed, 1)

        def early_half(m, r):
            return m[:, r, :, :].rearrange("p j (e k) -> p j e k", k=S)[:, :, 0:4, :]

        def late_half(m, r):
            return m[:, r, :, :].rearrange("p j (e k) -> p j e k", k=S)[:, :, 4:8, :]

        def diag_of(m, h):
            v = m[:, h, :, :].rearrange("p g (u r) -> p g u r", r=GB)
            return v[:, :, 0:CH * CH:CH + 1, :]

        @block.sync
        def _(sp):
            sp.dma_start(cond[:, :, :], condT).then_inc(cond_in, 16)
            sp.dma_start(Wl[:, 0:5, :, :], attw[0]).then_inc(w_in[0], 16)
            sp.dma_start(masks[:, :], masks_d).then_inc(ld, 16)
            sp.dma_start(ident[:, :], ident_d).then_inc(ld, 16)
            sp.dma_start(Wl[:, 5:10, :, :], attw[1]).then_inc(w_in[1], 16)
            sp.dma_start(X[:, 0, :, :], xT[:, 0]).then_inc(x_in[0], 16)
            sp.dma_start(X[:, 1:G, :, :], xT[:, 1:G]).then_inc(x_in[1], 16)
            sp.dma_start(sel[:, :, :], sel_d).then_inc(ld, 16)
            sp.dma_start(rowmask[:, :], rowmask_d).then_inc(ld, 16)
            sp.wait_ge(cst, 8)
            for i in range(PARTS):
                sp.dma_start(bpart_d[i, N:NB].rearrange("(a o) -> a o", o=1), zero_b[0:1, 0:1]).then_inc(zero_st, 16)
            sp.dma_start(kap_d[:, :, 0].rearrange("s i g b -> (s i) (g b)"), zero_b[0:PASSES * PARTS, :]).then_inc(zero_st, 16)
            sp.wait_ge(zero_st, 16 * (PARTS + 1))

            sp.wait_ge(w_use, LAYERS)
            def load_front(n):
                for dst, src in ((Win, win), (Wc, wconv), (Ch, chan), (Wx, wxp)):
                    sp.dma_start(dst[:, :, :], src[ds(n, 1)].rearrange("a p c o -> p (a c) o")).then_inc(sw_in, 16)
                for dst, src in ((Wdt, wdt), (dtp, dtv)):
                    sp.dma_start(dst[:, :], src[ds(n, 1)].rearrange("a p o -> (a p) o")).then_inc(sw_in, 16)

            load_front(0)
            sp.wait_ge(x_done, LAYERS * G + 1)
            sp.wait_ge(set_r, 4)
            with sp.Fori(0, LAYERS) as l:
                sp.wait_ge(po_done, l * G + 1)
                for dst, src in ((Wo, wout), (Dsk, dskip)):
                    sp.dma_start(dst[:, :, :], src[ds(l, 1)].rearrange("a p c o -> p (a c) o")).then_inc(so_in, 16)

                def store_gate(n, g):
                    sp.wait_ge(sg_r, n * DC + DC)
                    sp.dma_start(sg_d[ds(g, 1)].rearrange("a p c t -> p (a c) t"), sg[:, :, :]).then_inc(sg_st, 16)

                def store_x(it, g):
                    sp.wait_ge(xf_r, it * DC + DC)
                    sp.dma_start(xn_d[ds(g, 1)].rearrange("a p c t -> p (a c) t"), z[:, :, :]).then_inc(xf_st, 16)

                def store_scan(it, g, ps):
                    sp.wait_ge(pick_s, it * 2 + 2)
                    sp.dma_start(cc_d[ds(g, 1)].rearrange("a p s -> (a p) s"), ccs[:, :]).then_inc(pick_st, 16)
                    sp.dma_start(a_d[ds(g, 1)].rearrange("a p s -> (a p) s"), acs[:, :]).then_inc(pick_st, 16)
                    sp.wait_ge(tv_s, it * 11 + 11)
                    alone(sp)
                    for i in range(PARTS):
                        sp.dma_start(bpart_d[i, ds(g * (TOK * NB), TOK * NB)].rearrange("(k p n) -> p k n", p=P, n=NB)[:, :, 0:N],
                                     tvp[:, i, :, 0:N]).then_inc(tv_st, 16)
                        sp.dma_start(bpart_d[i, ds(g * (TOK * NB) + NB, TOK * NB)].rearrange("(k p n) -> p k n", p=P, n=NB)[:, :, N:NB],
                                     tvp[:, i, :, 2 * N:2 * N + 1]).then_inc(tv_st, 16)
                        for b2 in range(2):
                            rows = slice(b2 * S, (b2 + 1) * S)
                            sp.dma_start(kpart_d[i, ds(g, 1)].rearrange("a t (k b) n -> b (a t) k n", b=2)[b2],
                                         tvp[rows, i, :, N:2 * N]).then_inc(tv_st, 16)
                            sp.dma_start(kap_d[ps, i, 1:S + 1, ds(g - ps * QW, 1)].rearrange("t a (k b o) -> b (a t) k o", b=2, o=1)[b2],
                                         tvp[rows, i, :, 2 * N + 1:2 * N + 2]).then_inc(tv_st, 16)
                    sp.wait_ge(xh_r, it * TT + TT)
                    sp.wait_ge(xmi_r, it * TT + TT)
                    sp.wait_ge(xlo_r, it * TT + TT)
                    alone(sp)
                    for j, src in enumerate((xh, xmi, xlo)):
                        sp.dma_start(xpart_d[ds(g, 1), j].rearrange("a (k b) (t c) -> (a b t) k c", k=TT, c=DI),
                                     src[:, :, :]).then_inc(xq_st, 16)

                def stored(groups):
                    n = l * G + groups + 1
                    for landed, dmas in ((pick_st, 2), (tv_st, TV_STORES), (xq_st, 3)):
                        sp.wait_ge(landed, n * (16 * dmas))
                        alone(sp)

                def load_tables(ps):
                    Ub, Cc, At = pass_tables[ps]
                    for i in range(PARTS):
                        for j in range(PARTS):
                            r0 = (i * PARTS + j) * GB
                            sp.dma_start(Ub[r0:r0 + GB, :, :, :].rearrange("b g t n -> b g (t n)"),
                                         bpart_d[i, ps * (QW * TOK * NB):(ps + 1) * (QW * TOK * NB)]
                                         .rearrange("(g b f) -> b g f", g=QW, b=GB)).then_inc(tab_in[ps], 16)
                    sp.dma_start(Cc[:, :, :], cc_d[ps * QW:ps * QW + QW].rearrange("g p s -> p g s")).then_inc(tab_in[ps], 16)
                    sp.dma_start(At[:, :, :], a_d[ps * QW:ps * QW + QW].rearrange("g p s -> p g s")).then_inc(tab_in[ps], 16)
                    sp.dma_start(Bk[CROW:CROW + PARTS, ps, :, 0:GB], kap_d[ps, :, S]).then_inc(tab_in[ps], 16)

                def load(h, ps, ck_of):
                    for i in range(PARTS):
                        r0 = i * (PARTS * GB)
                        sp.dma_start(xq[r0:r0 + PARTS * GB, h, :, :, :].rearrange("p g t c -> p g (t c)"),
                                     xpart_d[ps * QW:ps * QW + QW, :, :, ds(ck_of * (CH * DI), CH * DI)]
                                     .rearrange("g j b f -> (j b) g f")).then_inc(xq_in[h], 16)
                    sp.dma_start(Uw[CROW:CROW + PARTS, h, :, :, :, :].rearrange("p g t b n -> p g (t b n)"),
                                 kpart_d[:, ps * QW:ps * QW + QW, ds(ck_of * CH, CH)].rearrange("i g t b n -> i g (t b n)")).then_inc(xq_in[h], 16)
                    sp.dma_start(By[CROW:KROWS, h, :, :, MID:MID + GB].rearrange("p t g b -> p (t g) b"),
                                 kap_d[ps, :, ds(ck_of * CH, CH)].rearrange("i t g b -> i (t g) b")).then_inc(xq_in[h], 16)

                def store(h, ps, cn, ck_of):
                    sp.wait_ge(dv_y, cn + 3)
                    for w in range(QW):
                        sp.dma_start(y_d[ps * QW + w, :, ds(ck_of * CH, CH), :].rearrange("b t c -> t b c"),
                                     ys[32 * w:32 * w + 32, h, :]).then_inc(y_out[h], 16)

                def load_y(g, u):
                    for b2 in range(2):
                        sp.dma_start(yt[b2 * S:(b2 + 1) * S, u, :, :],
                                     y_d[ds(g, 1), :, 1:S + 1, :].rearrange("a (k b) t c -> b (a t) k c", b=2)[b2]).then_inc(po_in[u], 16)

                def load_gate(g, u):
                    sp.dma_start(xnp[:, u, :, :], xn_d[ds(g, 1)].rearrange("a p c t -> p (a c) t")).then_inc(po_in[u], 16)
                    sp.dma_start(sgp[:, u, :, :], sg_d[ds(g, 1)].rearrange("a p c t -> p (a c) t")).then_inc(po_in[u], 16)

                store_gate(l * G, 0)
                with sp.Fori(0, QW) as g:
                    store_x(l * G + g, g)
                    store_gate(l * G + g + 1, g + 1)
                    store_scan(l * G + g, g, 0)
                stored(QW)
                load_tables(0)
                with sp.Fori(QW, G - 1) as g:
                    store_x(l * G + g, g)
                    store_gate(l * G + g + 1, g + 1)
                    store_scan(l * G + g, g, 1)
                store_x(l * G + G - 1, G - 1)
                sp.wait_ge(one_r, l + 1)
                load(0, 0, 0)
                load(1, 0, 1)
                store_scan(l * G + G - 1, G - 1, 1)
                stored(G)
                load_tables(1)
                for ps in range(PASSES):
                    c0 = (l * PASSES + ps) * CHUNKS
                    if ps == PASSES - 1:
                        sp.wait_ge(sg_st, l * (16 * G) + 16 * G + 16)
                        sp.wait_ge(xf_st, l * (16 * G) + 16 * G + 16)
                        alone(sp)
                        for u in range(2):
                            load_gate(u, u)
                        load_front(l * -1 + 1)
                    with sp.Fori(0, CHUNKS // 2 - 1) as c2:
                        for h in range(2):
                            cn = c0 + c2 * 2 + h
                            sp.wait_ge(pe_yq, cn * (2 * CH) + 2 * CH + 16)
                            load(h, ps, c2 * 2 + h + 2)
                            store(h, ps, cn, c2 * 2 + h)
                    for h in range(2):
                        cn = c0 + CHUNKS - 2 + h
                        if ps + 1 < PASSES:
                            sp.wait_ge(pe_yq, cn * (2 * CH) + 2 * CH + 16)
                            load(h, ps + 1, h)
                        elif h == 0:
                            sp.wait_ge(pe_yq, cn * (2 * CH) + 2 * CH + 16)
                            for n in range(2):
                                sp.wait_ge(y_out[n], l * Y_STORES + Y_STORES)
                                alone(sp)
                            sp.wait_ge(ep_out, l * (PASSES * QW * 16) + (PASSES - 1) * (QW * 16) + 16)
                            alone(sp)
                            for u in range(2):
                                load_y(u, u)
                        store(h, ps, cn, CHUNKS - 2 + h)
                    sp.wait_ge(ep_r, l * PASSES + ps + 2)
                    alone(sp)
                    for w in range(QW):
                        sp.dma_start(y_d[ps * QW + w, :, S, :], ye[32 * w:32 * w + GB, :]).then_inc(ep_out, 16)

                for n in range(2):
                    sp.wait_ge(y_out[n], l * Y_STORES + Y_STORES + QW * 16)
                    alone(sp)
                sp.wait_ge(ep_out, l * (PASSES * QW * 16) + PASSES * QW * 16 + 16)
                alone(sp)
                with sp.Fori(0, G // 2 - 1) as g2:
                    for u in range(2):
                        sp.wait_ge(yg_r, (l * G + g2 * 2 + u) * DC + DC)
                        load_gate(g2 * 2 + u + 2, u)
                        load_y(g2 * 2 + u + 2, u)
            with sp.Fori(0, G) as g:
                sp.wait_ge(po_done, g + (LAYERS - 1) * G + 2)
                sp.dma_start(out[:, ds(g, 1)], X[:, ds(g, 1), :, :]).then_inc(fin, 16)
            sp.wait_ge(sw_in, (LAYERS + 1) * (16 * SSM_LOADS))
            sp.wait_ge(fin, 16 * G)

        @block.gpsimd
        def _(pl):
            pl.memset(ones_h[:, :], 1.0 / H).then_inc(cst, 1)
            pl.memset(ones_d[:, :], 1.0 / DI).then_inc(cst, 1)
            pl.memset(ones_n[:, :], 1.0).then_inc(cst, 1)
            for n, value in enumerate((EPS_IN, 4 * EPS_IN, EPS_DM)):
                pl.memset(eps[:, n:n + 1], value).then_inc(cst, 1)
            pl.memset(zero_b[:, :], 0.0).then_inc(cst, 1)
            pl.memset(one_b[:, :], 1.0).then_inc(cst, 1)
            pl.sem_inc(pl_st, 1)
            pl.sem_inc(ep_w, 1)
            pl.wait_ge(cst, 8)
            with pl.Fori(0, LAYERS) as l:
                with pl.Fori(0, G) as g:
                    it = l * G + g
                    pl.wait_ge(v_r, it * 2 + 2)
                    pl.wait_ge(tab_r, l * 2 + 2)
                    pl.tensor_tensor(vsc[:, :, :].rearrange("p c (b t) -> p c b t", t=S), vTd[:, :, :, 0, :],
                                     vs_t[:, ds(l * HC, HC), ds(g * GB, GB)].unsqueeze(3).broadcast_to([P, HC, GB, S]),
                                     ALU.mult).then_inc(vs_r, 1)
                    for r in range(2):
                        pl.wait_ge(rcp_r, it * 2 + r + 1)
                        pl.tensor_tensor(late_half(pn, r), late_half(ex, r), rs[:, r, :].rearrange("p (j e) -> p j e", j=4)[:, :, 4:8]
                                         .unsqueeze(3).broadcast_to([P, 4, 4, S]), ALU.mult).then_inc(pn_r, 1)
                    pl.wait_ge(t2_r, it * 2 + 2)
                    pl.tensor_tensor(t3[:, :, :], X[:, ds(g, 1), :, :].rearrange("p a c t -> p (a c) t"), t2[:, :, :],
                                     ALU.add).then_inc(t3_r, 1)

            pl.wait_ge(x_done, LAYERS * G + 1)
            for buf, value in ((By[:, :, :, :, :], 0.0), (Wy[:, :, :, :], 0.0), (Bk[:, :, :, :], 0.0), (W64[:, :, :], 0.0)):
                pl.memset(buf, value).then_inc(set_r, 1)
            pl.wait_ge(set_r, 4)
            alone(pl)
            with pl.Fori(0, LAYERS) as l:
                pl.wait_ge(po_done, l * G + 1)
                alone(pl)

                def last_parts(it):
                    pl.wait_ge(xq_st, it * 48 + 48)
                    for k in range(TT):
                        pl.wait_ge(xmi_r, it * TT + k + 1)
                        pl.tensor_tensor(xlo[:, k, :], xr1[:, k, :], xmi[:, k, :], ALU.subtract).then_inc(xlo_r, 1)

                def stage(ps, c2, h):
                    Ub, Cc, At = pass_tables[ps]
                    cn = (l * PASSES + ps) * CHUNKS + c2 * 2 + h
                    s0 = c2 * (2 * CH) + h * CH
                    pl.wait_ge(pe_yq, cn * (2 * CH) + 2 * CH)
                    pl.wait_ge(dv_y, cn + 1)
                    pl.wait_ge(ac_r, cn * (4 * CH) + 4)
                    alone(pl)
                    for w in range(QW):
                        pl.tensor_tensor(Uw[0:XROWS, h, w, :, :, :],
                                         Ub[0:XROWS, w, ds(s0, CH), 0:N].unsqueeze(2).broadcast_to([XROWS, CH, GB, N]),
                                         rowmask[0:XROWS, :].unsqueeze(1).unsqueeze(3).broadcast_to([XROWS, CH, GB, N]),
                                         ALU.mult).then_inc(pl_st, 1)
                    pl.tensor_tensor(By[0:XROWS, h, :, :, MID:MID + GB],
                                     Ub[0:XROWS, :, ds(s0, CH), N:NB].rearrange("p g t o -> p t g o").broadcast_to([XROWS, CH, QW, GB]),
                                     rowmask[0:XROWS, :].unsqueeze(1).unsqueeze(1).broadcast_to([XROWS, CH, QW, GB]),
                                     ALU.mult).then_inc(pl_st, 1)
                    pl.tensor_tensor(diag_of(Wy, h), Cc[:, :, ds(s0, CH)].unsqueeze(3).broadcast_to([P, QW, CH, GB]),
                                     bmask.unsqueeze(1).unsqueeze(1).broadcast_to([P, QW, CH, GB]),
                                     ALU.mult).then_inc(pl_st, 1)
                    pl.tensor_copy(Ast[:, h, :, :], At[:, :, ds(s0, CH)]).then_inc(pl_st, 1)

                with pl.Fori(0, G - 1) as g:
                    last_parts(l * G + g)
                pl.wait_ge(xlo_r, l * (G * TT) + (G - 1) * TT)
                pl.wait_ge(zc_r, l * (G * DC) + G * DC)
                alone(pl)
                pl.memset(xq[64:96, :, :, :, :], 1.0).then_inc(one_r, 1)
                pl.wait_ge(one_r, l + 1)
                alone(pl)
                pl.wait_ge(tab_in[0], l * (16 * TABLES) + 16 * TABLES)
                alone(pl)
                for h in range(2):
                    stage(0, 0, h)
                last_parts(l * G + G - 1)
                pl.wait_ge(xlo_r, l * (G * TT) + G * TT)
                pl.wait_ge(sg_st, l * (16 * G) + 16 * G + 16)
                pl.wait_ge(xf_st, l * (16 * G) + 16 * G + 16)
                alone(pl)
                pl.memset(R[:, :, :], CLIP).then_inc(r_init, 1)
                pl.wait_ge(r_init, l * PASSES + 1)
                alone(pl)

                for ps in range(PASSES):
                    pi = l * PASSES + ps
                    with pl.Fori(1, CHUNKS // 2) as c2:
                        for h in range(2):
                            stage(ps, c2, h)
                    pl.wait_ge(ep_y, pi + 1)
                    pl.wait_ge(ep_r, pi + 1)
                    alone(pl)
                    Cc = pass_tables[ps][1]
                    pl.tensor_tensor(W64[:, :, 0:GB], Cc[:, :, S:S + 1].broadcast_to([P, QW, GB]),
                                     bmask.unsqueeze(1).broadcast_to([P, QW, GB]), ALU.mult).then_inc(ep_w, 1)
                    if ps + 1 < PASSES:
                        pl.wait_ge(tab_in[ps + 1], l * (16 * TABLES) + 16 * TABLES)
                        pl.wait_ge(ep_w, pi + 2)
                        alone(pl)
                        stage(ps + 1, 0, 0)
                        pl.wait_ge(ep_q, pi + 1)
                        alone(pl)
                        pl.memset(R[:, :, :], CLIP).then_inc(r_init, 1)
                        pl.wait_ge(r_init, pi + 2)
                        alone(pl)
                        stage(ps + 1, 0, 1)

        @block.scalar
        def _(act):
            def logarithm_set():
                act.add_instruction(mybir.InstLoadActFuncSet(name=nc.get_next_instruction_name(), act_func_set_id=LN_EXP_SET))

            logarithm_set()
            act.wait_ge(cond_in, 16)
            act.wait_ge(cst, 8)
            act.activation(condsq[:, :, :], cond[:, :, :], ACT.Square).then_inc(csq_r, 1)
            for l in range(LAYERS):
                act.wait_ge(w_in[l], 16)
                act.activation(Wsq[:, l * 5:l * 5 + 5, :, :], Wl[:, l * 5:l * 5 + 5, :, :], ACT.Square).then_inc(wsq_r, 1)
            act.wait_ge(dco_e, LAYERS * 2)
            act.activation(dlg[:, :, :], dsq[:, :, :], ACT.Ln, bias=eps[:, 2:3]).then_inc(dlg_r, 1)
            act.wait_ge(dlg_r, 1)
            act.activation(dco[:, :, :, :].rearrange("p w c b -> p (w c b)"), dlg[:, :, :].rearrange("p l f -> p (l f)"), ACT.Exp,
                           scale=-0.5).then_inc(dco_g, 1)
            act.wait_ge(ld, 16 * 4)
            with act.Fori(0, LAYERS) as l:

                def squares(n):
                    act.wait_ge(xm_r, n + 1)
                    act.activation(sq[:, :, :], xm[:, :, :], ACT.Square).then_inc(sq_r, 1)

                def deviation(n):
                    act.wait_ge(var_r, n + 1)
                    act.activation(rstd[:, :], PS[:, 7, :], ACT.Ln, bias=eps[:, 0:1]).then_inc(rg_r, 1)
                    act.wait_ge(rg_r, n * 2 + 1)
                    act.activation(rstd[:, :], rstd[:, :], ACT.Exp, scale=-0.5).then_inc(rg_r, 1)

                def keys(n):
                    for c in range(HC):
                        act.wait_ge(k_mm, n * 2 + c + 1)
                        for e in range(2):
                            act.activation(kz[:, c, e, :], PS[:, 6 + c, :], ACT.Copy, scale=par[e]).then_inc(k_r, 1)

                def values(n):
                    for c in range(HC):
                        act.wait_ge(v_mm, n * 2 + c + 1)
                        act.activation(vTd[:, c, :, :, :],
                                       PS[:, 6 + c, :].rearrange("p (b t) -> p b t", t=S).unsqueeze(2).broadcast_to([P, GB, 2, S]),
                                       ACT.Copy).then_inc(v_r, 1)

                def turned(it, r):
                    for k in range(4 * r, 4 * r + 4):
                        act.wait_ge(pt_mm, it * 8 + k + 1)
                        if k >= 4:
                            act.wait_ge(av_mm, it * 8 + k - 3)
                        act.activation(pT[:, k % 4, :, :].rearrange("p j q -> p (j q)"), PS[:, turn_bank[k], :], ACT.Copy).then_inc(pt_r, 1)

                def body(it, ahead):
                    def by_parity(b2):
                        act.wait_ge(vt_mm, it * 4 + b2 + 1)
                        for e in range(2):
                            act.activation(vbd[:, 2 * b2:2 * b2 + 2, :, e, :].rearrange("p b h d -> p (b h) d"),
                                           PS[:, 4 + b2 % 2, :].rearrange("p (m e d) -> p m e d", e=2, d=HD)[:, :, e, :],
                                           ACT.Copy, scale=masks[:, 2 + e:3 + e]).then_inc(vbd_r, 1)

                    by_parity(0)
                    by_parity(1)
                    act.wait_ge(sub_r, it * 2 + 1)
                    act.activation(ex[:, 0, :, :], ex[:, 0, :, :], ACT.Exp).then_inc(exp_r, 1)
                    if ahead:
                        squares(it + 1)
                    by_parity(2)
                    by_parity(3)
                    if ahead:
                        deviation(it + 1)
                    turned(it, 0)
                    act.wait_ge(sub_r, it * 2 + 2)
                    act.activation(ex[:, 1, :, :], ex[:, 1, :, :], ACT.Exp).then_inc(exp_r, 1)
                    if ahead:
                        keys(it + 1)
                    turned(it, 1)
                    if ahead:
                        values(it + 1)

                squares(l * G)
                deviation(l * G)
                keys(l * G)
                values(l * G)
                with act.Fori(0, G - 1) as g:
                    body(l * G + g, True)
                body(l * G + G - 1, False)

            act.wait_ge(x_done, LAYERS * G + 1)
            act.sem_inc(y_out[0], 64)
            act.sem_inc(y_out[1], 64)
            act.sem_inc(ep_out, 16)
            act.sem_inc(sg_st, 16)
            act.sem_inc(xf_st, 16)
            act.sem_inc(pick_st, 32)
            act.sem_inc(tv_st, TV_STORES * 16)
            act.sem_inc(xq_st, 48)
            with act.Fori(0, LAYERS) as l:
                act.wait_ge(sw_in, l * (16 * SSM_LOADS) + 16 * SSM_LOADS)
                act.wait_ge(po_done, l * G + 1)
                alone(act)
                act.activation(tA[:, :], dtp[:, 1:2], ACT.Tanh).then_inc(tA_r, 1)

                def tap(n):
                    for m in range(DC):
                        act.wait_ge(xp_r, n * DC + m + 1)
                        act.activation(acc[:, m, :].rearrange("p (b t) -> p b t", t=S), xp[:, m, :, 3:3 + S], ACT.Identity,
                                       scale=Wc[:, m, 3:4], bias=Ch[:, m, 0:1]).then_inc(acc_r, 1)

                def gate_tanh(n):
                    for m in range(DC):
                        act.wait_ge(g_mm, n * DC + m + 1)
                        act.wait_ge(z_r, n * DC + m + 1)
                        act.activation(th[:, m, :], PS[:, m, :], ACT.Tanh, scale=0.5).then_inc(sgt_r, 1)

                def conv_tanh(n):
                    for m in range(DC):
                        act.wait_ge(cv_r, n * (3 * DC) + 2 * DC + m + 1)
                        act.activation(th[:, m, :], acc[:, m, :], ACT.Tanh, scale=0.5).then_inc(th_r, 1)

                def squares(n):
                    for m in range(DC):
                        act.wait_ge(zc_r, n * DC + m + 1)
                        act.activation(zq[:, m, :], z[:, m, :], ACT.Square).then_inc(zq_r, 1)

                def body(it, ahead):
                    if ahead:
                        tap(it + 1)
                    act.wait_ge(zv_mm, it + 1)
                    act.activation(zlg[:, :], PS[:, 5, :], ACT.Ln, bias=eps[:, 1:2]).then_inc(zg_r, 1)
                    act.wait_ge(zg_r, it * 2 + 1)
                    act.activation(zr[:, :], zlg[:, :], ACT.Exp, scale=-0.5).then_inc(zg_r, 1)
                    for m in range(DC):
                        act.wait_ge(xg_r, it * DC + m + 1)
                        act.activation(z[:, m, :], z[:, m, :], ACT.Identity, bias=Ch[:, m, 2:3]).then_inc(xf_r, 1)
                    for m in range(DC):
                        act.wait_ge(xf_r, it * DC + m + 1)
                        act.activation(zq[:, m, :], z[:, m, :], ACT.Square).then_inc(x2_r, 1)
                    if ahead:
                        conv_tanh(it + 1)
                        gate_tanh(it + 1)
                    act.wait_ge(xw_mm, it + 1)
                    act.activation(dts[:, :], PS[64:64 + N, 6, :], ACT.Copy).then_inc(dts_r, 1)
                    act.activation(Cn[:, :], PS[32:32 + N, 6, :], ACT.Copy).then_inc(C_r, 1)
                    act.wait_ge(dt2_mm, it + 1)
                    act.activation(dtt[:, :], PS[0:N, 4, :], ACT.Tanh, bias=dtp[:, 0:1]).then_inc(dtt_r, 1)
                    logarithm_set()
                    act.wait_ge(n2_r, it + 1)
                    act.activation(n4[:, :], n2[:, :], ACT.Ln).then_inc(ng_r, 1)
                    act.wait_ge(ng_r, it * 2 + 1)
                    act.activation(mn[:, :], n4[:, :], ACT.Exp, scale=-0.5).then_inc(ng_r, 1)
                    act.wait_ge(pick_st, it * 32 + 32)
                    act.wait_ge(pk_mm, it * 2 + 1)
                    act.activation(ccs[:, 1:S + 1], PS[:, 5, 0:S], ACT.Copy, scale=-1.0).then_inc(pick_s, 1)
                    act.wait_ge(xq_st, it * 48 + 48)
                    for k in range(TT):
                        act.wait_ge(xt_mm, it * TT + k + 1)
                        act.activation(xh[:, k, :], PS[:, k, :], ACT.Copy).then_inc(xh_r, 1)
                    act.wait_ge(pk_mm, it * 2 + 2)
                    act.activation(acs[:, :], PS[:, 6, 0:S], ACT.Copy).then_inc(pick_s, 1)
                    for k in range(TT):
                        act.wait_ge(xr1_r, it * TT + k + 1 + TT)
                        act.activation(xmi[:, k, :], xr1[:, k, :], ACT.Copy).then_inc(xmi_r, 1)
                    if ahead:
                        squares(it + 1)

                tap(l * G)
                conv_tanh(l * G)
                gate_tanh(l * G)
                squares(l * G)
                with act.Fori(0, G - 1) as g:
                    body(l * G + g, True)
                body(l * G + G - 1, False)

                with act.Fori(0, PASSES) as ps:
                    pi = l * PASSES + ps
                    with act.Fori(0, CHUNKS // 2) as c2:
                        for h in range(2):
                            cn = pi * CHUNKS + c2 * 2 + h
                            act.wait_ge(pl_st, cn * STAGED + STAGED + 1)
                            for t in range(CH):
                                for w in range(QW):
                                    act.wait_ge(dv_q, cn * (QW * CH) + QW * t + w + 1 + QW)
                                    act.activation(R[:, w, :], q[:, t % 2, w, :], ACT.Relu,
                                                   scale=Ast[:, h, w, t:t + 1]).then_inc(ac_r, 1)

        @block.tensor
        def _(pe):
            def project(bank, w, rhs, done, free=None):
                for m in range(HC):
                    if free:
                        free(m)
                    for c in range(HC):
                        mm = pe.matmul(PS[:, bank + m, :], W[:, w, c, m * P:(m + 1) * P], rhs[:, c, :],
                                       start=(c == 0), stop=(c == HC - 1))
                    mm.then_inc(done, 1)

            pe.wait_ge(cst, 8)
            pe.wait_ge(csq_r, 1)
            for l in range(LAYERS):
                pe.wait_ge(wsq_r, l + 1)
                for w in range(5):
                    st = 0 if w < 3 else HC
                    for m in range(HC):
                        for c in range(HC):
                            mm = pe.matmul(PS[:, 2 * l + w // 4, (w % 4) * P + m * B:(w % 4) * P + (m + 1) * B],
                                           Wsq[:, l * 5 + w, c, m * P:(m + 1) * P], condsq[:, st + c, :],
                                           start=(c == 0), stop=(c == HC - 1))
                mm.then_inc(dco_mm, 1)
            pe.wait_ge(dco_e, LAYERS * 2)
            pe.wait_ge(ld, 16 * 4)
            alone(pe)
            with pe.Fori(0, LAYERS) as l:

                def mean(n):
                    pe.wait_ge(xs_r, n + 1)
                    for c in range(HC):
                        mm = pe.matmul(PS[:, 6, :], ones_h[:, :], xs[:, c, :], start=(c == 0), stop=(c == HC - 1))
                    mm.then_inc(mean_r, 1)

                def variance(n):
                    pe.wait_ge(sq_r, n + 1)
                    for c in range(HC):
                        mm = pe.matmul(PS[:, 7, :], ones_h[:, :], sq[:, c, :], start=(c == 0), stop=(c == HC - 1))
                    mm.then_inc(var_r, 1)

                def keys_queries(n):
                    pe.wait_ge(xn_r, n + 1)
                    project(6, 1, xn, k_mm)
                    project(6, 0, xn, q_mm, lambda m: pe.wait_ge(k_r, n * 4 + 2 * m + 2))

                def values(n):
                    project(6, 2, xn, v_mm, lambda m: pe.wait_ge(q_r, n * 2 + m + 1))

                def scores(it, r, ahead=False):
                    for b in range(4):
                        for c in range(HC):
                            if ahead and (b, c) == (1, 0):
                                variance(it + 1)
                            for j in range(4):
                                bb = 4 * r + b
                                col = ((b // 2) * HC + c) * P
                                mm = pe.matmul(PS[(b % 2) * S:(b % 2 + 1) * S, j, col:col + P],
                                               qs[32 * j:32 * j + 32, c, bb * S:(bb + 1) * S],
                                               kz[32 * j:32 * j + 32, c, :, bb * S:(bb + 1) * S],
                                               start=True, stop=True)
                    mm.then_inc(sc_mm, 1)

                def turn_values(it, b2s):
                    for b2 in b2s:
                        if b2 >= 2:
                            pe.wait_ge(vbd_r, it * 8 + 2 * b2 - 2)
                        for bb in (2 * b2, 2 * b2 + 1):
                            for c in range(HC):
                                col = (bb % 2) * H + c * P
                                mm = pe.transpose(PS[:, 4 + b2 % 2, col:col + P],
                                                  vTd[:, c, bb, :, :].rearrange("p a t -> p (a t)"), ident[:, :])
                        mm.then_inc(vt_mm, 1)

                def turn(it, k):
                    if k % 4 >= 2:
                        pe.wait_ge(pt_r, it * 8 + k - 1)
                    for j in range(4):
                        mm = pe.transpose(PS[:, turn_bank[k], j * P:(j + 1) * P],
                                          pn[:, k // 4, j, (k % 4) * P:(k % 4 + 1) * P], ident[:, :])
                    mm.then_inc(pt_mm, 1)

                def weigh(it, k):
                    pe.wait_ge(pt_r, it * 8 + k + 1)
                    for b in range(2):
                        for j in range(4):
                            bb, h4 = 4 * (k // 4) + 2 * (k // 2 % 2) + b, (k % 2) * 4 + j
                            col = (k % 2) * (4 * S) + (2 * (k // 2 % 2) + b) * S
                            mm = pe.matmul(PS[32 * j:32 * j + 32, 5, col:col + S],
                                           vbd[:, bb, h4, :, :].rearrange("p a d -> p (a d)"),
                                           pT[:, k % 4, j, b * S:(b + 1) * S], start=True, stop=True)
                    mm.then_inc(av_mm, 1)

                def attend(it, r):
                    pe.wait_ge(pe_r, it * 2 + r + 1)
                    if r == 0:
                        pe.wait_ge(vbd_r, it * 8 + 8)
                    else:
                        pe.wait_ge(sub_r, it * 2 + 2)
                        pe.wait_ge(av_r, it * 2 + 1)
                    k0 = 4 * r
                    turn(it, k0)
                    turn(it, k0 + 1)
                    for k in range(k0 + 2, k0 + 4):
                        weigh(it, k - 2)
                        if k == k0 + 2:
                            pe.wait_ge(pn_r, it * 2 + r + 1)
                        turn(it, k)
                    weigh(it, k0 + 2)
                    weigh(it, k0 + 3)

                def body(it, ahead):
                    pe.wait_ge(t1_r, it * 2 + 2)
                    pe.wait_ge(q_r, it * 2 + 2)
                    scores(it, 0)
                    pe.wait_ge(v_r, it * 2 + 2)
                    turn_values(it, (0, 1))
                    turn_values(it, (2, 3))
                    if ahead:
                        mean(it + 1)
                    pe.wait_ge(sub_r, it * 2 + 1)
                    scores(it, 1, ahead)
                    attend(it, 0)
                    pe.wait_ge(sub_r, it * 2 + 2)
                    pe.wait_ge(vs_r, it + 1)
                    project(2, 4, vsc, u_mm)
                    if ahead:
                        keys_queries(it + 1)
                    attend(it, 1)
                    pe.wait_ge(av_r, it * 2 + 2)
                    project(0, 3, av, w_mm)
                    if ahead:
                        values(it + 1)

                mean(l * G)
                variance(l * G)
                pe.wait_ge(w_use, l + 1)
                keys_queries(l * G)
                values(l * G)
                with pe.Fori(0, G - 1) as g:
                    body(l * G + g, True)
                body(l * G + G - 1, False)

            pe.wait_ge(x_done, LAYERS * G + 1)
            pe.sem_inc(pe_yq, 16)
            pe.sem_inc(ep_y, 1)
            with pe.Fori(0, LAYERS) as l:
                pe.wait_ge(sw_in, l * (16 * SSM_LOADS) + 16 * SSM_LOADS)
                pe.wait_ge(po_done, l * G + 1)
                alone(pe)

                def into(n, g, m, done):
                    for c in range(HC):
                        mm = pe.matmul(PS[:, m % DC, :], Win[:, c, m * P:(m + 1) * P],
                                       X[:, ds(g, 1), c, :].rearrange("p a t -> p (a t)"), start=(c == 0), stop=(c == HC - 1))
                    mm.then_inc(done, 1)

                def gates(n, g):
                    for m in range(DC):
                        pe.wait_ge(xp_r, n * DC + m + 1)
                        into(n, g, DC + m, g_mm)

                def mean(n):
                    for m in range(DC):
                        pe.wait_ge(z_r, n * DC + m + 1)
                        mm = pe.matmul(PS[:, 4, :], ones_d[:, :], zs[:, m, :], start=(m == 0), stop=(m == DC - 1))
                    mm.then_inc(zm_mm, 1)

                def body(it, g, ahead):
                    if ahead:
                        for m in range(DC):
                            pe.wait_ge(sg_r, it * DC + m + 1)
                            pe.wait_ge(xr1_r, it * TT + m + 1)
                            into(it + 1, g + 1, m, xr_mm)
                    for m in range(DC):
                        pe.wait_ge(zq_r, it * DC + m + 1)
                        mm = pe.matmul(PS[:, 5, :], ones_d[:, :], zq[:, m, :], start=(m == 0), stop=(m == DC - 1))
                    mm.then_inc(zv_mm, 1)
                    if ahead:
                        gates(it + 1, g + 1)
                    for m in range(DC):
                        pe.wait_ge(xf_r, it * DC + m + 1)
                        mm = pe.matmul(PS[0:96, 6, :], Wx[:, m, :], z[:, m, :], start=(m == 0), stop=(m == DC - 1))
                    mm.then_inc(xw_mm, 1)
                    for m in range(DC):
                        pe.wait_ge(x2_r, it * DC + m + 1)
                        mm = pe.matmul(PS[0:N, 7, :], ones_n[:, :], zq[:, m, :], start=(m == 0), stop=(m == DC - 1))
                    mm.then_inc(nrm_mm, 1)
                    pe.wait_ge(dts_r, it + 1)
                    alone(pe)
                    pe.matmul(PS[0:N, 4, :], Wdt[:, :], dts[:, :], start=True, stop=True).then_inc(dt2_mm, 1)

                    def pick(src, bank):
                        for b in range(GB):
                            mm = pe.matmul(PS[:, bank, 0:S], sel[:, b, :], src[:, b * S:(b + 1) * S],
                                           start=(b == 0), stop=(b == GB - 1))
                        mm.then_inc(pk_mm, 1)

                    pe.wait_ge(C_r, it + 1)
                    pick(Cn, 5)
                    for k in range(TT):
                        pe.wait_ge(sg_r, (it + (1 if ahead else 0)) * DC + k + 1)
                        for m in range(DC):
                            mm = pe.transpose(PS[:, k, m * P:(m + 1) * P], z[:, m, k * P:(k + 1) * P], ident[:, :])
                        mm.then_inc(xt_mm, 1)
                    if ahead:
                        pe.wait_ge(dtt_r, it + 1)
                        mean(it + 1)
                    pe.wait_ge(Bd_r, it + 1)
                    pe.wait_ge(am_r, it * 2 + 2)
                    pick(am, 6)
                    for i, (src, off) in enumerate(((Bd, 0), (am, 0), (Bd, 1), (am1, 0), (Cn, 0))):
                        for k in range(TT):
                            c0 = (i * TT + k) * N
                            mm = pe.transpose(PS[:, 7, c0:c0 + N], src[:, k * P + off:(k + 1) * P + off], ident[0:N, 0:N])
                    mm.then_inc(tok_mm, 1)

                for m in range(DC):
                    into(l * G, 0, m, xr_mm)
                gates(l * G, 0)
                mean(l * G)
                with pe.Fori(0, G - 1) as g:
                    body(l * G + g, g, True)
                body(l * G + G - 1, G - 1, False)

                pe.wait_ge(xr1_r, l * (G * TT) + G * TT + TT)
                pe.wait_ge(pick_s, l * (2 * G) + 2 * G)
                pe.wait_ge(tv_s, l * (11 * G) + 11 * G)
                alone(pe)
                with pe.Fori(0, PASSES) as ps:
                    pi = l * PASSES + ps

                    def inputs(cn, c2, h, t):
                        if t == 0:
                            pe.wait_ge(xq_in[h], (pi * (CHUNKS // 2) + c2) * (XQ * 16) + XQ * 16)
                            pe.wait_ge(pl_st, cn * STAGED + STAGED + 1)
                        for w in range(QW):
                            pe.wait_ge(dv_q, cn * (QW * CH) + QW * t + w + 1)
                            pe.matmul(PS[:, w, :], Uw[0:KROWS, h, w, t, :, :].rearrange("p b n -> p (b n)"),
                                      xq[0:KROWS, h, w, t, :], start=True, stop=True).then_inc(pe_w, 1)

                    def y_of(cn, h, t):
                        if t == 0:
                            pe.wait_ge(dv_y, cn + 1)
                        for p in range(2):
                            pe.wait_ge(dv_q, cn * (QW * CH) + QW * t + 2 * p + 2 + QW)
                            for w in (2 * p, 2 * p + 1):
                                pe.matmul(PS[32 * w:32 * w + 32, 4 + h, :], Wy[:, h, w, t * 32:(t + 1) * 32],
                                          q[:, t % 2, w, :], start=(t == 0), stop=False, skip_group_check=True)
                            for w in (2 * p, 2 * p + 1):
                                mm = pe.matmul(PS[32 * w:32 * w + 32, 4 + h, :], By[0:KROWS, h, t, w, MID - t * GB:MID + (CH - t) * GB],
                                               xq[0:KROWS, h, w, t, :], start=False, stop=(t == CH - 1), skip_group_check=True)
                            mm.then_inc(pe_yq, 1)

                    def chunk(c2, h, ahead):
                        cn = pi * CHUNKS + c2 * 2 + h
                        for t in range(1, CH):
                            inputs(cn, c2, h, t)
                            y_of(cn, h, t - 1)
                        if ahead:
                            inputs(cn + 1, c2 + h, 1 - h, 0)
                        y_of(cn, h, CH - 1)

                    inputs(pi * CHUNKS, 0, 0, 0)
                    with pe.Fori(0, CHUNKS // 2 - 1) as c2:
                        for h in range(2):
                            chunk(c2, h, True)
                    chunk(CHUNKS // 2 - 1, 0, True)
                    chunk(CHUNKS // 2 - 1, 1, False)
                    pe.wait_ge(ep_q, pi + 1)
                    pe.wait_ge(ep_w, pi + 2)
                    for w in range(QW):
                        mm = pe.matmul(PS[32 * w:32 * w + 32, 6, :], W64[:, w, :], q[:, 1, w, :],
                                       start=True, stop=False, skip_group_check=True)
                    mm = pe.matmul(PS[:, 6, :], Bk[0:KROWS, ds(ps, 1), :, :].rearrange("p a g c -> p (a g c)"), one_b[0:KROWS, :],
                                   start=False, stop=True, skip_group_check=True)
                    mm.then_inc(ep_y, 1)

                pe.wait_ge(ep_r, l * PASSES + PASSES + 1)
                pe.wait_ge(dv_y, l * (PASSES * CHUNKS) + PASSES * CHUNKS + 2)
                alone(pe)
                def turn_y(it, n2, u):
                    pe.wait_ge(so_in, l * 32 + 32)
                    alone(pe)
                    pe.wait_ge(po_in[u], (l * (G // 2) + n2) * 64 + 64)
                    for m in range(DC):
                        pe.wait_ge(yf_r, it * DC + m + 1)
                        for k in range(TT):
                            mm = pe.transpose(PS[:, m, k * P:(k + 1) * P], yt[:, u, k, m * P:(m + 1) * P], ident[:, :])
                        mm.then_inc(po_mm, 1)

                def outward(g2, u, ahead):
                    it = l * G + g2 * 2 + u
                    if ahead:
                        turn_y(it + 1, g2 + u, 1 - u)
                    for m in range(HC):
                        for c in range(DC):
                            if m == 0:
                                pe.wait_ge(yg_r, it * DC + c + 1)
                            mm = pe.matmul(PS[:, 4 + 2 * u + m, :], Wo[:, c, m * P:(m + 1) * P], yg[:, u, c, :],
                                           start=(c == 0), stop=(c == DC - 1))
                        mm.then_inc(o_mm, 1)

                turn_y(l * G, 0, 0)
                with pe.Fori(0, G // 2 - 1) as g2:
                    for u in range(2):
                        outward(g2, u, True)
                outward(G // 2 - 1, 0, True)
                outward(G // 2 - 1, 1, False)

        @block.vector
        def _(v):
            def tiled(ap):
                return ap.rearrange("p (b t) -> p b t", t=S)

            def by_batch(tab, c, g):
                return tab[:, c, ds(g * GB, GB)].unsqueeze(2).broadcast_to([P, GB, S])

            def of_layer(tab, n, g):
                return tab[:, ds(n, 1), ds(g * GB, GB)].rearrange("p a b -> p (a b)").unsqueeze(2).broadcast_to([P, GB, S])

            def root(y, x, e, y0, tmp, done, n):
                v.scalar_tensor_tensor(out=tmp, in0=x, scalar=e, in1=y0, op0=ALU.add, op1=ALU.mult).then_inc(done, 1)
                v.wait_ge(done, n + 1)
                v.scalar_tensor_tensor(out=tmp, in0=tmp, scalar=-0.5, in1=y0, op0=ALU.mult, op1=ALU.mult).then_inc(done, 1)
                v.wait_ge(done, n + 2)
                v.scalar_tensor_tensor(out=y, in0=tmp, scalar=1.5, in1=y0, op0=ALU.add, op1=ALU.mult).then_inc(done, 1)
                v.wait_ge(done, n + 3)

            v.wait_ge(cond_in, 16)
            v.sem_inc(x_done, 1)
            v.sem_inc(t1_r, 2)
            for l in range(LAYERS):
                v.wait_ge(dco_mm, l + 1)
                v.tensor_copy(dsq[:, l, 0:512], PS[:, 2 * l, :]).then_inc(dco_e, 1)
                v.tensor_copy(dsq[:, l, 512:5 * P], PS[:, 2 * l + 1, 0:P]).then_inc(dco_e, 1)
            v.wait_ge(dco_e, LAYERS * 2)
            v.wait_ge(x_in[0], 16)
            v.wait_ge(ld, 16 * 4)
            alone(v)
            with v.Fori(0, LAYERS) as l:
                v.wait_ge(x_done, l * G + 1)
                alone(v)

                def styled(n, g):
                    v.tensor_tensor(xs[:, :, :].rearrange("p c (b t) -> p c b t", t=S),
                                    X[:, ds(g, 1), :, :].rearrange("p a c (b t) -> p (a c) b t", t=S),
                                    cond[:, 0:HC, ds(g * GB, GB)].unsqueeze(3).broadcast_to([P, HC, GB, S]),
                                    ALU.mult).then_inc(xs_r, 1)

                def centred(n):
                    v.wait_ge(mean_r, n + 1)
                    v.tensor_tensor(xm[:, :, :], xs[:, :, :], PS[:, 6:7, :].broadcast_to([P, HC, TOK]),
                                    ALU.subtract).then_inc(xm_r, 1)

                def normed(n):
                    v.wait_ge(var_r, n + 1)
                    v.wait_ge(rg_r, n * 2 + 2)
                    root(rstd[:, :], PS[:, 7, :], EPS_IN, rstd[:, :], vare[:, :], rstd_r, n * 3)
                    v.tensor_tensor(xn[:, :, :], xm[:, :, :], rstd[:, :].unsqueeze(1).broadcast_to([P, HC, TOK]),
                                    ALU.mult).then_inc(xn_r, 1)

                def queries(n, g):
                    for c in range(HC):
                        v.wait_ge(q_mm, n * 2 + c + 1)
                        v.tensor_tensor(tiled(qs[:, c, :]), tiled(PS[:, 6 + c, :]), of_layer(qk_t, l * HC + c, g),
                                        ALU.mult).then_inc(q_r, 1)

                def scores(it, r):
                    sc = PS[:, 0:4, :].rearrange("p j (e k) -> p (j e) k", k=S)
                    v.wait_ge(sc_mm, it * 2 + r + 1)
                    v.tensor_reduce(mx[:, r, :], sc, AX.X, ALU.max).then_inc(max_r, 1)
                    v.wait_ge(max_r, it * 2 + r + 1)
                    v.tensor_tensor(ex[:, r, :, :].rearrange("p j (e k) -> p (j e) k", k=S), sc,
                                    mx[:, r, :].unsqueeze(2).broadcast_to([P, 32, S]), ALU.subtract).then_inc(sub_r, 1)

                def sums(it, r):
                    v.wait_ge(exp_r, it * 2 + r + 1)
                    v.tensor_reduce(sm[:, r, :], ex[:, r, :, :].rearrange("p j (e k) -> p (j e) k", k=S),
                                    AX.X, ALU.add).then_inc(sum_r, 1)
                    v.wait_ge(sum_r, it * 2 + r + 1)
                    v.reciprocal(rs[:, r, :], sm[:, r, :]).then_inc(rcp_r, 1)
                    v.wait_ge(rcp_r, it * 2 + r + 1)
                    v.tensor_tensor(early_half(pn, r), early_half(ex, r), rs[:, r, :].rearrange("p (j e) -> p j e", j=4)[:, :, 0:4]
                                    .unsqueeze(3).broadcast_to([P, 4, 4, S]), ALU.mult).then_inc(pe_r, 1)

                def out_of(it, g, r):
                    v.wait_ge(av_mm, it * 8 + 4 * r + 4)
                    v.tensor_tensor(av[:, :, r * 4 * S:(r + 1) * 4 * S].rearrange("p c (b t) -> p c b t", t=S),
                                    PS[:, 5, :].rearrange("p (c b t) -> p c b t", c=HC, t=S),
                                    vs_t[:, ds(l * HC, HC), ds(g * GB + 4 * r, 4)].unsqueeze(3).broadcast_to([P, HC, 4, S]),
                                    ALU.mult).then_inc(av_r, 1)

                def body(it, g, ahead):
                    if ahead:
                        styled(it + 1, g + 1)
                    scores(it, 0)
                    if ahead:
                        centred(it + 1)
                    sums(it, 0)
                    scores(it, 1)
                    if ahead:
                        normed(it + 1)
                    sums(it, 1)
                    out_of(it, g, 0)
                    if ahead:
                        queries(it + 1, g + 1)
                    out_of(it, g, 1)
                    for c in range(HC):
                        v.wait_ge(u_mm, it * 2 + c + 1)
                        v.tensor_tensor(tiled(t2[:, c, :]), tiled(PS[:, 2 + c, :]), of_layer(dco[:, :, :, :].rearrange("p w c b -> p (w c) b"), l * (5 * HC) + 4 * HC + c, g),
                                        ALU.mult).then_inc(t2_r, 1)
                    for c in range(HC):
                        v.wait_ge(w_mm, it * 2 + c + 1)
                        v.tensor_tensor(tiled(t1[:, c, :]), tiled(PS[:, c, :]), of_layer(dco[:, :, :, :].rearrange("p w c b -> p (w c) b"), l * (5 * HC) + 3 * HC + c, g),
                                        ALU.mult).then_inc(t1_r, 1)
                    v.wait_ge(t1_r, it * 2 + 4)
                    v.wait_ge(t3_r, it + 1)
                    v.tensor_tensor(X[:, ds(g, 1), :, :].rearrange("p a c t -> p (a c t)"), t3[:, :, :].rearrange("p c t -> p (c t)"),
                                    t1[:, :, :].rearrange("p c t -> p (c t)"), ALU.add).then_inc(x_done, 1)

                def demodulation():
                    dcv = dco[:, ds(l * 5, 5), :, :].rearrange("p w c b -> p (w c b)")
                    root(dcv, dsq[:, ds(l, 1), :].rearrange("p l f -> p (l f)"), EPS_DM, dcv,
                         t1[:, :, :].rearrange("p c t -> p (c t)")[:, 0:5 * HC * B], dco_r, l * 3)
                    v.scalar_tensor_tensor(out=qk_t[:, ds(l * HC, HC), :], in0=dco[:, ds(l * 5, 1), :, :].rearrange("p w c b -> p (w c) b"),
                                           scalar=float(HD) ** -0.5, in1=dco[:, ds(l * 5 + 1, 1), :, :].rearrange("p w c b -> p (w c) b"),
                                           op0=ALU.mult, op1=ALU.mult).then_inc(tab_r, 1)
                    v.tensor_tensor(vs_t[:, ds(l * HC, HC), :], dco[:, ds(l * 5 + 2, 1), :, :].rearrange("p w c b -> p (w c) b"),
                                    cond[:, HC:2 * HC, :], ALU.mult).then_inc(tab_r, 1)
                    v.wait_ge(tab_r, l * 2 + 2)
                    alone(v)

                styled(l * G, 0)
                v.tensor_copy(W[:, :, :, :], Wl[:, ds(l * 5, 5), :, :]).then_inc(w_use, 1)
                centred(l * G)
                v.wait_ge(dco_g, 1)
                v.wait_ge(x_in[1], 16)
                alone(v)
                demodulation()
                normed(l * G)
                queries(l * G, 0)
                with v.Fori(0, G - 1) as g:
                    body(l * G + g, g, True)
                body(l * G + G - 1, G - 1, False)

            v.wait_ge(x_done, LAYERS * G + 1)
            v.sem_inc(po_done, 1)
            v.sem_inc(xr1_r, TT)
            v.sem_inc(yf_r, DC)
            v.sem_inc(dv_q, QW)
            v.sem_inc(ac_r, 20)
            v.sem_inc(dv_y, 2)
            v.sem_inc(ep_r, 1)
            with v.Fori(0, LAYERS) as l:
                v.wait_ge(po_done, l * G + 1)
                v.wait_ge(tA_r, l + 1)
                v.tensor_scalar(A01[:, :], tA[:, :], -0.01, None, ALU.mult).then_inc(A_r, 1)
                v.memset(xp[:, :, :, 0:3], 0.0).then_inc(A_r, 1)
                v.memset(ccs[:, 0:1], 0.0).then_inc(A_r, 1)
                v.memset(am1[:, :], 1.0).then_inc(A_r, 1)
                v.memset(Bd[:, TOK:TOK + 1], 0.0).then_inc(A_r, 1)
                v.wait_ge(A_r, l * 5 + 5)
                alone(v)

                def embed(n, g):
                    for m in range(DC):
                        v.wait_ge(xr_mm, n * DC + m + 1)
                        v.tensor_tensor(xp[:, m, :, 3:3 + S], tiled(PS[:, m, :]), by_batch(cond, m, g), ALU.add).then_inc(xp_r, 1)

                def conv(n, taps):
                    for j in taps:
                        for m in range(DC):
                            if j == 0:
                                v.wait_ge(acc_r, n * DC + m + 1)
                            else:
                                v.wait_ge(cv_r, n * (3 * DC) + (j - 1) * DC + m + 1)
                            v.scalar_tensor_tensor(out=tiled(acc[:, m, :]), in0=xp[:, m, :, j:j + S], scalar=Wc[:, m, j:j + 1],
                                                   in1=tiled(acc[:, m, :]), op0=ALU.mult, op1=ALU.add).then_inc(cv_r, 1)

                def silu(n):
                    for m in range(DC):
                        v.wait_ge(th_r, n * DC + m + 1)
                        v.scalar_tensor_tensor(out=zs[:, m, :], in0=th[:, m, :], scalar=1.0, in1=acc[:, m, :],
                                               op0=ALU.add, op1=ALU.mult).then_inc(z_r, 1)

                def gate(n):
                    v.wait_ge(sg_st, n * 16 + 16)
                    for m in range(DC):
                        v.wait_ge(sgt_r, n * DC + m + 1)
                        v.scalar_tensor_tensor(out=sg[:, m, :], in0=th[:, m, :], scalar=1.0, in1=PS[:, m, :],
                                               op0=ALU.add, op1=ALU.mult).then_inc(sg_r, 1)

                def centred(n):
                    v.wait_ge(xf_st, n * 16 + 16)
                    v.wait_ge(zm_mm, n + 1)
                    for m in range(DC):
                        v.tensor_tensor(z[:, m, :], zs[:, m, :], PS[:, 4, :], ALU.subtract).then_inc(zc_r, 1)

                def body(it, g, ahead):
                    if ahead:
                        embed(it + 1, g + 1)
                        conv(it + 1, (0, 1))
                    v.wait_ge(zv_mm, it + 1)
                    v.wait_ge(zg_r, it * 2 + 2)
                    root(zr[:, :], PS[:, 5, :], 4 * EPS_IN, zr[:, :], zve[:, :], zr_r, it * 3)
                    for m in range(DC):
                        v.scalar_tensor_tensor(out=z[:, m, :], in0=z[:, m, :], scalar=Ch[:, m, 1:2], in1=zr[:, :],
                                               op0=ALU.mult, op1=ALU.mult).then_inc(xg_r, 1)
                    if ahead:
                        conv(it + 1, (2,))
                        silu(it + 1)
                        gate(it + 1)
                    v.wait_ge(nrm_mm, it + 1)
                    v.tensor_scalar(n2[:, :], PS[0:N, 7, :], 1.0, LEAST, ALU.min, ALU.max).then_inc(n2_r, 1)
                    v.wait_ge(dtt_r, it + 1)
                    v.tensor_scalar(am[:, :], dtt[:, :], A01[:, 0:1], 1.0, ALU.mult, ALU.add).then_inc(am_r, 1)
                    v.tensor_scalar(tiled(am1[:, :])[:, :, 0:S - 1], tiled(dtt[:, :])[:, :, 1:S], A01[:, 0:1], 1.0,
                                    ALU.mult, ALU.add).then_inc(am_r, 1)
                    v.wait_ge(n2_r, it + 1)
                    v.wait_ge(ng_r, it * 2 + 2)
                    root(mn[:, :], n2[:, :], 0.0, mn[:, :], n3[:, :], mn_r, it * 3)
                    v.tensor_tensor(mn[:, :], mn[:, :], n2[:, :], ALU.mult).then_inc(mm_r, 1)
                    v.wait_ge(mm_r, it + 1)
                    v.tensor_tensor(Bd[:, 0:TOK], PS[0:N, 6, :], mn[:, :], ALU.mult).then_inc(Bd_r, 1)
                    for k in range(TT):
                        v.wait_ge(xh_r, it * TT + k + 1)
                        v.tensor_tensor(xr1[:, k, :], PS[:, k, :], xh[:, k, :], ALU.subtract).then_inc(xr1_r, 1)
                    if ahead:
                        centred(it + 1)
                    v.wait_ge(tv_st, it * (TV_STORES * 16) + TV_STORES * 16)
                    v.wait_ge(tok_mm, it + 1)
                    rows = PS[:, 7, 0:5 * TT * N].rearrange("p (i k n) -> p i k n", i=5, n=N)
                    v.reciprocal(rT[:, :, :, :], rows[:, 1:4:2, :, :]).then_inc(rt_r, 1)
                    v.wait_ge(rt_r, it + 1)
                    v.tensor_tensor(tv[:, :, 0:N], rows[:, 0, :, :], rT[:, 0, :, :], ALU.mult).then_inc(tv_s, 1)
                    v.tensor_scalar(tv[:, :, N:2 * N], rT[:, 0, :, :], -CLIP, CLIP, ALU.mult, ALU.add).then_inc(tv_s, 1)
                    v.tensor_tensor(tb[:, :, :], rows[:, 2, :, :], rT[:, 1, :, :], ALU.mult).then_inc(tv_s, 1)
                    v.scalar_tensor_tensor(out=tc[:, :, :], in0=rT[:, 1, :, :], scalar=CLIP, in1=rows[:, 4, :, :],
                                           op0=ALU.mult, op1=ALU.mult).then_inc(tv_s, 1)
                    v.wait_ge(tv_s, it * 11 + 3)
                    v.scalar_tensor_tensor(out=tb2[:, :, :], in0=tb[:, :, :], scalar=-1.0, in1=rows[:, 4, :, :],
                                           op0=ALU.mult, op1=ALU.mult).then_inc(tv_s, 1)
                    v.wait_ge(tv_s, it * 11 + 4)
                    v.tensor_reduce(tv[:, :, 2 * N + 1], tc[:, :, :], AX.X, ALU.add).then_inc(tv_s, 1)
                    v.wait_ge(tv_s, it * 11 + 5)
                    v.tensor_reduce(tv[:, :, 2 * N], tb2[:, :, :], AX.X, ALU.add).then_inc(tv_s, 1)
                    v.wait_ge(tv_s, it * 11 + 7)
                    v.tensor_copy(tvp[:, 0, :, :], tv[:, :, :]).then_inc(tv_s, 1)
                    v.wait_ge(tv_s, it * 11 + 8)
                    v.tensor_tensor(tvr[:, :, :], tv[:, :, :], tvp[:, 0, :, :], ALU.subtract).then_inc(tv_s, 1)
                    v.wait_ge(tv_s, it * 11 + 9)
                    v.tensor_copy(tvp[:, 1, :, :], tvr[:, :, :]).then_inc(tv_s, 1)
                    v.wait_ge(tv_s, it * 11 + 10)
                    v.tensor_tensor(tvp[:, 2, :, :], tvr[:, :, :], tvp[:, 1, :, :], ALU.subtract).then_inc(tv_s, 1)

                embed(l * G, 0)
                conv(l * G, range(3))
                silu(l * G)
                gate(l * G)
                centred(l * G)
                with v.Fori(0, G - 1) as g:
                    body(l * G + g, g, True)
                body(l * G + G - 1, G - 1, False)

                v.wait_ge(xf_st, l * (16 * G) + 16 * G + 16)
                v.wait_ge(sg_st, l * (16 * G) + 16 * G + 16)
                alone(v)
                with v.Fori(0, PASSES) as ps:
                    pi = l * PASSES + ps
                    v.wait_ge(r_init, pi + 1)
                    alone(v)

                    def step(cn, t):
                        for w in range(QW):
                            n = QW * t + w
                            v.wait_ge(pe_w, cn * (QW * CH) + n + 1)
                            v.wait_ge(ac_r, cn * (QW * CH) + n + 17)
                            if w % 2 == 0:
                                v.wait_ge(pe_yq, cn * (2 * CH) + 2 * t + w // 2 + 13)
                            v.scalar_tensor_tensor(out=q[:, t % 2, w, :], in0=R[:, w, :], scalar=2 * CLIP, in1=PS[:, w, :],
                                                   op0=ALU.min, op1=ALU.subtract).then_inc(dv_q, 1)

                    def chunk(c2, h, ahead):
                        cn = pi * CHUNKS + c2 * 2 + h
                        for t in range(1, CH):
                            step(cn, t)
                        if ahead:
                            step(cn + 1, 0)
                        v.wait_ge(pe_yq, cn * (2 * CH) + 2 * CH + 16)
                        v.wait_ge(y_out[h], (pi * (CHUNKS // 2) + c2) * 64 + 64)
                        v.tensor_copy(ys[:, h, :], PS[:, 4 + h, :]).then_inc(dv_y, 1)

                    step(pi * CHUNKS, 0)
                    with v.Fori(0, CHUNKS // 2 - 1) as c2:
                        for h in range(2):
                            chunk(c2, h, True)
                    chunk(CHUNKS // 2 - 1, 0, True)
                    chunk(CHUNKS // 2 - 1, 1, False)
                    v.wait_ge(ac_r, pi * (4 * S) + 4 * S + 20)
                    v.wait_ge(pe_yq, pi * (CHUNKS * 2 * CH) + CHUNKS * 2 * CH + 16)
                    v.tensor_scalar(q[:, 1, :, :], R[:, :, :], 2 * CLIP, None, ALU.min).then_inc(ep_q, 1)
                    v.wait_ge(ep_y, pi + 2)
                    v.wait_ge(ep_out, pi * 64 + 16)
                    v.tensor_copy(ye[:, :], PS[:, 6, :]).then_inc(ep_r, 1)

                def gated(it, n2, u):
                    v.wait_ge(so_in, l * 32 + 32)
                    alone(v)
                    v.wait_ge(po_in[u], (l * (G // 2) + n2) * 64 + 64)
                    for m in range(DC):
                        v.wait_ge(po_mm, it * DC + m + 1)
                        v.scalar_tensor_tensor(out=yf[:, m, :], in0=xnp[:, u, m, :], scalar=Dsk[:, m, :], in1=PS[:, m, :],
                                               op0=ALU.mult, op1=ALU.add).then_inc(yf_r, 1)
                        v.wait_ge(yf_r, it * DC + m + 1 + DC)
                        v.tensor_tensor(yg[:, u, m, :], yf[:, m, :], sgp[:, u, m, :], ALU.mult).then_inc(yg_r, 1)

                def residual(g2, u, ahead):
                    g = g2 * 2 + u
                    it = l * G + g
                    if ahead:
                        gated(it + 1, g2 + u, 1 - u)
                    v.wait_ge(o_mm, it * HC + HC)
                    xg = X[:, ds(g, 1), :, :].rearrange("p a c t -> p (a c t)")
                    v.scalar_tensor_tensor(out=xg, in0=PS[:, 4 + 2 * u:6 + 2 * u, :].rearrange("p c t -> p (c t)"), scalar=0.5,
                                           in1=xg, op0=ALU.mult, op1=ALU.add).then_inc(po_done, 1)

                gated(l * G, 0, 0)
                with v.Fori(0, G // 2 - 1) as g2:
                    for u in range(2):
                        residual(g2, u, True)
                residual(G // 2 - 1, 0, True)
                residual(G // 2 - 1, 1, False)


def kernel(**inputs):
    import concourse.bacc as bacc
    from concourse.bass_utils import run_bass_kernel_spmd

    a = {k: np.asarray(v) for k, v in inputs.items()}

    def cols(w):
        return w.T.reshape(-1, P, w.shape[0]).transpose(1, 0, 2)

    def chan(v):
        return v.reshape(-1, P, v.shape[-1]).transpose(1, 0, 2)

    def two(name, fn):
        return np.stack([fn(a[f"L{n}_cond_{name}"]) for n in (2, 3)])

    arrays = {
        "xT": a["x"].reshape(G, TOK, HC, P).transpose(3, 0, 2, 1),
        "condT": a["cond_2048"].reshape(B, DC, P).transpose(2, 1, 0),
        "attw": np.stack([np.stack([cols(a[f"L{n}_cond_{w}_weight"]) for w in "qkvwu"], axis=1) for n in (0, 1)]),
        "win": two("W_in", cols),
        "wconv": two("W_conv", lambda w: chan(w[:, 0, :])),
        "chan": np.stack([chan(np.stack([a[f"L{n}_cond_{v}"] for v in ("b_conv", "ln_g", "ln_b")], axis=1)) for n in (2, 3)]),
        "wxp": np.pad(two("W_xproj", cols).reshape(2, P, DC, 3, N), [(0, 0)] * 4 + [(0, 32 - N)]).reshape(2, P, DC, 96),
        "wdt": two("W_dt", lambda w: w.T),
        "dtv": np.stack([np.stack([a[f"L{n}_cond_{v}"] for v in ("b_dt", "A_log")], axis=1) for n in (2, 3)]),
        "wout": two("W_out", cols),
        "dskip": two("D", lambda d: chan(d[:, None])),
    }
    p = np.arange(P)
    arrays["ident"] = np.eye(P, dtype=np.float32)
    arrays["sel"] = (p == np.arange(GB)[:, None] * N + np.arange(N)[:, None, None]).astype(np.float32)
    arrays["masks"] = np.concatenate([(p[:, None] // HD % 2 == np.arange(2)), (p[:, None] // S == np.arange(2)),
                                      (p[:, None] // N == np.arange(GB))], axis=1).astype(np.float32)
    rowmask = ((p[:, None] % GB == np.arange(GB)) & (p[:, None] < XROWS)).astype(np.float32)

    nc = bacc.Bacc("TRN2", target_bir_lowering=False, num_devices=1)
    bf = mybir.dt.np(mybir.dt.bfloat16)
    arrays["rowmask"] = rowmask.astype(bf)
    feed, args = {}, []
    for name in ("xT", "condT", "attw", "win", "wconv", "chan", "wxp", "wdt", "dtv", "wout", "dskip", "ident", "sel", "masks", "rowmask"):
        arr = np.ascontiguousarray(arrays[name])
        feed[f"in_{name}"] = arr
        args.append(nc.dram_tensor(f"in_{name}", arr.shape, mybir.dt.from_np(arr.dtype), kind="ExternalInput").ap())
    args.append(nc.dram_tensor("out_x", (P, G, HC, TOK), mybir.dt.float32, kind="ExternalOutput").ap())
    cond_resid_kernel(nc, *args)
    r = run_bass_kernel_spmd(nc, [feed], core_ids=[0])
    return np.ascontiguousarray(r.results[0]["out_x"].transpose(1, 3, 2, 0).reshape(B, S, H))
```
